# Optimizing a Trainium2 kernel written in Bass

```python
import numpy as np
import jax
import jax.numpy as jnp

def _softmax(x, axis=-1):
    return jax.nn.softmax(x, axis=axis)

def _gelu(x):
    return jax.nn.gelu(x, approximate=True)

def _silu(x):
    return jax.nn.silu(x)

def _sigmoid(x):
    return jax.nn.sigmoid(x)

def _layernorm(x, axis=-1, eps=1e-05):
    m = jnp.mean(x, axis=axis, keepdims=True)
    v = jnp.var(x, axis=axis, keepdims=True)
    return (x - m) / jnp.sqrt(v + eps)

def _scatter_add(tgt, idx, src, axis=0):
    return tgt.at[idx].add(src)

def _segment_sum(src, seg, n):
    return jax.ops.segment_sum(src, seg, n)
kernel_name = 'mk_xattn_ffn_d2_seqx_r8_e89d2b'

def setup_inputs(seed: int=0):
    np.random.seed(seed)
    _w = jnp.asarray

    def _rec_inputs():
        import jax
        import jax.numpy as jnp
        _rk = jax.random.key(seed)
        x = 0.0002417 + 0.9998 * jax.random.normal(jax.random.fold_in(_rk, 1), (2, 512, 128), jnp.float32)
        _lenS = 512 - jax.random.randint(jax.random.fold_in(_rk, 7), (2,), 0, max(1, 512 // 4) + 1, jnp.int32)
        _lenS2 = 154 - jax.random.randint(jax.random.fold_in(_rk, 8), (2,), 0, max(1, 154 // 4) + 1, jnp.int32)
        _ctx_1024P = jax.random.normal(jax.random.fold_in(_rk, 11), (2, 16, 128), jnp.float32)
        _ctx_1024c = jax.random.dirichlet(jax.random.fold_in(_rk, 511), 0.3 * jnp.ones((16,), jnp.float32), (2, 154))
        _ctx_1024t = jnp.einsum('bsk,bkd->bsd', _ctx_1024c, _ctx_1024P)
        _ctx_1024t = _ctx_1024t * jax.lax.rsqrt(jnp.mean(jnp.square(_ctx_1024t)) + 1e-12) * 0.953939
        ctx_1024 = 7.22013e-05 + 1.00017 * (_ctx_1024t + 0.3 * jax.random.normal(jax.random.fold_in(_rk, 611), (2, 154, 128), jnp.float32))
        return (x, ctx_1024)
    x, ctx_1024 = _rec_inputs()

    def _L0_xattn_setup():
        import jax, jax.numpy as jnp
        import numpy as np
        EMBED = 128
        HEADS = 16
        HEAD_DIM = EMBED // HEADS
        EXP_DIM = 2 * HEAD_DIM

        def _feature_map(x, fm_w, fm_b):
            z = jnp.einsum('nshd,ed->nshe', x, fm_w) + fm_b
            return jnp.concatenate([jnp.exp(z), jnp.exp(-z)], axis=-1)
        key = jax.random.key(seed)
        ks = jax.random.split(key, 7)
        N, S = (4, 256)
        values = jax.random.normal(ks[0], (N, S, EMBED), dtype=jnp.float32)
        keys_ = jax.random.normal(ks[1], (N, S, EMBED), dtype=jnp.float32)
        query = jax.random.normal(ks[2], (N, S, EMBED), dtype=jnp.float32)
        fm_w = jnp.eye(HEAD_DIM, dtype=jnp.float32) + 0.02 * jax.random.normal(ks[3], (HEAD_DIM, HEAD_DIM), dtype=jnp.float32)
        fm_b = 0.02 * jax.random.normal(ks[4], (HEAD_DIM,), dtype=jnp.float32)
        fc_w = jax.random.normal(ks[5], (EMBED, HEADS * EXP_DIM), dtype=jnp.float32) * (1.0 / np.sqrt(HEADS * EXP_DIM))
        fc_b = jnp.zeros((EMBED,), dtype=jnp.float32)
        return {'values': values, 'keys': keys_, 'query': query, 'fm_w': fm_w, 'fm_b': fm_b, 'fc_w': fc_w, 'fc_b': fc_b}
    _L0_xattn_all = _L0_xattn_setup()
    _L0_xattn_in = {k: v for k, v in _L0_xattn_all.items() if k in ('fm_w', 'fm_b', 'fc_w', 'fc_b')}
    del _L0_xattn_all

    def _L0_ffn_setup():
        import jax, jax.numpy as jnp
        import numpy as np
        K = 2
        key = jax.random.key(seed)
        ks = jax.random.split(key, 7)
        B, S, D, E = (2, 256, 128, 8)
        H = 4 * D
        sd = 1.0 / np.sqrt(D)
        sh = 1.0 / np.sqrt(H)
        return {'x': jax.random.normal(ks[0], (B, S, D), jnp.float32), 'Wr': jax.random.normal(ks[1], (D, E), jnp.float32) * sd, 'br': jax.random.normal(ks[2], (E,), jnp.float32) * sd, 'W1': jax.random.normal(ks[3], (E, D, H), jnp.float32) * sd, 'b1': jax.random.normal(ks[4], (E, H), jnp.float32) * sd, 'W2': jax.random.normal(ks[5], (E, H, D), jnp.float32) * sh, 'b2': jax.random.normal(ks[6], (E, D), jnp.float32) * sh}
    _L0_ffn_all = _L0_ffn_setup()
    _L0_ffn_in = {k: v for k, v in _L0_ffn_all.items() if k in ('Wr', 'br', 'W1', 'b1', 'W2', 'b2')}
    del _L0_ffn_all

    def _L1_xattn_setup():
        import jax, jax.numpy as jnp
        import numpy as np
        N_HEAD = 16
        key = jax.random.key(seed)
        ks = jax.random.split(key, 5)
        b, l, d = (4, 256, 128)
        dh = d // N_HEAD
        return {'q': jax.random.normal(ks[0], (b, l, d), dtype=jnp.float32), 'kv': jax.random.normal(ks[1], (b, l, d), dtype=jnp.float32), 'Wq': jax.random.normal(ks[2], (d, d), dtype=jnp.float32) * 0.02, 'Wkv': jax.random.normal(ks[3], (2 * dh, d), dtype=jnp.float32) * 0.02, 'Wc': jax.random.normal(ks[4], (d, d), dtype=jnp.float32) * 0.02}
    _L1_xattn_all = _L1_xattn_setup()
    _L1_xattn_in = {k: v for k, v in _L1_xattn_all.items() if k in ('Wq', 'Wkv', 'Wc')}
    del _L1_xattn_all

    def _L1_ffn_setup():
        import jax, jax.numpy as jnp
        import numpy as np
        B, N, D, F, E, K = (4, 256, 128, 512, 16, 2)
        EPS = 1e-05
        key = jax.random.key(seed)
        ks = jax.random.split(key, 6)
        scaled = lambda k, shape, fan: jax.random.normal(k, shape, jnp.float32) / np.float32(np.sqrt(fan))
        return {'x': jax.random.normal(ks[0], (B, N, D), jnp.float32), 'Wr': scaled(ks[1], (D, E), D), 'br': jnp.zeros((E,), jnp.float32), 'W1': scaled(ks[2], (E, D, F), D), 'W3': scaled(ks[3], (E, D, F), D), 'W2': scaled(ks[4], (E, F, D), F), 'gamma': jnp.ones((E, D), jnp.float32), 'beta': jnp.zeros((E, D), jnp.float32)}
    _L1_ffn_all = _L1_ffn_setup()
    _L1_ffn_in = {k: v for k, v in _L1_ffn_all.items() if k in ('Wr', 'br', 'W1', 'W3', 'W2', 'gamma', 'beta')}
    del _L1_ffn_all
    return {'x': x, 'ctx_1024': ctx_1024, 'L0_xattn_fm_w': _L0_xattn_in['fm_w'], 'L0_xattn_fm_b': _L0_xattn_in['fm_b'], 'L0_xattn_fc_w': _L0_xattn_in['fc_w'], 'L0_xattn_fc_b': _L0_xattn_in['fc_b'], 'L0_ffn_Wr': _L0_ffn_in['Wr'], 'L0_ffn_br': _L0_ffn_in['br'], 'L0_ffn_W1': _L0_ffn_in['W1'], 'L0_ffn_b1': _L0_ffn_in['b1'], 'L0_ffn_W2': _L0_ffn_in['W2'], 'L0_ffn_b2': _L0_ffn_in['b2'], 'L1_xattn_Wq': _L1_xattn_in['Wq'], 'L1_xattn_Wkv': _L1_xattn_in['Wkv'], 'L1_xattn_Wc': _L1_xattn_in['Wc'], 'L1_ffn_Wr': _L1_ffn_in['Wr'], 'L1_ffn_br': _L1_ffn_in['br'], 'L1_ffn_W1': _L1_ffn_in['W1'], 'L1_ffn_W3': _L1_ffn_in['W3'], 'L1_ffn_W2': _L1_ffn_in['W2'], 'L1_ffn_gamma': _L1_ffn_in['gamma'], 'L1_ffn_beta': _L1_ffn_in['beta']}

def reference(x, ctx_1024, L0_xattn_fm_w, L0_xattn_fm_b, L0_xattn_fc_w, L0_xattn_fc_b, L0_ffn_Wr, L0_ffn_br, L0_ffn_W1, L0_ffn_b1, L0_ffn_W2, L0_ffn_b2, L1_xattn_Wq, L1_xattn_Wkv, L1_xattn_Wc, L1_ffn_Wr, L1_ffn_br, L1_ffn_W1, L1_ffn_W3, L1_ffn_W2, L1_ffn_gamma, L1_ffn_beta):
    import jax
    import jax.numpy as jnp

    def _L0_xattn_ref(values, keys, query, fm_w, fm_b, fc_w, fc_b):
        import jax, jax.numpy as jnp
        import numpy as np
        EMBED = 128
        HEADS = 16
        HEAD_DIM = EMBED // HEADS
        EXP_DIM = 2 * HEAD_DIM

        def _feature_map(x, fm_w, fm_b):
            z = jnp.einsum('nshd,ed->nshe', x, fm_w) + fm_b
            return jnp.concatenate([jnp.exp(z), jnp.exp(-z)], axis=-1)
        N, S, _ = query.shape
        v = values.reshape(N, -1, HEADS, HEAD_DIM)
        k = keys.reshape(N, -1, HEADS, HEAD_DIM)
        q = query.reshape(N, -1, HEADS, HEAD_DIM)
        v, k, q = (_feature_map(x, fm_w, fm_b) for x in (v, k, q))
        scores = jnp.einsum('nqhd,nkhd->nhqk', q, k) / jnp.sqrt(jnp.float32(EMBED))
        attn = jax.nn.softmax(scores, axis=-1)
        out = jnp.einsum('nhql,nlhd->nqhd', attn, v)
        out = out.reshape(N, S, HEADS * EXP_DIM)
        return out @ fc_w.T + fc_b

    def _L0_ffn_ref(x, Wr, br, W1, b1, W2, b2):
        import jax, jax.numpy as jnp
        import numpy as np
        K = 2
        E = Wr.shape[-1]
        scores = jnp.einsum('bsd,de->bse', x, Wr) + br
        _, topk_idx = jax.lax.top_k(scores, K)
        indicator = jax.nn.one_hot(topk_idx, E, dtype=scores.dtype).sum(-2)
        neg_inf = jnp.asarray(-jnp.inf, scores.dtype)
        weights = jax.nn.softmax(jnp.where(indicator > 0, scores, neg_inf), axis=-1)
        out = jnp.zeros_like(x)
        for i in range(E):
            xi = x * indicator[..., i:i + 1]
            h = jax.nn.relu(jnp.einsum('bsd,dh->bsh', xi, W1[i]) + b1[i])
            yi = jnp.einsum('bsh,hd->bsd', h, W2[i]) + b2[i]
            out = out + yi * weights[..., i:i + 1]
        return out

    def _L1_xattn_ref(q, kv, Wq, Wkv, Wc):
        import jax, jax.numpy as jnp
        import numpy as np
        N_HEAD = 16
        b, l, d = q.shape
        h = N_HEAD
        dh = d // h
        qp = jnp.einsum('bld,ed->ble', q, Wq)
        scores = jnp.einsum('bld,bmd->blm', qp, kv)
        idx = jnp.argmax(scores, axis=-1)
        mem = jnp.take_along_axis(kv, idx[..., None], axis=1)
        mkv = jnp.einsum('bld,ed->ble', mem, Wkv)
        mk, mv = jnp.split(mkv, 2, axis=-1)
        qh = qp.reshape(b, l, h, dh).transpose(0, 2, 1, 3)
        scale = 1.0 / np.sqrt(dh).astype(np.float32)
        logits = jnp.einsum('bhld,bmd->bhlm', qh, mk) * scale
        attn = jax.nn.softmax(logits, axis=-1)
        out = jnp.einsum('bhlm,bmd->bhld', attn, mv)
        out = out.transpose(0, 2, 1, 3).reshape(b, l, d)
        return jnp.einsum('bld,ed->ble', out, Wc)

    def _L1_ffn_ref(x, Wr, br, W1, W3, W2, gamma, beta):
        import jax, jax.numpy as jnp
        import numpy as np
        B, N, D, F, E, K = (4, 256, 128, 512, 16, 2)
        EPS = 1e-05
        b, n, d = x.shape
        e = Wr.shape[1]
        xf = x.reshape(-1, d)
        logits = xf @ Wr + br
        probs = jax.nn.softmax(logits, axis=-1)
        vals, idx = jax.lax.top_k(probs, K)
        w = vals / vals.sum(axis=-1, keepdims=True)
        combine = jnp.zeros((xf.shape[0], e), x.dtype)
        for k in range(K):
            combine = combine + w[:, k:k + 1] * jax.nn.one_hot(idx[:, k], e, dtype=x.dtype)
        out = jnp.zeros_like(xf)
        for ei in range(e):
            h = jax.nn.silu(xf @ W1[ei]) * (xf @ W3[ei])
            y = h @ W2[ei]
            mu = y.mean(axis=-1, keepdims=True)
            var = ((y - mu) ** 2).mean(axis=-1, keepdims=True)
            y = (y - mu) * jax.lax.rsqrt(var + EPS) * gamma[ei] + beta[ei]
            out = out + combine[:, ei:ei + 1] * y
        return out.reshape(b, n, d)
    x = x + _L0_xattn_ref(ctx_1024, ctx_1024, _layernorm(x, axis=-1), L0_xattn_fm_w, L0_xattn_fm_b, L0_xattn_fc_w, L0_xattn_fc_b)
    x = x + _L0_ffn_ref(_layernorm(x, axis=-1), L0_ffn_Wr, L0_ffn_br, L0_ffn_W1, L0_ffn_b1, L0_ffn_W2, L0_ffn_b2)
    x = x + _L1_xattn_ref(_layernorm(x, axis=-1), ctx_1024, L1_xattn_Wq, L1_xattn_Wkv, L1_xattn_Wc)
    x = x + _L1_ffn_ref(_layernorm(x, axis=-1), L1_ffn_Wr, L1_ffn_br, L1_ffn_W1, L1_ffn_W3, L1_ffn_W2, L1_ffn_gamma, L1_ffn_beta)
    return x

_drawn_inputs = setup_inputs


def setup_inputs(seed=0):
    import zlib

    import numpy as np

    out = dict(_drawn_inputs(seed))
    spreads = {'L0_xattn_fc_b': (0.0, 0.8),
     'L1_ffn_br': (0.0, 0.675),
     'L1_ffn_gamma': (1.0, 0.6),
     'L1_ffn_beta': (0.0, 0.8)}
    factors = {'L0_ffn_br': 8.0,
     'L0_ffn_b1': 8.0,
     'L0_ffn_b2': 8.0,
     'L1_xattn_Wq': 8.0,
     'L1_xattn_Wkv': 8.0,
     'L1_xattn_Wc': 8.0}
    for name, (base, spread) in spreads.items():
        noise = np.random.default_rng([zlib.crc32(name.encode()), seed]).standard_normal(out[name].shape)
        drawn = base * np.exp(spread * noise) if base else spread * noise
        out[name] = jnp.asarray(drawn.astype(out[name].dtype))
    for name, factor in factors.items():
        out[name] = (out[name] * factor).astype(out[name].dtype)
    return out
```

```python
import numpy as np
import concourse.bass as bass
from concourse import mybir
from contextlib import ExitStack

F32 = mybir.dt.float32
F32R = mybir.dt.float32r
BF16 = mybir.dt.bfloat16
I32 = mybir.dt.int32
U32 = mybir.dt.uint32
ALU = mybir.AluOpType
ACT = mybir.ActivationFunctionType
AX = mybir.AxisListType

P = 128
B, S, D = 2, 512, 128
T = B * S // P
QT = S // P
KEYS = 154
KM, KR = P, KEYS - P
KP = 160
H, DH = 16, D // 16
F0 = 2 * DH
NPAIR, NQUAD = H // 2, H // 4
STORED = ("y_stored_0", "y_stored_1", "y_stored_2", "y_stored_3")
HID = 512
EXPERTS = (8, 16)
TILES = tuple((2 * B * S - E) // P + E for E in EXPERTS)
EPS = 1e-5
MASKED = -float(2 ** 100)
SCALE0 = float(1.0 / np.sqrt(np.float32(D)))
SCALE1 = float(np.float32(1.0 / np.sqrt(DH)))


class Steps:

    def __init__(self, engine, semaphore):
        self.engine, self.semaphore, self.count = engine, semaphore, 0

    def __call__(self, instruction):
        self.count += 1
        instruction.then_inc(self.semaphore, 1)
        self.engine.wait_ge(self.semaphore, self.count)


def build(nc, A, out, stop=9):
    ctx = ExitStack()
    with ctx:
        base = [(nc.sbuf_base + 31) // 32 * 32]

        def sb(name, shape, dt):
            n = int(np.prod(shape[1:])) * (2 if dt == BF16 else 4)
            t = nc.alloc_sbuf_tensor_at(name, shape, dt, offset=base[0])
            base[0] += (n + 31) // 32 * 32
            return t

        def sem(name):
            return ctx.enter_context(nc.semaphore(name))

        bank = [ctx.enter_context(nc.psum_tensor(f"bank{i}", [P, 512], F32)) for i in range(8)]

        ident = sb("ident", [P, P], F32)
        ones = sb("ones", [P, P], F32)
        ones_r = sb("ones_r", [P, 512], F32R)
        ones_b = sb("ones_b", [P, P], BF16)
        tri = sb("tri", [P, P], BF16)
        zero_rows = sb("zero_rows", [P, D], F32)
        iota_e = sb("iota_e", [P, 16], F32)
        iota_s = sb("iota_s", [P, 32], F32)
        iota_k = sb("iota_k", [P, 2 * P], F32)
        x = sb("x", [P, T, D], F32)
        xn = sb("xn", [P, T, D], F32)
        xnT = sb("xnT", [P, B, S], F32)
        stats = sb("stats", [P, T, 6], F32)
        mv = sb("mv", [P, T, 2], F32)
        rstd = sb("rstd", [P, T], F32)
        var = sb("var", [P, T], F32)
        guess = sb("guess", [P, T], F32)
        newton = sb("newton", [P, T], F32)
        ctx_main = sb("ctx_main", [P, B, D], F32)
        ctx_rem = sb("ctx_rem", [P, B, D], F32)
        ctxT = sb("ctxT", [P, B, KP], F32)
        ctxT_rep = sb("ctxT_rep", [P, B, 4, 32], F32)
        small_w = sb("small_w", [P, 4, D], F32)
        small_wT = sb("small_wT", [P, 4, D], F32)
        wkv = sb("wkv", [P, D], F32)
        wkvT = sb("wkvT", [P, 2 * DH], F32)
        fm_w = sb("fm_w", [P, DH], F32)
        fm_b = sb("fm_b", [P, 1], F32)
        fc_b = sb("fc_b", [P, D], F32)
        ind = sb("ind", [P, H, P], F32R)
        ind_rem = sb("ind_rem", [P, H, 32], F32R)
        pair32 = sb("pair32", [P, H], F32)
        wr = [sb(f"wr{L}", [P, E], F32) for L, E in enumerate(EXPERTS)]
        br = [sb(f"br{L}", [P, E], F32) for L, E in enumerate(EXPERTS)]
        logits = sb("logits", [P, T, 16], F32)
        top8 = sb("top8", [P, T, 8], F32)
        top8_at = sb("top8_at", [P, T, 8], U32)
        top2_at = sb("top2_at", [P, 2, T], F32)
        onehot = sb("onehot", [P, 2, T, 16], F32)
        chosen = sb("chosen", [P, T, 16], BF16)
        gate = sb("gate", [P, 4, T], F32)
        counts_f = sb("counts_f", [P, 16], F32)
        counts_i = sb("counts_i", [P, 2, 16], I32)
        tiles_f = sb("tiles_f", [P, 16], F32)
        scan = [sb(f"scan{i}", [P, 32], F32) for i in range(2)]
        rank = sb("rank", [P, T, 16], F32)
        ranked = sb("ranked", [P, 2, T, 16], F32)
        slot_f = sb("slot_f", [P, 2, T], F32)
        slot_i = sb("slot_i", [P, 2, T], I32)
        before = sb("before", [P, 32, 16], F32)
        expert_f = sb("expert_f", [P, 32], F32)
        expert_i = sb("expert_i", [P, 32], I32)
        shared = base[0]
        mx = sb("mx", [P, B, QT, H], F32)
        nm_hi = sb("nm_hi", [P, B, QT, H], F32R)
        nm = sb("nm", [P, B, QT, 2, H], F32)
        nmT = sb("nmT", [P, B, S], F32R)
        qst = sb("qst", [P, NPAIR, B, S], F32R)
        prob = sb("prob", [P, 2, 5, 512], F32)
        recip = sb("recip", [P, QT, 4], F32)
        o = sb("o", [P, B * QT, H * F0], F32)
        oT = prob[:, 0].rearrange("p a q -> p (a q)")[:, 0:2 * B * S].rearrange("p (n b q) -> p n b q", n=2, b=B)
        f = oT
        kf = prob[:, 1].rearrange("p a q -> p (a q)")[:, 0:2 * B * KP].rearrange("p (n k) -> p n k", n=2)
        shared_end = base[0]
        base[0] = shared
        gx = sb("gx", [P, max(TILES), D], F32)
        gxT = sb("gxT", [P, 2, P], F32)
        hid = sb("hid", [P, 2, HID], F32)
        act_h = sb("act_h", [P, 2, HID], F32)
        hidT = sb("hidT", [P, 2, HID], F32)
        y = sb("y", [P, 8, D], F32)
        yn = sb("yn", [P, 4, D], F32)
        ys = sb("ys", [P, 4, D], F32)
        y_stats = sb("y_stats", [P, 4, 6], F32)
        y_mv = sb("y_mv", [P, 4, 2], F32)
        y_root = sb("y_root", [P, 4, 4], F32)
        yg = sb("yg", [P, 2, T, D], F32)
        spare = base[0]
        b1_cols = sb("b1_cols", [P, 32 + 8], F32)
        b1_hi = sb("b1_hi", [P, 32 + 8], F32R)
        b1_lo = sb("b1_lo", [P, 32 + 8], F32R)
        b1_rows = sb("b1_rows", [P, EXPERTS[0] * (HID + D)], F32R)
        assert base[0] <= shared_end, (base[0], shared_end)
        base[0] = spare
        gamma = sb("gamma", [P, EXPERTS[1], D], F32)
        beta = sb("beta", [P, EXPERTS[1], D], F32)
        assert base[0] <= shared_end, (base[0], shared_end)
        base[0] = scratch0 = shared_end
        bmask = sb("bmask", [P, H], F32)
        sign_id = sb("sign_id", [P, H, 2, DH], F32)
        fm_rep = sb("fm_rep", [P, H, DH], F32)
        wexp = sb("wexp", [P, H, 2, DH], F32)
        bias_col = sb("bias_col", [P, 1], F32)
        bias_row = sb("bias_row", [P, H * F0], F32)
        f_hi = sb("f_hi", [P, 2, B, S], F32R)
        f_lo = sb("f_lo", [P, 2, B, S], F32R)
        kf_hi = sb("kf_hi", [P, 2, B * KP], F32R)
        kf_lo = sb("kf_lo", [P, 2, B * KP], F32R)
        sel0 = {n: sb(f"sel0_{n}", [P, 8, 4, F0], F32R) for n in ("q_hi", "q_lo", "k_hi", "k_lo")}
        kst0 = sb("kst0", [P, H, B, KP], F32R)
        krem0 = sb("krem0", [P, B, NPAIR, 4, 32], F32R)
        v0 = sb("v0", [P, B, H, F0 + 1], F32)
        vrem0 = sb("vrem0", [P, B, NQUAD, 4, F0 + 1], F32)
        scratch0_end = base[0]
        base[0] = scratch0
        w1_1 = sb("w1_1", [P, EXPERTS[1] * HID], F32)
        w3_1 = sb("w3_1", [P, EXPERTS[1] * HID], F32)
        base[0] = weights0 = max(base[0], scratch0_end)
        w1_0 = sb("w1_0", [P, EXPERTS[0] * HID], F32)
        w2_0 = sb("w2_0", [P, EXPERTS[0] * HID], F32)
        base[0] = weights0
        w2_1 = sb("w2_1", [P, EXPERTS[1] * HID], F32)
        base[0] = weights0
        qp = sb("qp", [P, B, S], F32)
        qp_hi = sb("qp_hi", [P, B, S], F32R)
        qp_lo = sb("qp_lo", [P, B, S], F32R)
        sel1 = {n: sb(f"sel1_{n}", [P, H, 4, DH], F32R) for n in ("q_hi", "q_lo")}
        sel1k = {n: sb(f"sel1_{n}", [P, 4, 4, DH], F32R) for n in ("k_hi", "k_lo", "mask")}
        hits = sb("hits", [P, QT, 2 * P], BF16)
        hit8 = sb("hit8", [P, T, 8], F32)
        hit8_at = sb("hit8_at", [P, T, 8], U32)
        hit_f = sb("hit_f", [P, T], F32)
        counts = sb("counts", [P, 2 * B], F32)
        mask_row = sb("mask_row", [P, B * KP], F32R)
        mk_hi = sb("mk_hi", [P, B * KP], F32R)
        mk_lo = sb("mk_lo", [P, B * KP], F32R)
        kst1 = sb("kst1", [P, 4, B, KP], F32R)
        krem1 = sb("krem1", [P, B, 4, 32], F32R)
        v1 = sb("v1", [P, B, DH + 1], F32)
        vrem1 = sb("vrem1", [P, B, 4, DH + 1], F32)
        assert base[0] <= weights0 + EXPERTS[1] * HID * 4, (base[0], weights0)
        slots_x = [nc.dram_tensor(f"slots_x{L}", (n * P, D), F32, kind="Internal").ap() for L, n in enumerate(TILES)]
        slots_y = [nc.dram_tensor(f"slots_y{L}", (n * P, D), F32, kind="Internal").ap() for L, n in enumerate(TILES)]

        s = {n: sem(n) for n in (
            "ld_x", "ld_ctx", "ld_small", "pool_step", "pool_consts", "dve_zeroed", "dve_step", "act_step",
            "xn_ok", "ctxT_pe", "wT_pe", "ctxT_ok", "wT_ok", "xnT_pe", "xnT_ok",
            "fm_pe", "fm_ok", "fm2_pe", "fm2_ok", "zq_pe", "f_ok", "zk_pe", "kf_ok", "vz_pe", "v_ok", "f_split",
            "kf_split", "consts_dve", "kst_pe", "kst_ok", "qst_pe", "qst_dve", "qst_act", "score_pe", "max_ok", "nm_ok",
            "nmT_pe", "nmT_ok", "prob_pe", "prob_ok", "pv_pe", "o_ok", "oT_pe", "oT_ok", "fc_pe", "x1_ok", "stored",
            "ld_b1", "ld_b1_rows", "ld_gb", "qp_pe", "qp_ok", "qp_split", "sel1_ok", "hit_pe", "hit_ok", "count_pe", "count_ok",
            "mk_pe", "mk_ok", "kst1_pe", "kst1_ok", "qst1_pe", "qst1_ok", "b1_ok")}
        r = [{n: sem(f"{n}_L{L}") for n in (
            "ld_w", "ld_w2", "logits_pe", "logits_ok", "diff_ok", "exp_ok", "chosen_ok", "rank_pe", "slots_ok", "experts_ok",
            "zero_x", "scattered", "gx_ok", "gxT_pe", "gxT_ok", "up_pe", "act_ok", "hid_ok", "hidT_pe", "hidT_ok", "y_pe",
            "y_ok", "y_copied", "y_normed", "y_stats_ok", *STORED, "gathered", "mixed")} for L in range(2)]

        block = ctx.enter_context(nc.Block())

        LD_SMALL = 16 * 11

        POOL_CONSTS = 5

        def inverse_root(step, variance, var, guess, newton, root):
            step(nc.vector.tensor_scalar(var, variance, EPS, None, ALU.add))
            step(nc.vector.tensor_scalar(guess.bitcast(I32), var.bitcast(I32), 1, None, ALU.arith_shift_right))
            step(nc.vector.tensor_scalar(root.bitcast(I32), guess.bitcast(I32), -1.0, float(0x5F3759DF), ALU.mult, ALU.add))
            for _ in range(3):
                step(nc.vector.tensor_tensor(newton, root, root, ALU.mult))
                step(nc.vector.scalar_tensor_tensor(out=newton, in0=newton, scalar=-0.5, in1=var, op0=ALU.mult, op1=ALU.mult))
                step(nc.vector.scalar_tensor_tensor(out=root, in0=newton, scalar=1.5, in1=root, op0=ALU.add, op1=ALU.mult))

        def layer_norm(dve, step, done):
            for t in range(T):
                ins = nc.vector.bn_stats(stats[:, t, :], x[:, t, :])
            step(ins)
            for t in range(T):
                ins = nc.vector.bn_aggr(mv[:, t, :], stats[:, t, :])
            step(ins)
            inverse_root(step, mv[:, :, 1], var[:], guess[:], newton[:], rstd[:])
            for t in range(T):
                ins = nc.vector.tensor_scalar(xn[:, t, :], x[:, t, :], mv[:, t, 0:1], rstd[:, t:t + 1],
                                              ALU.subtract, ALU.mult)
            ins.then_inc(done, 1)

        def max_tile(dve, L, b, qt):
            for g in range(6):
                n = min(3, H - 3 * g)
                u = (b * QT + qt) * 6 + g
                dve.wait_ge(s["score_pe"], L * B * QT * 6 + u + 1)
                ins = nc.vector.tensor_reduce(mx[:, b, qt, 3 * g:3 * g + n],
                                              bank[5 + u % 2][:, 0:n * KEYS].rearrange("p (h k) -> p h k", h=n),
                                              AX.X, ALU.max)
                ins.then_inc(s["max_ok"], 1)

        def negate_max(dve, step, L, b):
            dve.wait_ge(s["max_ok"], (L * B + b + 1) * QT * 6)
            step(nc.vector.tensor_scalar(nm_hi[:, b], mx[:, b], -1.0, None, ALU.mult))
            nc.vector.tensor_copy(nm[:, b, :, 0, :], nm_hi[:, b].bitcast(F32))
            nc.vector.scalar_tensor_tensor(out=nm[:, b, :, 1, :], in0=mx[:, b], scalar=-1.0, in1=nm_hi[:, b].bitcast(F32),
                                           op0=ALU.mult, op1=ALU.subtract).then_inc(s["nm_ok"], 1)
            dve.wait_ge(s["nmT_pe"], L * B + b + 1)
            nc.vector.tensor_copy(nmT[0:32, b, :], bank[7][0:32, :]).then_inc(s["nmT_ok"], 1)

        def normalise(dve, step, L, b, hg, vw):
            g = (L * B + b) * NQUAD + hg
            dve.wait_ge(s["pv_pe"], g + 1)
            acc = bank[0][:, 0:QT * 4 * vw].rearrange("p (q j v) -> p q j v", q=QT, j=4)
            step(nc.vector.reciprocal(recip[:], acc[:, :, :, vw - 1]))
            w = vw - 1
            for qt in range(QT):
                dst = o[:, b * QT + qt, 0:H * w].rearrange("p (h v) -> p h v", v=w)[:, 4 * hg:4 * hg + 4, :]
                ins = nc.vector.tensor_tensor(dst, acc[:, qt, :, 0:w], recip[:, qt, :].unsqueeze(2).to_broadcast([P, 4, w]),
                                              ALU.mult)
            ins.then_inc(s["o_ok"], 1)

        def attention_dve(dve, step, L, vw):
            for qt in range(QT):
                max_tile(dve, L, 0, qt)
            negate_max(dve, step, L, 0)
            for hg in range(NQUAD):
                max_tile(dve, L, 1, hg)
                normalise(dve, step, L, 0, hg, vw)
            negate_max(dve, step, L, 1)
            for hg in range(NQUAD):
                normalise(dve, step, L, 1, hg, vw)
            for b in range(B):
                dve.wait_ge(s["fc_pe"], L * B + b + 1)
                ins = nc.vector.tensor_tensor(x[:, b * QT:(b + 1) * QT, :], x[:, b * QT:(b + 1) * QT, :],
                                              bank[5 + b][:].rearrange("p (q e) -> p q e", q=QT), ALU.add)
                ins.then_inc(s["x1_ok"], 1)

        def attention_act(act, L, scale):
            for g in range(B * NQUAD):
                group = L * B * NQUAD + g
                if group >= 2:
                    act.wait_ge(s["pv_pe"], group - 1)
                for i in range(5):
                    u = group * 5 + i
                    act.wait_ge(s["prob_pe"], u + 1)
                    nc.scalar.activation(prob[:, group % 2, i, :], bank[1 + u % 4][:], ACT.Exp,
                                         scale=scale).then_inc(s["prob_ok"], 1)
            n = H * (F0 if L == 0 else DH) // P
            for u in range(T):
                act.wait_ge(s["oT_pe"], L * T + u + 1)
                b, qt = divmod(u, QT)
                nc.scalar.copy(oT[:, 0:n, b, qt * P:(qt + 1) * P],
                               bank[1 + u % 4][:, 0:n * P].rearrange("p (n q) -> p n q", n=n)).then_inc(s["oT_ok"], 1)

        mm = nc.tensor.matmul

        def wait_qst(pe, u):
            pe.wait_ge(s["qst_act" if u % 2 else "qst_dve"], u // 2 + 1)

        def transpose_xn(pe):
            for t in range(T):
                b, qt = divmod(t, QT)
                ins = nc.tensor.transpose(bank[3 + b][:, qt * P:(qt + 1) * P], xn[:, t, :], ident[:])
            ins.then_inc(s["xnT_pe"], 1)

        def copy_xnT(act, n):
            act.wait_ge(s["xnT_pe"], n + 1)
            for b in range(B):
                nc.scalar.copy(xnT[:, b, :], bank[3 + b][:]).then_inc(s["xnT_ok"], 1)

        def attention_pe(pe, L, query, keys, rem_scores, values, rem_values, vw):
            def score_tile(b, qt):
                for g in range(6):
                    u = (L * B + b) * QT * 6 + qt * 6 + g
                    if u % (B * QT * 6) >= 2:
                        pe.wait_ge(s["max_ok"], u - 1)
                    n = min(3, H - 3 * g)
                    for i in range(n):
                        h = 3 * g + i
                        ins = mm(bank[5 + u % 2][:, i * KEYS:(i + 1) * KEYS], query(b, h, slice(qt * P, (qt + 1) * P)),
                                 keys(b, h, KEYS), start=True, stop=True)
                    ins.then_inc(s["score_pe"], 1)

            def turn_max(b):
                pe.wait_ge(s["nm_ok"], L * B + b + 1)
                for qt in range(QT):
                    ins = nc.tensor.transpose(bank[7][0:32, qt * P:(qt + 1) * P],
                                              nm[:, b, qt].rearrange("p a h -> p (a h)"), ident[:])
                ins.then_inc(s["nmT_pe"], 1)
                pe.wait_ge(s["nmT_ok"], L * B + b + 1)

            def prob_group(b, hg):
                group = (L * B + b) * NQUAD + hg
                for i in range(5):
                    u = group * 5 + i
                    if u % (B * NQUAD * 5) >= 4:
                        pe.wait_ge(s["prob_ok"], u - 3)
                    dst = bank[1 + u % 4][:]
                    if i == 0:
                        rem_scores(dst, b, hg)
                        lhs = ind_rem[:, 4 * hg:4 * hg + 4, :].rearrange("p h k -> p (h k)")
                    else:
                        h = 4 * hg + i - 1
                        mm(dst, keys(b, h, P), query(b, h, slice(0, S)), start=True, stop=False)
                        lhs = ind[:, h, :]
                    mm(dst, lhs, nmT[:, b, :], start=False, stop=True).then_inc(s["prob_pe"], 1)

            def weighted_sum(b, hg):
                group = (L * B + b) * NQUAD + hg
                pe.wait_ge(s["prob_ok"], 5 * group + 5)
                if group:
                    pe.wait_ge(s["o_ok"], group)
                for qt in range(QT):
                    cols = slice(qt * P, (qt + 1) * P)
                    at = qt * 4 * vw
                    mm(bank[0][:, at:at + 4 * vw], prob[:, group % 2, 0, cols], rem_values(b, hg).rearrange("p j v -> p (j v)"),
                       start=(qt == 0), stop=False, skip_group_check=True)
                    for j in range(4):
                        ins = mm(bank[0][:, at + j * vw:at + (j + 1) * vw], prob[:, group % 2, 1 + j, cols],
                                 values(b, 4 * hg + j), start=False, stop=True, skip_group_check=True)
                ins.then_inc(s["pv_pe"], 1)

            for qt in range(QT):
                score_tile(0, qt)
            turn_max(0)
            for hg in range(NQUAD):
                prob_group(0, hg)
                score_tile(1, hg)
                weighted_sum(0, hg)
            turn_max(1)
            for hg in range(NQUAD):
                prob_group(1, hg)
                if hg:
                    weighted_sum(1, hg - 1)
            weighted_sum(1, NQUAD - 1)
            w = H * (vw - 1)
            n = w // P
            pe.wait_ge(s["o_ok"], (L + 1) * B * NQUAD)
            for u in range(T):
                if u >= 4:
                    pe.wait_ge(s["oT_ok"], L * T + u - 3)
                for i in range(n):
                    ins = nc.tensor.transpose(bank[1 + u % 4][:, i * P:(i + 1) * P], o[:, u, i * P:(i + 1) * P], ident[:])
                ins.then_inc(s["oT_pe"], 1)
            pe.wait_ge(s["oT_ok"], (L + 1) * T)
            for b in range(B):
                for qt in range(QT):
                    dst = bank[5 + b][:, qt * P:(qt + 1) * P]
                    for i in range(n):
                        ins = mm(dst, oT[:, i, b, qt * P:(qt + 1) * P], small_wT[:, (0 if L == 0 else 3) + i, :],
                                 start=(i == 0), stop=(L == 1))
                    if L == 0:
                        ins = mm(dst, ones[0:1, 0:P], fc_b[0:1, :], start=False, stop=True)
                ins.then_inc(s["fc_pe"], 1)



        def experts_sync(sp, L):
            if L == 0:
                sp.wait_ge(s["x1_ok"], 2)
                sp.dma_start(b1_cols[:, 0:32], A["L0_ffn_b1"].rearrange("e f -> (e f)").rearrange("(p c) -> p c", c=32)).then_inc(s["ld_b1"], 16)
                sp.dma_start(b1_cols[:, 32:40], A["L0_ffn_b2"].rearrange("e f -> (e f)").rearrange("(p c) -> p c", c=8)).then_inc(s["ld_b1"], 16)
                sp.wait_ge(s["b1_ok"], 1)
                n = EXPERTS[0] * HID
                for row, part in enumerate((b1_hi, b1_lo)):
                    sp.dma_start(b1_rows[row:row + 1, 0:n].bitcast(F32), part[:, 0:32].bitcast(F32)).then_inc(s["ld_b1_rows"], 16)
                    sp.dma_start(b1_rows[row:row + 1, n:].bitcast(F32), part[:, 32:40].bitcast(F32)).then_inc(s["ld_b1_rows"], 16)
            sp.wait_ge(r[L]["scattered"], 16 * 2 * T)
            sp.dma_start(gx[:, 0:TILES[L], :], slots_x[L].rearrange("(t p) d -> p t d", p=P)).then_inc(r[L]["gx_ok"], 16)
            for t in range(TILES[L]):
                sp.wait_ge(r[L]["y_copied" if L == 0 else "y_ok"], t + 1)
                sp.dma_start(slots_y[L][t * P:(t + 1) * P, :], (y if L == 0 else ys)[:, t % 4, :]).then_inc(r[L][STORED[t % 4]], 16)

        def experts_pool(pool, step, L):
            pool.wait_ge(r[L]["zero_x"], 16)
            pool.wait_ge(r[L]["slots_ok"], 1)
            for k in range(2):
                for t in range(T):
                    nc.gpsimd.indirect_dma_start(
                        out=slots_x[L], out_offset=bass.IndirectOffsetOnAxis(ap=slot_i[:, k, t:t + 1].bitcast(U32), axis=0),
                        in_=xn[:, t, :], in_offset=None).then_inc(r[L]["scattered"], 16)
            if L == 1:
                q = r[L]
                pool.wait_ge(q["experts_ok"], 1)
                pool.wait_ge(s["ld_gb"], 32)
                for t in range(TILES[L]):
                    e = pool.value_load(expert_i[0:1, t:t + 1], min_val=0, max_val=EXPERTS[L] - 1)
                    pool.wait_ge(q["y_normed"], t + 1)
                    if t >= 4:
                        pool.wait_ge(q[STORED[t % 4]], 16 * (t // 4))
                    step(nc.gpsimd.tensor_tensor(ys[:, t % 4, :], yn[:, t % 4, :], gamma[:].rearrange("p e d -> p (e d)")[:, bass.ds(e * D, D)], ALU.mult))
                    nc.gpsimd.tensor_tensor(ys[:, t % 4, :], ys[:, t % 4, :], beta[:].rearrange("p e d -> p (e d)")[:, bass.ds(e * D, D)],
                                            ALU.add).then_inc(q["y_ok"], 1)
            for i in range(4):
                pool.wait_ge(r[L][STORED[i]], 16 * ((TILES[L] + 3 - i) // 4))
            for k in range(2):
                for t in range(T):
                    nc.gpsimd.indirect_dma_start(
                        out=yg[:, k, t, :], out_offset=None, in_=slots_y[L],
                        in_offset=bass.IndirectOffsetOnAxis(ap=slot_i[:, k, t:t + 1].bitcast(U32), axis=0)).then_inc(r[L]["gathered"], 16)

        def route_dve(dve, step, L):
            E, q = EXPERTS[L], r[L]
            dve.wait_ge(q["logits_pe"], 1)
            step(nc.vector.tensor_copy(logits[:, :, 0:E], bank[5][:, 0:T * E].rearrange("p (t e) -> p t e", e=E)))
            for t in range(T):
                ins = nc.vector.max(top8[:, t, :], logits[:, t, 0:E])
            step(ins)
            for t in range(T):
                ins = nc.vector.max_index(top8_at[:, t, :], top8[:, t, :], logits[:, t, 0:E])
            step(ins)
            nc.vector.tensor_tensor(gate[:, 0, :], top8[:, :, 1], top8[:, :, 0], ALU.subtract).then_inc(q["diff_ok"], 1)
            step(nc.vector.tensor_copy(top2_at[:], top8_at[:, :, 0:2].rearrange("p t k -> p k t")))
            for k in range(2):
                ins = nc.vector.tensor_tensor(onehot[:, k, :, 0:E], iota_e[:, 0:E].unsqueeze(1).to_broadcast([P, T, E]),
                                              top2_at[:, k, :].unsqueeze(2).to_broadcast([P, T, E]), ALU.is_equal)
            step(ins)
            nc.vector.tensor_tensor(chosen[:, :, 0:E], onehot[:, 0, :, 0:E], onehot[:, 1, :, 0:E], ALU.add).then_inc(q["chosen_ok"], 1)
            dve.wait_ge(q["exp_ok"], 1)
            step(nc.vector.tensor_scalar(gate[:, 1, :], gate[:, 0, :], 1.0, None, ALU.add))
            step(nc.vector.reciprocal(gate[:, 2, :], gate[:, 1, :]))
            step(nc.vector.tensor_tensor(gate[:, 3, :], gate[:, 0, :], gate[:, 2, :], ALU.mult))
            dve.wait_ge(q["rank_pe"], 1)
            step(nc.vector.tensor_scalar(counts_i[:, 0, 0:E], bank[7][:, 0:E], float(P - 1), None, ALU.add))
            step(nc.vector.tensor_scalar(counts_i[:, 1, 0:E], counts_i[:, 0, 0:E], 7, None, ALU.arith_shift_right))
            nc.vector.memset(scan[0][:, 0:16], 0.0)
            nc.vector.memset(scan[1][:, 0:16], 0.0)
            nc.vector.tensor_copy(tiles_f[:, 0:E], counts_i[:, 1, 0:E])
            step(nc.vector.tensor_copy(scan[0][:, 16:16 + E], counts_i[:, 1, 0:E]))
            a = 0
            shift = 1
            while shift < E:
                step(nc.vector.tensor_tensor(scan[1 - a][:, 16:16 + E], scan[a][:, 16:16 + E],
                                             scan[a][:, 16 - shift:16 - shift + E], ALU.add))
                a, shift = 1 - a, shift * 2
            upto = scan[a][:, 16:16 + E]
            step(nc.vector.tensor_tensor(counts_f[:, 0:E], upto, tiles_f[:, 0:E], ALU.subtract))
            step(nc.vector.tensor_scalar(counts_f[:, 0:E], counts_f[:, 0:E], float(P), None, ALU.mult))
            step(nc.vector.tensor_tensor(rank[:, :, 0:E], bank[6][:, 0:T * E].rearrange("p (t e) -> p t e", e=E),
                                         counts_f[:, 0:E].unsqueeze(1).to_broadcast([P, T, E]), ALU.add))
            for k in range(2):
                ins = nc.vector.tensor_tensor(ranked[:, k, :, 0:E], onehot[:, k, :, 0:E], rank[:, :, 0:E], ALU.mult)
            step(ins)
            step(nc.vector.tensor_reduce(slot_f[:].rearrange("p k t -> p (k t)"), ranked[:, :, :, 0:E].rearrange("p k t e -> p (k t) e"), AX.X, ALU.add))
            nc.vector.tensor_copy(slot_i[:], slot_f[:]).then_inc(q["slots_ok"], 1)
            NT = TILES[L]
            step(nc.vector.tensor_tensor(before[:, 0:NT, 0:E], upto.unsqueeze(1).to_broadcast([P, NT, E]),
                                         iota_s[:, 0:NT].unsqueeze(2).to_broadcast([P, NT, E]), ALU.is_le))
            step(nc.vector.tensor_reduce(expert_f[:, 0:NT], before[:, 0:NT, 0:E], AX.X, ALU.add))
            nc.vector.tensor_scalar(expert_i[:, 0:NT], expert_f[:, 0:NT], float(E - 1), None, ALU.min).then_inc(q["experts_ok"], 1)
            if L == 0:
                dve.wait_ge(s["ld_b1"], 32)
                step(nc.vector.tensor_copy(b1_hi[:], b1_cols[:]))
                nc.vector.tensor_tensor(b1_lo[:], b1_cols[:], b1_hi[:].bitcast(F32), ALU.subtract).then_inc(s["b1_ok"], 1)

        def experts_dve(dve, step, L):
            q = r[L]
            if L == 1:
                n = TILES[L]
                for t in range(n + 2):
                    if t < n:
                        dve.wait_ge(q["act_ok"], t + 1)
                        if t >= 2:
                            dve.wait_ge(q["hidT_pe"], t - 1)
                        nc.vector.tensor_tensor(hid[:, t % 2, :], act_h[:, t % 2, :], bank[2 + 2 * (t % 2)][:], ALU.mult).then_inc(q["hid_ok"], 1)
                    u = t - 2
                    if u >= 0:
                        dve.wait_ge(q["y_copied"], u + 1)
                        if u % 4 == 0 and u >= 4:
                            dve.wait_ge(q["y_normed"], u)
                        nc.vector.bn_stats(y_stats[:, u % 4, :], y[:, u % 8, :]).then_inc(q["y_stats_ok"], 1)
                        if u % 4 == 3 or u == n - 1:
                            expert_norm(dve, step, q, u // 4 * 4, u + 1)
            dve.wait_ge(q["gathered"], 16 * 2 * T)
            for k in range(2):
                for t in range(T):
                    ins = nc.vector.scalar_tensor_tensor(out=x[:, t, :], in0=yg[:, k, t, :], scalar=gate[:, 2 + k, t:t + 1],
                                                         in1=x[:, t, :], op0=ALU.mult, op1=ALU.add)
                    if k == 0 and t == T - 1:
                        step(ins)
            ins.then_inc(q["mixed"], 1)

        def expert_norm(dve, step, q, first, end):
            m = end - first
            dve.wait_ge(q["y_stats_ok"], end)
            for u in range(first, end):
                ins = nc.vector.bn_aggr(y_mv[:, u - first, :], y_stats[:, u - first, :])
            step(ins)
            inverse_root(step, y_mv[:, 0:m, 1], y_root[:, 0, 0:m], y_root[:, 1, 0:m], y_root[:, 2, 0:m], y_root[:, 3, 0:m])
            for u in range(first, end):
                if u >= 4:
                    dve.wait_ge(q["y_ok"], u - 3)
                nc.vector.tensor_scalar(yn[:, u % 4, :], y[:, u % 8, :], y_mv[:, u - first, 0:1], y_root[:, 3, u - first:u - first + 1],
                                        ALU.subtract, ALU.mult).then_inc(q["y_normed"], 1)

        def experts_act(act, L):
            q = r[L]
            act.wait_ge(q["diff_ok"], 1)
            nc.scalar.activation(gate[:, 0, :], gate[:, 0, :], ACT.Exp).then_inc(q["exp_ok"], 1)
            def rows(t):
                act.wait_ge(q["gxT_pe"], t + 1)
                if t >= 2:
                    act.wait_ge(q["up_pe"], t - 1)
                nc.scalar.copy(gxT[:, t % 2, :], bank[0][:, 0:P]).then_inc(q["gxT_ok"], 1)

            def hidden(t):
                act.wait_ge(q["up_pe"], t + 1)
                if L == 0:
                    if t >= 2:
                        act.wait_ge(q["hidT_pe"], t - 1)
                    nc.scalar.activation(hid[:, t % 2, :], bank[1 + 2 * (t % 2)][:], ACT.Relu).then_inc(q["hid_ok"], 1)
                else:
                    if t >= 2:
                        act.wait_ge(q["hid_ok"], t - 1)
                    nc.scalar.activation(act_h[:, t % 2, :], bank[1 + 2 * (t % 2)][:], ACT.Silu).then_inc(q["act_ok"], 1)

            n = TILES[L]
            for t in range(3):
                rows(t)
                if t >= 1:
                    hidden(t - 1)
            for t in range(n):
                act.wait_ge(q["hidT_pe"], t + 1)
                if t >= 2:
                    act.wait_ge(q["y_pe"], t - 1)
                nc.scalar.copy(hidT[:, t % 2, :], bank[5][:]).then_inc(q["hidT_ok"], 1)
                if t + 3 < n:
                    rows(t + 3)
                if t + 2 < n:
                    hidden(t + 2)
                act.wait_ge(q["y_pe"], t + 1)
                if L == 0:
                    if t >= 4:
                        act.wait_ge(q[STORED[t % 4]], 16 * (t // 4))
                    nc.scalar.copy(y[:, t % 4, :], bank[6 + t % 2][:, 0:D]).then_inc(q["y_copied"], 1)
                else:
                    if t >= 8:
                        act.wait_ge(q["y_ok"], t - 7)
                    nc.scalar.copy(y[:, t % 8, :], bank[6 + t % 2][:, 0:D]).then_inc(q["y_copied"], 1)

        def experts_pe(pe, L):
            E, q = EXPERTS[L], r[L]
            pe.wait_ge(s["xnT_ok"], 2 * (2 * L + 2))
            for t in range(T):
                b, qt = divmod(t, QT)
                dst = bank[5][:, t * E:(t + 1) * E]
                mm(dst, xnT[:, b, qt * P:(qt + 1) * P], wr[L][:], start=True, stop=False)
                ins = mm(dst, ones[0:1, 0:P], br[L][0:1, :], start=False, stop=True)
            ins.then_inc(q["logits_pe"], 1)
            pe.wait_ge(q["chosen_ok"], 1)
            for back in range(T):
                ins = mm(bank[6][:, back * E:T * E], tri[:] if back == 0 else ones_b[:], chosen[:, 0:T - back, 0:E],
                         start=(back == 0), stop=(back == T - 1), skip_group_check=True)
            for t in range(T):
                ins = mm(bank[7][:, 0:E], ones_b[:], chosen[:, t, 0:E], start=(t == 0), stop=(t == T - 1))
            ins.then_inc(q["rank_pe"], 1)
            w1, w2 = (w1_0, w2_0) if L == 0 else (w1_1, w2_1)

            def expert_of(t):
                return pe.value_load(expert_i[0:1, t:t + 1], min_val=0, max_val=E - 1)

            def turn_rows(t):
                if t:
                    pe.wait_ge(q["gxT_ok"], t)
                nc.tensor.transpose(bank[0][:, 0:P], gx[:, t, :], ident[:]).then_inc(q["gxT_pe"], 1)

            def up(t, e):
                pe.wait_ge(q["gxT_ok"], t + 1)
                if t >= 2:
                    pe.wait_ge(q["hid_ok"], t - 1)
                cols = bass.ds(e * HID, HID)
                first, second = bank[1 + 2 * (t % 2)], bank[2 + 2 * (t % 2)]
                if L == 0:
                    mm(first[:], gxT[:, t % 2, :], w1[:, cols], start=True, stop=False)
                    mm(first[:], ones_r[0:2, 0:P], b1_rows[0:2, cols], start=False, stop=True).then_inc(q["up_pe"], 1)
                else:
                    mm(first[:], gxT[:, t % 2, :], w1[:, cols], start=True, stop=True)
                    mm(second[:], gxT[:, t % 2, :], w3_1[:, cols], start=True, stop=True).then_inc(q["up_pe"], 1)

            def turn_hidden(t):
                pe.wait_ge(q["hid_ok"], t + 1)
                if t:
                    pe.wait_ge(q["hidT_ok"], t)
                for c in range(4):
                    ins = nc.tensor.transpose(bank[5][:, c * P:(c + 1) * P], hid[:, t % 2, c * P:(c + 1) * P], ident[:])
                ins.then_inc(q["hidT_pe"], 1)

            def down(t, e):
                pe.wait_ge(q["hidT_ok"], t + 1)
                result = bank[6 + t % 2][:, 0:D]
                if t >= 2:
                    pe.wait_ge(q["y_copied"], t - 1)
                for c in range(4):
                    ins = mm(result, hidT[:, t % 2, c * P:(c + 1) * P], w2[:, bass.ds(e * HID + c * P, P)],
                             start=(c == 0), stop=(L == 1 and c == 3))
                if L == 0:
                    ins = mm(result, ones_r[0:2, 0:P], b1_rows[0:2, bass.ds(e * D + E * HID, D)], start=False, stop=True)
                ins.then_inc(q["y_pe"], 1)

            pe.wait_ge(q["experts_ok"], 1)
            if L == 0:
                pe.wait_ge(s["ld_b1_rows"], 64)
            pe.wait_ge(q["ld_w"], 16 * (2 + L))
            pe.wait_ge(q["gx_ok"], 16)
            n = TILES[L]
            e = {}
            for t in range(3):
                turn_rows(t)
                if t >= 1:
                    e[t - 1] = expert_of(t - 1)
                    up(t - 1, e[t - 1])
            for t in range(n):
                turn_hidden(t)
                if t + 2 < n:
                    e[t + 2] = expert_of(t + 2)
                if t + 3 < n:
                    turn_rows(t + 3)
                if t + 2 < n:
                    up(t + 2, e[t + 2])
                down(t, e[t])


        def hard_attention_dve(dve, step):
            nc.vector.memset(nmT[:].bitcast(F32), 0.0)
            for n in ("q_hi", "q_lo"):
                nc.vector.memset(sel1[n][:].bitcast(F32), 0.0)
            for n in ("k_hi", "k_lo", "mask"):
                nc.vector.memset(sel1k[n][:].bitcast(F32), 0.0)
            nc.vector.memset(kst1[:].bitcast(F32), 0.0)
            nc.vector.memset(krem1[:].bitcast(F32), 0.0)
            step(nc.vector.memset(vrem1[:], 0.0))
            id_q = ident[:].rearrange("p (h f) -> p h f", f=DH)
            id_k = ident[0:DH, 0:DH].unsqueeze(1).to_broadcast([DH, 4, DH])
            nc.vector.memset(sel1k["mask"][0:1, :, 3, 0:1].bitcast(F32), 1.0)
            for tile, quarter, src in ((sel1["q_hi"], 0, id_q), (sel1["q_hi"], 1, id_q), (sel1["q_lo"], 2, id_q),
                                       (sel1k["k_hi"][0:DH], 0, id_k), (sel1k["k_hi"][0:DH], 2, id_k), (sel1k["k_lo"][0:DH], 1, id_k)):
                ins = nc.vector.tensor_copy(tile[:, :, quarter, :], src)
            ins.then_inc(s["sel1_ok"], 1)
            for b in range(B):
                dve.wait_ge(s["qp_ok"], b + 1)
                step(nc.vector.tensor_copy(qp_hi[:, b, :], qp[:, b, :]))
                nc.vector.tensor_tensor(qp_lo[:, b, :], qp[:, b, :], qp_hi[:, b, :].bitcast(F32), ALU.subtract).then_inc(s["qp_split"], 1)
            for b in range(B):
                for qt in range(QT):
                    u = b * QT + qt
                    score = bank[u % 3][:, 0:KEYS]
                    dve.wait_ge(s["hit_pe"], u + 1)
                    step(nc.vector.max(hit8[:, u, :], score))
                    step(nc.vector.max_index(hit8_at[:, u, :], hit8[:, u, :], score))
                    step(nc.vector.tensor_copy(hit_f[:, u:u + 1], hit8_at[:, u, 0:1]))
                    if u >= QT:
                        dve.wait_ge(s["count_pe"], 1)
                    nc.vector.tensor_scalar(hits[:, qt, :], iota_k[:], hit_f[:, u:u + 1], None, ALU.is_equal).then_inc(s["hit_ok"], 1)
            dve.wait_ge(s["count_pe"], 2)
            step(nc.vector.tensor_copy(counts[:], bank[7][:, 0:2 * B]))
            step(nc.vector.tensor_scalar(mask_row[0:1, :], bank[7][0:1, 128:128 + B * KP], 0.5, MASKED, ALU.is_lt, ALU.mult))
            dve.wait_ge(s["mk_pe"], 1)
            for b in range(B):
                nc.vector.tensor_scalar(v1[:, b, 0:DH], bank[3][:, (2 * b) * 16 + DH:(2 * b) * 16 + 2 * DH], counts[:, 2 * b:2 * b + 1], None, ALU.mult)
                nc.vector.tensor_copy(v1[:, b, DH:DH + 1], counts[:, 2 * b:2 * b + 1])
                for j in range(4):
                    rows = slice(32 * j, 32 * j + 32)
                    nc.vector.tensor_scalar(vrem1[rows, b, j, 0:DH], bank[3][rows, (2 * b + 1) * 16 + DH:(2 * b + 1) * 16 + 2 * DH],
                                            counts[rows, 2 * b + 1:2 * b + 2], None, ALU.mult)
                    nc.vector.tensor_copy(vrem1[rows, b, j, DH:DH + 1], counts[rows, 2 * b + 1:2 * b + 2])
            step(nc.vector.tensor_copy(mk_hi[0:DH, :], bank[4][0:DH, 0:B * KP]))
            nc.vector.tensor_tensor(mk_lo[0:DH, :], bank[4][0:DH, 0:B * KP], mk_hi[0:DH, :].bitcast(F32), ALU.subtract).then_inc(s["mk_ok"], 1)
            dve.wait_ge(s["kst1_pe"], 1)
            src = bank[0][:, 0:B * KP].rearrange("p (b k) -> p b k", b=B)
            for a in range(4):
                rows = slice(32 * a, 32 * a + 32)
                nc.vector.tensor_copy(kst1[rows, a], src[rows])
                ins = nc.vector.tensor_copy(krem1[rows, :, a, :], src[rows, :, P:KP])
            ins.then_inc(s["kst1_ok"], 1)
            for u in range(B * NQUAD):
                b, g = divmod(u, NQUAD)
                dve.wait_ge(s["qst1_pe"], u + 1)
                nc.vector.tensor_copy(qst[:, g, b, :], bank[1 + u % 4][:]).then_inc(s["qst1_ok"], 1)

        def hard_attention_pe(pe):
            for b in range(B):
                pe.wait_ge(s["xnT_ok"], 4 + b + 1)
                mm(bank[5 + b][:], small_wT[:, 2, :], xnT[:, b, :], start=True, stop=True).then_inc(s["qp_pe"], 1)
            for b in range(B):
                for half, lhs in enumerate((ctxT[:, b, 0:P], ctxT_rep[:, b].rearrange("p j k -> p (j k)"))):
                    i = 2 * b + half
                    if i == 0:
                        pe.wait_ge(s["xnT_ok"], 6)
                    mm(bank[3][:, i * 16:(i + 1) * 16], lhs, wkvT[:], start=True, stop=True)
            mm(bank[4][0:DH, 0:B * KP], wkvT[:, 0:DH], ctxT[:].rearrange("p b k -> p (b k)"), start=True, stop=True).then_inc(s["mk_pe"], 1)
            for b in range(B):
                pe.wait_ge(s["qp_ok"], b + 1)
                for qt in range(QT):
                    u = b * QT + qt
                    if u >= 3:
                        pe.wait_ge(s["hit_ok"], u - 2)
                    mm(bank[u % 3][:, 0:KEYS], qp[:, b, qt * P:(qt + 1) * P], ctxT[:, b, 0:KEYS], start=True, stop=True).then_inc(s["hit_pe"], 1)
                pe.wait_ge(s["hit_ok"], (b + 1) * QT)
                for half in range(2):
                    for qt in range(QT):
                        mm(bank[7][:, 2 * b + half:2 * b + half + 1], hits[:, qt, half * P:(half + 1) * P], ones_b[:, 0:1],
                           start=(qt == 0), stop=(qt == QT - 1))
                for qt in range(QT):
                    ins = mm(bank[7][0:1, 128 + b * KP:128 + (b + 1) * KP], ones_b[:, 0:1], hits[:, qt, 0:KP],
                             start=(qt == 0), stop=(qt == QT - 1))
                ins.then_inc(s["count_pe"], 1)
            pe.wait_ge(s["mk_ok"], 1)
            pe.wait_ge(s["sel1_ok"], 1)
            dst = bank[0][:, 0:B * KP]
            mm(dst, sel1k["k_hi"][0:DH].rearrange("p a c f -> p (a c f)"), mk_hi[0:DH, :], start=True, stop=False)
            mm(dst, sel1k["k_lo"][0:DH].rearrange("p a c f -> p (a c f)"), mk_lo[0:DH, :], start=False, stop=False)
            mm(dst, sel1k["mask"][0:1].rearrange("p a c f -> p (a c f)"), mask_row[0:1, :], start=False, stop=True).then_inc(s["kst1_pe"], 1)
            for u in range(B * NQUAD):
                b, g = divmod(u, NQUAD)
                pe.wait_ge(s["qp_split"], b + 1)
                if u >= 4:
                    pe.wait_ge(s["qst1_ok"], u - 3)
                dst = bank[1 + u % 4][:]
                for i, n in enumerate(("q_hi", "q_lo")):
                    mm(dst, sel1[n][:, 4 * g:4 * g + 4].rearrange("p a c f -> p (a c f)"), (qp_hi, qp_lo)[i][:, b, :], start=(i == 0), stop=False)
                mm(dst, sel1k["mask"][0:1].rearrange("p a c f -> p (a c f)"), ones_r[0:1, :], start=False, stop=True).then_inc(s["qst1_pe"], 1)
            pe.wait_ge(s["kst1_ok"], 1)
            pe.wait_ge(s["qst1_ok"], B * NQUAD)

        @block.sync
        def _(sp):
            sp.dma_start(ctx_main[:], A["ctx_1024"][:, 0:P, :].rearrange("b k d -> k b d")).then_inc(s["ld_ctx"], 16)
            sp.dma_start(ctx_rem[0:KR], A["ctx_1024"][:, P:KEYS, :].rearrange("b k d -> k b d")).then_inc(s["ld_ctx"], 16)
            sp.dma_start(fm_w[0:DH, :], A["L0_xattn_fm_w"]).then_inc(s["ld_small"], 16)
            sp.dma_start(fm_b[0:DH, :], A["L0_xattn_fm_b"].rearrange("(e a) -> e a", a=1)).then_inc(s["ld_small"], 16)
            sp.dma_start(x[:], A["x"].rearrange("b (t p) d -> p (b t) d", p=P)).then_inc(s["ld_x"], 16)
            sp.dma_start(small_w[:, 0:2, :], A["L0_xattn_fc_w"].rearrange("e (a f) -> e a f", a=2)).then_inc(s["ld_small"], 16)
            sp.dma_start(small_w[:, 2, :], A["L1_xattn_Wq"]).then_inc(s["ld_small"], 16)
            sp.dma_start(small_w[:, 3, :], A["L1_xattn_Wc"]).then_inc(s["ld_small"], 16)
            sp.dma_start(wkv[0:2 * DH, :], A["L1_xattn_Wkv"]).then_inc(s["ld_small"], 16)
            sp.dma_start(fc_b[0:1, :], A["L0_xattn_fc_b"].rearrange("(a e) -> a e", a=1)).then_inc(s["ld_small"], 16)
            for L in range(2):
                sp.dma_start(wr[L][:], A[f"L{L}_ffn_Wr"]).then_inc(s["ld_small"], 16)
                sp.dma_start(br[L][0:1, :], A[f"L{L}_ffn_br"].rearrange("(a e) -> a e", a=1)).then_inc(s["ld_small"], 16)
            sp.dma_start(w1_0[:].rearrange("p (e f) -> p e f", f=HID), A["L0_ffn_W1"].rearrange("e d f -> d e f")).then_inc(r[0]["ld_w"], 16)
            sp.dma_start(w2_0[:].rearrange("p (e c d) -> p e c d", c=4, d=D),
                         A["L0_ffn_W2"].rearrange("e (c p) d -> p e c d", p=P)).then_inc(r[0]["ld_w"], 16)
            experts_sync(sp, 0)
            sp.wait_ge(s["x1_ok"], 2)
            sp.dma_start(w1_1[:].rearrange("p (e f) -> p e f", f=HID), A["L1_ffn_W1"].rearrange("e d f -> d e f")).then_inc(r[1]["ld_w"], 16)
            sp.dma_start(w3_1[:].rearrange("p (e f) -> p e f", f=HID), A["L1_ffn_W3"].rearrange("e d f -> d e f")).then_inc(r[1]["ld_w"], 16)
            sp.wait_ge(s["x1_ok"], 4)
            sp.dma_start(w2_1[:].rearrange("p (e c d) -> p e c d", c=4, d=D),
                         A["L1_ffn_W2"].rearrange("e (c p) d -> p e c d", p=P)).then_inc(r[1]["ld_w"], 16)
            sp.dma_start(gamma[:].rearrange("p e d -> p (e d)"), A["L1_ffn_gamma"].rearrange("e d -> (e d)").partition_broadcast(P)).then_inc(s["ld_gb"], 16)
            sp.dma_start(beta[:].rearrange("p e d -> p (e d)"), A["L1_ffn_beta"].rearrange("e d -> (e d)").partition_broadcast(P)).then_inc(s["ld_gb"], 16)
            experts_sync(sp, 1)
            sp.wait_ge(r[1]["mixed"], 1)
            sp.dma_start(out.rearrange("b (t p) d -> p (b t) d", p=P), x[:]).then_inc(s["stored"], 16)
            sp.wait_ge(s["stored"], 16)

        @block.gpsimd
        def _(pool):
            step = Steps(pool, s["pool_step"])
            step(nc.gpsimd.memset(ident[:], 0.0))
            step(nc.gpsimd.affine_select(out=ident[:], in_=ident[:], pattern=[[-1, P]], compare_op=ALU.not_equal,
                                         fill=1.0, base=0, channel_multiplier=1))
            nc.gpsimd.memset(ones[:], 1.0).then_inc(s["pool_consts"], 1)
            step(nc.gpsimd.memset(bmask[:], 1.0))
            step(nc.gpsimd.affine_select(out=bmask[:], in_=bmask[:], pattern=[[-DH, H]], compare_op=ALU.is_ge,
                                         fill=0.0, base=0, channel_multiplier=1))
            nc.gpsimd.affine_select(out=bmask[:], in_=bmask[:], pattern=[[DH, H]], compare_op=ALU.is_ge,
                                    fill=0.0, base=DH - 1, channel_multiplier=-1).then_inc(s["pool_consts"], 1)
            pool.wait_ge(s["pool_consts"], 2)
            for a in range(2):
                step(nc.gpsimd.memset(kst0[64 * (1 - a):64 * (1 - a) + 64].rearrange("p (n a) b k -> p n a (b k)", a=2)[:, :, a].bitcast(F32), 0.0))
            nc.gpsimd.memset(ind[:].bitcast(F32), 0.0)
            nc.gpsimd.memset(ind_rem[:].bitcast(F32), 0.0)
            nc.gpsimd.memset(nmT[:].bitcast(F32), 0.0)
            nc.gpsimd.memset(krem0[:].bitcast(F32), 0.0).then_inc(s["pool_consts"], 1)
            nc.gpsimd.memset(vrem0[:], 0.0).then_inc(s["pool_consts"], 1)
            nc.gpsimd.memset(ones_r[:].bitcast(F32), 1.0)
            nc.gpsimd.iota(iota_e[:], pattern=[[1, 16]], base=0, channel_multiplier=0, allow_small_or_imprecise_dtypes=True)
            nc.gpsimd.iota(iota_s[:], pattern=[[1, 32]], base=0, channel_multiplier=0, allow_small_or_imprecise_dtypes=True)
            nc.gpsimd.iota(iota_k[:, 0:P], pattern=[[1, P]], base=0, channel_multiplier=0, allow_small_or_imprecise_dtypes=True)
            nc.gpsimd.iota(iota_k[:, P:], pattern=[[0, 4], [1, 32]], base=P, channel_multiplier=0, allow_small_or_imprecise_dtypes=True)
            step(nc.gpsimd.memset(ones_b[:], 1.0))
            nc.gpsimd.affine_select(out=tri[:], in_=ones_b[:], pattern=[[1, P]], compare_op=ALU.is_gt,
                                    fill=0.0, base=0, channel_multiplier=-1).then_inc(s["pool_consts"], 1)
            step(nc.gpsimd.memset(zero_rows[:], 0.0))
            for L in range(2):
                pool.dma_start(slots_x[L].rearrange("(t p) d -> p t d", p=P), zero_rows[:].unsqueeze(1).to_broadcast([P, TILES[L], D])).then_inc(r[L]["zero_x"], 16)
            experts_pool(pool, step, 0)
            experts_pool(pool, step, 1)

        @block.vector
        def _(dve):
            step = Steps(dve, s["dve_step"])
            step(nc.vector.memset(ctxT[:], 0.0))
            nc.vector.memset(sel0["q_hi"][:].bitcast(F32), 0.0)
            nc.vector.memset(sel0["q_lo"][:].bitcast(F32), 0.0)
            nc.vector.memset(sel0["k_hi"][:].bitcast(F32), 0.0)
            step(nc.vector.memset(sel0["k_lo"][:].bitcast(F32), 0.0))
            dve.wait_ge(s["ld_small"], LD_SMALL)
            dve.wait_ge(s["pool_consts"], POOL_CONSTS)
            nc.vector.tensor_copy(fm_rep[0:DH], fm_w[0:DH, :].unsqueeze(1).to_broadcast([DH, H, DH]))
            nc.vector.tensor_copy(sign_id[0:DH, :, 0, :], ident[0:DH, 0:DH].unsqueeze(1).to_broadcast([DH, H, DH]))
            step(nc.vector.tensor_scalar(sign_id[0:DH, :, 1, :], ident[0:DH, 0:DH].unsqueeze(1).to_broadcast([DH, H, DH]),
                                         -1.0, None, ALU.mult))
            nc.vector.tensor_copy(v0[:, :, :, F0:F0 + 1], ones[:, 0:B * H].rearrange("p (b h o) -> p b h o", b=B, o=1)).then_inc(s["fm_ok"], 1)
            sel_in = ident[:].rearrange("p (h f) -> p h f", f=F0)
            for name, quarters in (("q_hi", (0, 1)), ("q_lo", (2, 3)), ("k_hi", (0, 2)), ("k_lo", (1, 3))):
                for quarter in quarters:
                    ins = nc.vector.tensor_copy(sel0[name][:, :, quarter, :], sel_in)
            step(ins)
            step(nc.vector.tensor_tensor(pair32[0:32, :], ident[0:32, 0:16], ident[0:32, 16:32], ALU.add))
            nc.vector.tensor_copy(ind_rem[0:32], pair32[0:32, :].unsqueeze(2).to_broadcast([32, H, 32]))
            nc.vector.tensor_copy(ind[0:32], pair32[0:32, :].unsqueeze(2).to_broadcast([32, H, P])).then_inc(s["consts_dve"], 1)
            dve.wait_ge(s["ld_x"], 16)
            layer_norm(dve, step, s["xn_ok"])
            dve.wait_ge(s["ctxT_pe"], 1)
            step(nc.vector.tensor_copy(ctxT[:, :, 0:KEYS], bank[0][:, 0:B * KP].rearrange("p (b k) -> p b k", b=B)[:, :, 0:KEYS]))
            nc.vector.tensor_copy(ctxT_rep[:], ctxT[:, :, P:KP].unsqueeze(2).to_broadcast([P, B, 4, 32])).then_inc(s["ctxT_ok"], 1)
            dve.wait_ge(s["fm_pe"], 1)
            nc.vector.tensor_copy(wkvT[:], bank[2][:, 0:2 * DH])
            fmT = bank[2][:, 16:16 + DH].unsqueeze(1).to_broadcast([P, H, DH])
            mask = bmask[:].unsqueeze(2).to_broadcast([P, H, DH])
            nc.vector.tensor_copy(bias_col[:], bank[2][:, 24:25])
            nc.vector.tensor_copy(bias_row[0:1, :], bank[2][0:1, 128:128 + H * F0])
            nc.vector.tensor_tensor(wexp[:, :, 0, :], fmT, mask, ALU.mult)
            nc.vector.scalar_tensor_tensor(out=wexp[:, :, 1, :], in0=fmT, scalar=-1.0, in1=mask,
                                           op0=ALU.mult, op1=ALU.mult).then_inc(s["fm2_ok"], 1)
            for t in range(2):
                dve.wait_ge(s["kf_ok"], t + 1)
                step(nc.vector.tensor_copy(kf_hi[:, t, :], kf[:, t, :]))
                nc.vector.tensor_tensor(kf_lo[:, t, :], kf[:, t, :], kf_hi[:, t, :].bitcast(F32), ALU.subtract).then_inc(s["kf_split"], 1)
            for b in range(B):
                for t in range(2):
                    dve.wait_ge(s["f_ok"], 2 * b + t + 1)
                    step(nc.vector.tensor_copy(f_hi[:, t, b, :], f[:, t, b, :]))
                    nc.vector.tensor_tensor(f_lo[:, t, b, :], f[:, t, b, :], f_hi[:, t, b, :].bitcast(F32),
                                            ALU.subtract).then_inc(s["f_split"], 1)
            for p in range(NPAIR):
                dve.wait_ge(s["kst_pe"], p + 1)
                src = bank[(5, 6, 7, 0)[p % 4]][:, 0:B * KP].rearrange("p (b k) -> p b k", b=B)
                for a in range(2):
                    j = (2 * p + a) % 4
                    nc.vector.tensor_copy(kst0[64 * a:64 * a + 64, 2 * p + a], src[64 * a:64 * a + 64])
                    ins = nc.vector.tensor_copy(krem0[64 * a:64 * a + 64, :, p, j, 0:KR], src[64 * a:64 * a + 64, :, P:KEYS])
                ins.then_inc(s["kst_ok"], 1)
            for u in range(0, B * NPAIR, 2):
                b, p = divmod(u, NPAIR)
                dve.wait_ge(s["qst_pe"], u + 1)
                nc.vector.tensor_copy(qst[:, p, b, :], bank[1 + u % 4][:]).then_inc(s["qst_dve"], 1)

            attention_dve(dve, step, 0, F0 + 1)
            dve.wait_ge(s["x1_ok"], 2)
            layer_norm(dve, step, s["xn_ok"])
            route_dve(dve, step, 0)
            experts_dve(dve, step, 0)
            dve.wait_ge(r[0]["mixed"], 1)
            layer_norm(dve, step, s["xn_ok"])
            hard_attention_dve(dve, step)
            attention_dve(dve, step, 1, DH + 1)
            dve.wait_ge(s["x1_ok"], 4)
            layer_norm(dve, step, s["xn_ok"])
            route_dve(dve, step, 1)
            dve.wait_ge(s["ld_gb"], 32)
            experts_dve(dve, step, 1)

        @block.scalar
        def _(act):
            act.wait_ge(s["wT_pe"], 1)
            nc.scalar.copy(small_wT[:].rearrange("p a d -> p (a d)"), bank[1][:]).then_inc(s["wT_ok"], 1)
            copy_xnT(act, 0)
            act.wait_ge(s["fm2_ok"], 1)
            for t in range(2):
                act.wait_ge(s["zk_pe"], t + 1)
                nc.scalar.activation(kf[:, t, :], bank[1 + t][:, 0:B * KP], ACT.Exp, bias=bias_col[:]).then_inc(s["kf_ok"], 1)
            for b in range(B):
                for t in range(2):
                    act.wait_ge(s["zq_pe"], 2 * b + t + 1)
                    nc.scalar.activation(f[:, t, b, :], bank[(5, 6, 7, 0)[2 * b + t]][:], ACT.Exp,
                                         bias=bias_col[:]).then_inc(s["f_ok"], 1)
            act.wait_ge(s["pool_consts"], POOL_CONSTS)
            act.wait_ge(s["fm_ok"], 1)
            for b in range(B):
                act.wait_ge(s["vz_pe"], b + 1)
                nc.scalar.activation(v0[:, b, :, 0:F0], bank[3 + b][:, 0:H * F0].rearrange("p (h v) -> p h v", h=H), ACT.Exp)
                for j in range(4):
                    rows = slice(32 * j, 32 * j + KR)
                    nc.scalar.activation(vrem0[rows, b, :, j, 0:F0],
                                         bank[3 + b][rows, H * F0:2 * H * F0].rearrange("p (g j v) -> p g j v", g=NQUAD, j=4)[:, :, j, :],
                                         ACT.Exp)
                    ins = nc.scalar.copy(vrem0[rows, b, :, j, F0], ones[rows, 0:NQUAD])
                ins.then_inc(s["v_ok"], 1)
            for u in range(1, B * NPAIR, 2):
                b, p = divmod(u, NPAIR)
                act.wait_ge(s["qst_pe"], u + 1)
                nc.scalar.copy(qst[:, p, b, :], bank[1 + u % 4][:]).then_inc(s["qst_act"], 1)
            attention_act(act, 0, SCALE0)
            copy_xnT(act, 1)
            experts_act(act, 0)
            copy_xnT(act, 2)
            for b in range(B):
                act.wait_ge(s["qp_pe"], b + 1)
                nc.scalar.copy(qp[:, b, :], bank[5 + b][:]).then_inc(s["qp_ok"], 1)
            attention_act(act, 1, SCALE1)
            copy_xnT(act, 3)
            experts_act(act, 1)

        @block.tensor
        def _(pe):
            pe.wait_ge(s["pool_consts"], 1)
            pe.wait_ge(s["ld_ctx"], 32)
            for b in range(B):
                nc.tensor.transpose(bank[0][:, b * KP:b * KP + P], ctx_main[:, b, :], ident[:])
                ins = nc.tensor.transpose(bank[0][:, b * KP + P:b * KP + KEYS], ctx_rem[0:KR, b, :], ident[0:KR, 0:KR])
            ins.then_inc(s["ctxT_pe"], 1)
            pe.wait_ge(s["ld_small"], LD_SMALL)
            for a in range(4):
                ins = nc.tensor.transpose(bank[1][:, a * P:(a + 1) * P], small_w[:, a, :], ident[:])
            ins.then_inc(s["wT_pe"], 1)
            nc.tensor.transpose(bank[2][:, 0:2 * DH], wkv[0:2 * DH, :], ident[0:2 * DH, 0:2 * DH])
            pe.wait_ge(s["fm_ok"], 1)
            mm(bank[2][:, 16:16 + DH], fm_rep[0:DH].rearrange("e h d -> e (h d)"), ident[0:DH, 0:DH], start=True, stop=True)
            mm(bank[2][:, 24:25], sign_id[0:DH, 0:8].rearrange("e h s f -> e (h s f)"), fm_b[0:DH, :], start=True, stop=True)
            mm(bank[2][0:1, 128:128 + H * F0], fm_b[0:DH, :], sign_id[0:DH].rearrange("e h s f -> e (h s f)"),
               start=True, stop=True).then_inc(s["fm_pe"], 1)
            pe.wait_ge(s["xn_ok"], 1)
            transpose_xn(pe)
            pe.wait_ge(s["wT_ok"], 1)
            pe.wait_ge(s["ctxT_ok"], 1)
            pe.wait_ge(s["fm2_ok"], 1)
            wexp_t = wexp[:].rearrange("p h s e -> p (h s e)")
            for t in range(2):
                mm(bank[1 + t][:, 0:B * KP], wexp_t[:, t * P:(t + 1) * P], ctxT[:].rearrange("p b k -> p (b k)"),
                   start=True, stop=True).then_inc(s["zk_pe"], 1)
            for b in range(B):
                pe.wait_ge(s["xnT_ok"], b + 1)
                for t in range(2):
                    mm(bank[(5, 6, 7, 0)[2 * b + t]][:], wexp_t[:, t * P:(t + 1) * P], xnT[:, b, :],
                       start=True, stop=True).then_inc(s["zq_pe"], 1)
            for b in range(B):
                for half, lhs in enumerate((ctxT[:, b, 0:P], ctxT_rep[:, b].rearrange("p j k -> p (j k)"))):
                    dst = bank[3 + b][:, half * H * F0:(half + 1) * H * F0]
                    mm(dst, lhs, wexp_t[:], start=True, stop=False)
                    ins = mm(dst, ones[0:1, 0:P], bias_row[0:1, :], start=False, stop=True)
                ins.then_inc(s["vz_pe"], 1)
            pe.wait_ge(s["f_ok"], 4)
            pe.wait_ge(s["kf_split"], 2)
            pe.wait_ge(s["consts_dve"], 1)
            for p in range(NPAIR):
                t, i = divmod(p, 4)
                if p >= 4:
                    pe.wait_ge(s["kst_ok"], p - 3)
                dst = bank[(5, 6, 7, 0)[p % 4]][:, 0:B * KP]
                mm(dst, sel0["k_hi"][:, 2 * i:2 * i + 2].rearrange("p a c f -> p (a c f)"), kf_hi[:, t, :], start=True, stop=False)
                mm(dst, sel0["k_lo"][:, 2 * i:2 * i + 2].rearrange("p a c f -> p (a c f)"), kf_lo[:, t, :],
                   start=False, stop=True).then_inc(s["kst_pe"], 1)
            pe.wait_ge(s["kf_ok"], 2)
            pe.wait_ge(s["v_ok"], 2)
            for u in range(B * NPAIR):
                b, p = divmod(u, NPAIR)
                t, i = divmod(p, 4)
                pe.wait_ge(s["f_split"], 2 * b + t + 1)
                if u >= 4:
                    wait_qst(pe, u - 4)
                dst = bank[1 + u % 4][:]
                mm(dst, sel0["q_hi"][:, 2 * i:2 * i + 2].rearrange("p a c f -> p (a c f)"), f_hi[:, t, b, :], start=True, stop=False)
                mm(dst, sel0["q_lo"][:, 2 * i:2 * i + 2].rearrange("p a c f -> p (a c f)"), f_lo[:, t, b, :],
                   start=False, stop=True).then_inc(s["qst_pe"], 1)
            pe.wait_ge(s["kst_ok"], NPAIR)
            pe.wait_ge(s["qst_dve"], B * NPAIR // 2)
            pe.wait_ge(s["qst_act"], B * NPAIR // 2)

            def query(b, h, cols):
                return qst[:, h // 2, b, cols]

            def keys(b, h, n):
                return kst0[:, h, b, 0:n]

            def rem_scores(dst, b, hg):
                for i in range(2):
                    p = 2 * hg + i
                    mm(dst, krem0[:, b, p].rearrange("p j k -> p (j k)"), qst[:, p, b, :], start=(i == 0), stop=False)

            attention_pe(pe, 0, query, keys, rem_scores, lambda b, h: v0[:, b, h, :], lambda b, hg: vrem0[:, b, hg], F0 + 1)
            pe.wait_ge(s["xn_ok"], 2)
            transpose_xn(pe)
            experts_pe(pe, 0)
            pe.wait_ge(s["xn_ok"], 3)
            transpose_xn(pe)
            hard_attention_pe(pe)
            attention_pe(pe, 1, lambda b, h, cols: qst[:, h // 4, b, cols], lambda b, h, n: kst1[:, h % 4, b, 0:n],
                         lambda dst, b, hg: mm(dst, krem1[:, b].rearrange("p a k -> p (a k)"), qst[:, hg, b, :], start=True, stop=False),
                         lambda b, h: v1[:, b, :], lambda b, hg: vrem1[:, b], DH + 1)
            pe.wait_ge(s["xn_ok"], 4)
            transpose_xn(pe)
            experts_pe(pe, 1)

_OUTS = [((B, S, D), "float32")]


def kernel(**inputs):
    import numpy as _np
    import concourse.bacc as _bacc
    from concourse import mybir as _mybir
    from concourse.bass_utils import run_bass_kernel_spmd as _run

    nc = _bacc.Bacc("TRN2", target_bir_lowering=False, num_devices=1)
    arrays, args = {}, {}
    for name in inputs:
        a = _np.ascontiguousarray(inputs[name])
        arrays[f"in_{name}_dram"] = a
        args[name] = nc.dram_tensor(f"in_{name}_dram", a.shape, _mybir.dt.from_np(a.dtype), kind="ExternalInput").ap()
    out = nc.dram_tensor("out_0_dram", _OUTS[0][0], _mybir.dt.float32, kind="ExternalOutput").ap()
    build(nc, args, out)
    r = _run(nc, [arrays], core_ids=[0])
    return r.results[0]["out_0_dram"]
```

```python
import numpy as np
import concourse.bass as bass
from concourse import mybir
from contextlib import ExitStack

F32 = mybir.dt.float32
F32R = mybir.dt.float32r
BF16 = mybir.dt.bfloat16
I32 = mybir.dt.int32
U32 = mybir.dt.uint32
ALU = mybir.AluOpType
ACT = mybir.ActivationFunctionType
AX = mybir.AxisListType

P = 128
B, S, D = 2, 512, 128
T = B * S // P
QT = S // P
KEYS = 154
KM, KR = P, KEYS - P
KP = 160
H, DH = 16, D // 16
F0 = 2 * DH
NPAIR, NQUAD = H // 2, H // 4
GATHERED = tuple(f"gathered_{i}" for i in range(14))
SCATTERED = tuple(f"scattered_{i}" for i in range(4))
HID = 512
EXPERTS = (8, 16)
TILES = tuple((2 * B * S - E) // P + E for E in EXPERTS)
EPS = 1e-5
MASKED = -float(2 ** 100)
SCALE0 = float(1.0 / np.sqrt(np.float32(D)))
SCALE1 = float(np.float32(1.0 / np.sqrt(DH)))


class Steps:

    def __init__(self, engine, semaphore):
        self.engine, self.semaphore, self.count = engine, semaphore, 0

    def __call__(self, instruction):
        self.count += 1
        instruction.then_inc(self.semaphore, 1)
        self.engine.wait_ge(self.semaphore, self.count)


def build(nc, A, out, stop=9):
    ctx = ExitStack()
    with ctx:
        base = [(nc.sbuf_base + 31) // 32 * 32]

        def sb(name, shape, dt):
            n = int(np.prod(shape[1:])) * (2 if dt == BF16 else 4)
            t = nc.alloc_sbuf_tensor_at(name, shape, dt, offset=base[0])
            base[0] += (n + 31) // 32 * 32
            return t

        def sem(name):
            return ctx.enter_context(nc.semaphore(name))

        bank = [ctx.enter_context(nc.psum_tensor(f"bank{i}", [P, 512], F32)) for i in range(8)]

        ident = sb("ident", [P, P], F32)
        ones = sb("ones", [P, P], F32)
        ones_r = sb("ones_r", [P, 512], F32R)
        ones_b = sb("ones_b", [P, P], BF16)
        tri = sb("tri", [P, P], BF16)
        iota_e = sb("iota_e", [P, 16], F32)
        iota_s = sb("iota_s", [P, 32], F32)
        iota_k = sb("iota_k", [P, 2 * P], F32)
        x = sb("x", [P, T, D], F32)
        xn = sb("xn", [P, T, D], F32)
        xnT = sb("xnT", [P, B, S], F32)
        stats = sb("stats", [P, T, 6], F32)
        mv = sb("mv", [P, T, 2], F32)
        rstd = sb("rstd", [P, T], F32)
        var = sb("var", [P, T], F32)
        guess = sb("guess", [P, T], F32)
        newton = sb("newton", [P, T], F32)
        ctx_main = sb("ctx_main", [P, B, D], F32)
        ctx_rem = sb("ctx_rem", [P, B, D], F32)
        ctxT = sb("ctxT", [P, B, KP], F32)
        ctxT_rep = sb("ctxT_rep", [P, B, 4, 32], F32)
        small_w = sb("small_w", [P, 4, D], F32)
        small_wT = sb("small_wT", [P, 4, D], F32)
        wkv = sb("wkv", [P, D], F32)
        wkvT = sb("wkvT", [P, 2 * DH], F32)
        fm_w = sb("fm_w", [P, DH], F32)
        fm_b = sb("fm_b", [P, 1], F32)
        fc_b = sb("fc_b", [P, D], F32)
        ind = sb("ind", [P, H, P], F32R)
        ind_rem = sb("ind_rem", [P, H, 32], F32R)
        pair32 = sb("pair32", [P, H], F32)
        wr = [sb(f"wr{L}", [P, E], F32) for L, E in enumerate(EXPERTS)]
        br = [sb(f"br{L}", [P, E], F32) for L, E in enumerate(EXPERTS)]
        logits = sb("logits", [P, T, 16], F32)
        top8 = sb("top8", [P, T, 8], F32)
        top8_at = sb("top8_at", [P, T, 8], U32)
        top2_at = sb("top2_at", [P, 2, T], F32)
        onehot = sb("onehot", [P, 2, T, 16], F32)
        chosen = sb("chosen", [P, T, 16], BF16)
        gate = sb("gate", [P, 4, T], F32)
        counts_f = sb("counts_f", [P, 16], F32)
        counts_i = sb("counts_i", [P, 2, 16], I32)
        tiles_f = sb("tiles_f", [P, 16], F32)
        scan = [sb(f"scan{i}", [P, 32], F32) for i in range(2)]
        rank = sb("rank", [P, T, 16], F32)
        ranked = sb("ranked", [P, 2, T, 16], F32)
        slot_f = sb("slot_f", [P, 2, T], F32)
        slot_i = sb("slot_i", [P, 3, 2, T], I32)
        slot_rt = sb("slot_rt", [P, 2, 2, T], F32)
        slot_gate = sb("slot_gate", [P, 32], F32)
        slot_from = sb("slot_from", [P, 32], I32)
        slot_to = sb("slot_to", [P, 32], I32)
        slot_none = sb("slot_none", [P, 32], F32)
        place_1 = sb("place_1", [P, 2, T], F32)
        iota_r = sb("iota_r", [P, P], F32)
        spare_row = sb("spare_row", [P, 32], F32)
        before = sb("before", [P, 32, 16], F32)
        expert_f = sb("expert_f", [P, 32], F32)
        expert_i = sb("expert_i", [P, 32], I32)
        shared = base[0]
        mx = sb("mx", [P, B, QT, H], F32)
        nm_hi = sb("nm_hi", [P, B, QT, H], F32R)
        nm = sb("nm", [P, B, QT, 2, H], F32)
        nmT = sb("nmT", [P, B, S], F32R)
        qst = sb("qst", [P, NPAIR, B, S], F32R)
        prob = sb("prob", [P, 2, 5, 512], F32)
        recips = xnT
        oT = sb("oT", [P, 2, B, S], F32)
        f = prob[:, 0].rearrange("p a q -> p (a q)")[:, 0:2 * B * S].rearrange("p (n b q) -> p n b q", n=2, b=B)
        kf = prob[:, 1].rearrange("p a q -> p (a q)")[:, 0:2 * B * KP].rearrange("p (n k) -> p n k", n=2)
        shared_end = base[0]
        base[0] = shared
        gx = sb("gx", [P, max(TILES), D], F32)
        gxT = sb("gxT", [P, 2, P], F32)
        parts = gx[:, 0:2 * T, :]
        slots_at = base[0]
        slot_hit = sb("slot_hit", [P, 2 * T, 32], F32)
        slot_tile = sb("slot_tile", [P, 2 * T, 2, 32], F32)
        slot_row = sb("slot_row", [P, 2 * T, P], F32)
        slots_end, base[0] = base[0], slots_at
        hid = sb("hid", [P, 2, HID], F32)
        act_h = sb("act_h", [P, 2, HID], F32)
        hidT = sb("hidT", [P, 2, HID], F32)
        y = sb("y", [P, 8, D], F32)
        ys = sb("ys", [P, 4, D], F32)
        y_stats = sb("y_stats", [P, 4, 6], F32)
        y_mv = sb("y_mv", [P, 4, 2], F32)
        y_root = sb("y_root", [P, 5, 4], F32)
        spare = base[0]
        assert slots_end <= spare
        b1_cols = sb("b1_cols", [P, 32 + 8], F32)
        b1_hi = sb("b1_hi", [P, 32 + 8], F32R)
        b1_lo = sb("b1_lo", [P, 32 + 8], F32R)
        b1_rows = sb("b1_rows", [P, EXPERTS[0] * (HID + D)], F32R)
        assert base[0] <= shared_end, (base[0], shared_end)
        base[0] = spare
        gamma = sb("gamma", [P, EXPERTS[1], D], F32)
        beta = sb("beta", [P, EXPERTS[1], D], F32)
        assert base[0] <= shared_end, (base[0], shared_end)
        base[0] = scratch0 = shared_end
        bmask = sb("bmask", [P, H], F32)
        sign_id = sb("sign_id", [P, H, 2, DH], F32)
        fm_rep = sb("fm_rep", [P, H, DH], F32)
        wexp = sb("wexp", [P, H, 2, DH], F32)
        bias_col = sb("bias_col", [P, 1], F32)
        bias_row = sb("bias_row", [P, H * F0], F32)
        f_hi = sb("f_hi", [P, 2, B, S], F32R)
        f_lo = sb("f_lo", [P, 2, B, S], F32R)
        kf_hi = sb("kf_hi", [P, 2, B * KP], F32R)
        kf_lo = sb("kf_lo", [P, 2, B * KP], F32R)
        sel0 = {n: sb(f"sel0_{n}", [P, 8, 4, F0], F32R) for n in ("q_hi", "q_lo", "k_hi", "k_lo")}
        kst0 = sb("kst0", [P, H, B, KP], F32R)
        krem0 = sb("krem0", [P, B, NPAIR, 4, 32], F32R)
        scratch0_end = base[0]
        base[0] = scratch0
        w1_1 = sb("w1_1", [P, EXPERTS[1] * HID], F32)
        w3_1 = sb("w3_1", [P, EXPERTS[1] * HID], F32)
        base[0] = weights0 = max(base[0], scratch0_end)
        w1_0 = sb("w1_0", [P, EXPERTS[0] * HID], F32)
        w2_0 = sb("w2_0", [P, EXPERTS[0] * HID], F32)
        base[0] = weights0
        v0 = sb("v0", [P, B, NQUAD, 4 * (8 + 1) * F0], F32)
        vrem0 = sb("vrem0", [P, B, NQUAD, 8 * F0], F32)
        base[0] = weights0
        w2_1 = sb("w2_1", [P, EXPERTS[1] * HID], F32)
        base[0] = weights0
        qp = sb("qp", [P, B, S], F32)
        qp_hi = sb("qp_hi", [P, B, S], F32R)
        qp_lo = sb("qp_lo", [P, B, S], F32R)
        sel1 = {n: sb(f"sel1_{n}", [P, H, 4, DH], F32R) for n in ("q_hi", "q_lo")}
        sel1k = {n: sb(f"sel1_{n}", [P, 4, 4, DH], F32R) for n in ("k_hi", "k_lo", "mask")}
        hits = sb("hits", [P, QT, 2 * P], BF16)
        hit8 = sb("hit8", [P, T, 8], F32)
        hit8_at = sb("hit8_at", [P, T, 8], U32)
        hit_f = sb("hit_f", [P, T], F32)
        counts = sb("counts", [P, 2 * B], F32)
        mask_row = sb("mask_row", [P, B * KP], F32R)
        mk_hi = sb("mk_hi", [P, B * KP], F32R)
        mk_lo = sb("mk_lo", [P, B * KP], F32R)
        kst1 = sb("kst1", [P, 4, B, KP], F32R)
        krem1 = sb("krem1", [P, B, 4, 32], F32R)
        v1 = sb("v1", [P, B, 4 * (8 + 1) * DH], F32)
        vrem1 = sb("vrem1", [P, B, 8 * DH], F32)
        normed = [nc.dram_tensor(f"normed{L}", (B * S, D), F32, kind="Internal").ap() for L in range(2)]
        results = [nc.dram_tensor(f"results{L}", (2 * B * S + TILES[L] * P, D), F32, kind="Internal").ap() for L in range(2)]

        s = {n: sem(n) for n in (
            "ld_x", "ld_ctx", "ld_small", "pool_step", "pool_consts", "dve_zeroed", "dve_step", "act_step",
            "xn_ok", "ctxT_pe", "wT_pe", "ctxT_ok", "wT_ok", "xnT_pe", "xnT_ok",
            "fm_pe", "fm_ok", "fm2_pe", "fm2_ok", "zq_pe", "f_ok", "zk_pe", "kf_ok", "vz_pe", "v_ok", "f_split",
            "kf_split", "consts_dve", "kst_pe", "kst_ok", "qst_pe", "qst_dve", "qst_act", "score_pe", "max_ok", "nm_ok",
            "nmT_pe", "nmT_ok", "prob_pe", "prob_ok", "pv_pe", "o_ok", "oT_pe", "oT_ok", "fc_pe", "x1_ok", "stored",
            "ld_b1", "ld_b1_rows", "ld_gb", "qp_pe", "qp_ok", "qp_split", "sel1_ok", "hit_pe", "hit_ok", "count_pe", "count_ok",
            "mk_pe", "mk_ok", "kst1_pe", "kst1_ok", "qst1_pe", "qst1_ok", "b1_ok")}
        r = [{n: sem(f"{n}_L{L}") for n in (
            "ld_w", "ld_w2", "logits_pe", "logits_ok", "diff_ok", "exp_ok", "chosen_ok", "rank_pe", "slots_ok", "experts_ok",
            "saved", "slot_hit_ok", "slot_pe", *GATHERED, *SCATTERED, "gxT_pe", "gxT_ok", "up_pe", "act_ok", "hid_ok", "hidT_pe", "hidT_ok", "y_pe",
            "y_ok", "y_copied", "y_normed", "y_stats_ok", "mixed", "summed")} for L in range(2)]

        block = ctx.enter_context(nc.Block())

        LD_SMALL = 16 * 11

        POOL_CONSTS = 6

        def inverse_root(step, variance, var, guess, newton, root):
            step(nc.vector.tensor_scalar(var, variance, EPS, None, ALU.add))
            step(nc.vector.tensor_scalar(guess.bitcast(I32), var.bitcast(I32), 1, None, ALU.arith_shift_right))
            step(nc.vector.tensor_scalar(root.bitcast(I32), guess.bitcast(I32), -1.0, float(0x5F3759DF), ALU.mult, ALU.add))
            for _ in range(3):
                step(nc.vector.tensor_tensor(newton, root, root, ALU.mult))
                step(nc.vector.scalar_tensor_tensor(out=newton, in0=newton, scalar=-0.5, in1=var, op0=ALU.mult, op1=ALU.mult))
                step(nc.vector.scalar_tensor_tensor(out=root, in0=newton, scalar=1.5, in1=root, op0=ALU.add, op1=ALU.mult))

        def layer_norm(dve, step, done):
            for t in range(T):
                ins = nc.vector.bn_stats(stats[:, t, :], x[:, t, :])
            step(ins)
            for t in range(T):
                ins = nc.vector.bn_aggr(mv[:, t, :], stats[:, t, :])
            step(ins)
            inverse_root(step, mv[:, :, 1], var[:], guess[:], newton[:], rstd[:])
            for t in range(T):
                ins = nc.vector.tensor_scalar(xn[:, t, :], x[:, t, :], mv[:, t, 0:1], rstd[:, t:t + 1],
                                              ALU.subtract, ALU.mult)
            ins.then_inc(done, 1)

        def max_tile(dve, L, b, qt):
            for g in range(6):
                n = min(3, H - 3 * g)
                u = (b * QT + qt) * 6 + g
                dve.wait_ge(s["score_pe"], L * B * QT * 6 + u + 1)
                ins = nc.vector.tensor_reduce(mx[:, b, qt, 3 * g:3 * g + n],
                                              bank[5 + u % 2][:, 0:n * KEYS].rearrange("p (h k) -> p h k", h=n),
                                              AX.X, ALU.max)
                ins.then_inc(s["max_ok"], 1)

        def negate_max(dve, step, L, b):
            dve.wait_ge(s["max_ok"], (L * B + b + 1) * QT * 6)
            step(nc.vector.tensor_scalar(nm_hi[:, b], mx[:, b], -1.0, None, ALU.mult))
            nc.vector.tensor_copy(nm[:, b, :, 0, :], nm_hi[:, b].bitcast(F32))
            nc.vector.scalar_tensor_tensor(out=nm[:, b, :, 1, :], in0=mx[:, b], scalar=-1.0, in1=nm_hi[:, b].bitcast(F32),
                                           op0=ALU.mult, op1=ALU.subtract).then_inc(s["nm_ok"], 1)

        def turned_max(dve, L, b):
            dve.wait_ge(s["nmT_pe"], L * B + b + 1)
            nc.vector.tensor_copy(nmT[0:32, b, :], bank[7][0:32, :]).then_inc(s["nmT_ok"], 1)

        def normalise(dve, step, L, b, hg):
            g = (L * B + b) * NQUAD + hg
            rows = 4 * (F0 if L == 0 else DH)
            acc = bank[(0, 4)[g % 2]]
            n, at = divmod(hg * rows, P)
            dve.wait_ge(s["pv_pe"], g + 1)
            recip = recips[:, g % 2, :]
            step(nc.vector.reciprocal(recip[0:rows, :], acc[rows:2 * rows, :]))
            nc.vector.tensor_tensor(oT[at:at + rows, n, b, :], acc[0:rows, :], recip[0:rows, :], ALU.mult).then_inc(s["o_ok"], 1)

        def add_projected(dve, L, b):
            dve.wait_ge(s["fc_pe"], L * B + b + 1)
            nc.vector.tensor_tensor(x[:, b * QT:(b + 1) * QT, :], x[:, b * QT:(b + 1) * QT, :],
                                    bank[5 + b][:].rearrange("p (q e) -> p q e", q=QT), ALU.add).then_inc(s["x1_ok"], 1)

        def attention_dve(dve, step, L):
            for qt in range(QT):
                max_tile(dve, L, 0, qt)
            negate_max(dve, step, L, 0)
            turned_max(dve, L, 0)
            for hg in range(NQUAD):
                max_tile(dve, L, 1, hg)
                if hg == NQUAD - 1:
                    negate_max(dve, step, L, 1)
                if hg:
                    normalise(dve, step, L, 0, hg - 1)
            turned_max(dve, L, 1)
            normalise(dve, step, L, 0, NQUAD - 1)
            for hg in range(NQUAD):
                normalise(dve, step, L, 1, hg)
                if hg == 1:
                    add_projected(dve, L, 0)
            add_projected(dve, L, 1)

        def attention_act(act, L, scale):
            for g in range(B * NQUAD):
                group = L * B * NQUAD + g
                if group >= 2:
                    act.wait_ge(s["pv_pe"], group - 1)
                for i in range(5):
                    u = g * 5 + i
                    act.wait_ge(s["prob_pe"], L * B * NQUAD * 5 + u + 1)
                    nc.scalar.activation(prob[:, group % 2, i, :], bank[1 + u % 3][:], ACT.Exp,
                                         scale=scale).then_inc(s["prob_ok"], 1)

        mm = nc.tensor.matmul

        def wait_qst(pe, u):
            pe.wait_ge(s["qst_act" if u % 2 else "qst_dve"], u // 2 + 1)

        def transpose_xn(pe):
            for t in range(T):
                b, qt = divmod(t, QT)
                ins = nc.tensor.transpose(bank[3 + b][:, qt * P:(qt + 1) * P], xn[:, t, :], ident[:])
            ins.then_inc(s["xnT_pe"], 1)

        def copy_xnT(act, n):
            act.wait_ge(s["xnT_pe"], n + 1)
            for b in range(B):
                nc.scalar.copy(xnT[:, b, :], bank[3 + b][:]).then_inc(s["xnT_ok"], 1)

        def attention_pe(pe, L, heads_of_stack, query, keys, rem_scores, values, rem_values, beside=lambda i: None):
            first = L * B * NQUAD

            def score_part(b, qt, g):
                u = ((L * B + b) * QT + qt) * 6 + g
                if u % (B * QT * 6) >= 2:
                    pe.wait_ge(s["max_ok"], u - 1)
                h, end = 3 * g, min(3 * g + 3, H)
                at = 0
                while h < end:
                    n = min(end, (h // heads_of_stack + 1) * heads_of_stack) - h
                    ins = mm(bank[5 + u % 2][:, at:at + n * KEYS].rearrange("p (h k) -> p h k", h=n),
                             query(b, h, slice(qt * P, (qt + 1) * P)), keys(b, h, n, KEYS), start=True, stop=True)
                    h, at = h + n, at + n * KEYS
                ins.then_inc(s["score_pe"], 1)

            def turn_max(b):
                pe.wait_ge(s["nm_ok"], L * B + b + 1)
                for qt in range(QT):
                    ins = nc.tensor.transpose(bank[7][0:32, qt * P:(qt + 1) * P],
                                              nm[:, b, qt].rearrange("p a h -> p (a h)"), ident[:])
                ins.then_inc(s["nmT_pe"], 1)

            def prob_unit(b, hg, i):
                u = (b * NQUAD + hg) * 5 + i
                if u >= 3:
                    pe.wait_ge(s["prob_ok"], first * 5 + u - 2)
                dst = bank[1 + u % 3][:]
                if i == 0:
                    rem_scores(dst, b, hg)
                    lhs = ind_rem[:, 4 * hg:4 * hg + 4, :].rearrange("p h k -> p (h k)")
                else:
                    h = 4 * hg + i - 1
                    mm(dst, keys(b, h, 1, P)[:, 0, :], query(b, h, slice(0, S)), start=True, stop=False)
                    lhs = ind[:, h, :]
                mm(dst, lhs, nmT[:, b, :], start=False, stop=True).then_inc(s["prob_pe"], 1)

            def sum_unit(group, i):
                b, hg = divmod(group, NQUAD)
                pe.wait_ge(s["prob_ok"], 5 * (first + group) + i + 1)
                if i == 0 and group >= 2:
                    pe.wait_ge(s["o_ok"], first + group - 1)
                lhs = rem_values(b, hg) if i == 0 else values(b, hg, i - 1)
                ins = mm(bank[(0, 4)[group % 2]][0:lhs.shape[-1], :], lhs, prob[:, group % 2, i, :], start=(i == 0), stop=(i == 4))
                if i == 4:
                    ins.then_inc(s["pv_pe"], 1)

            def project(b):
                pe.wait_ge(s["o_ok"], first + (b + 1) * NQUAD)
                n = 2 if L == 0 else 1
                for qt in range(QT):
                    dst = bank[5 + b][:, qt * P:(qt + 1) * P]
                    for i in range(n):
                        ins = mm(dst, oT[:, i, b, qt * P:(qt + 1) * P], small_wT[:, (0 if L == 0 else 3) + i, :],
                                 start=(i == 0), stop=(L == 1))
                    if L == 0:
                        ins = mm(dst, ones[0:1, 0:P], fc_b[0:1, :], start=False, stop=True)
                ins.then_inc(s["fc_pe"], 1)

            for qt in range(QT):
                for g in range(6):
                    score_part(0, qt, g)
                    beside(qt * 6 + g)
            turn_max(0)
            pe.wait_ge(s["nmT_ok"], L * B + 1)
            for group in range(B * NQUAD):
                b, hg = divmod(group, NQUAD)
                if group == NQUAD:
                    for i in range(5):
                        sum_unit(group - 1, i)
                        if i == 2:
                            turn_max(1)
                    pe.wait_ge(s["nmT_ok"], L * B + 2)
                if group == NQUAD + 1:
                    project(0)
                for i in range(5):
                    prob_unit(b, hg, i)
                    if group and group != NQUAD:
                        sum_unit(group - 1, i)
                    if b == 0:
                        score_part(1, hg, i)
                        if i == 4:
                            score_part(1, hg, 5)
            for i in range(5):
                sum_unit(B * NQUAD - 1, i)
            project(1)


        def experts_sync(sp, L):
            if L == 0:
                sp.wait_ge(s["x1_ok"], 2)
                sp.dma_start(w1_0[:].rearrange("p (e f) -> p e f", f=HID), A["L0_ffn_W1"].rearrange("e d f -> d e f")).then_inc(r[0]["ld_w"], 16)
                sp.dma_start(w2_0[:].rearrange("p (e c d) -> p e c d", c=4, d=D),
                             A["L0_ffn_W2"].rearrange("e (c p) d -> p e c d", p=P)).then_inc(r[0]["ld_w"], 16)
                sp.dma_start(b1_cols[:, 0:32], A["L0_ffn_b1"].rearrange("e f -> (e f)").rearrange("(p c) -> p c", c=32)).then_inc(s["ld_b1"], 16)
                sp.dma_start(b1_cols[:, 32:40], A["L0_ffn_b2"].rearrange("e f -> (e f)").rearrange("(p c) -> p c", c=8)).then_inc(s["ld_b1"], 16)
                sp.wait_ge(s["b1_ok"], 1)
                n = EXPERTS[0] * HID
                for row, part in enumerate((b1_hi, b1_lo)):
                    sp.dma_start(b1_rows[row:row + 1, 0:n].bitcast(F32), part[:, 0:32].bitcast(F32)).then_inc(s["ld_b1_rows"], 16)
                    sp.dma_start(b1_rows[row:row + 1, n:].bitcast(F32), part[:, 32:40].bitcast(F32)).then_inc(s["ld_b1_rows"], 16)
            sp.wait_ge(s["xn_ok"], 2 * L + 2)
            sp.dma_start(normed[L].rearrange("(t p) d -> p t d", p=P), xn[:]).then_inc(r[L]["saved"], 16)

        def mix_sync(sp, L):
            for i, name in enumerate(SCATTERED):
                sp.wait_ge(r[L][name], 16 * ((TILES[L] - 1 - i) // 4 + 1))
            for k in range(2):
                sp.dma_start(parts[:, k * T:(k + 1) * T, :],
                             results[L][k * B * S:(k + 1) * B * S, :].rearrange("(t p) d -> p t d", p=P)).then_inc(r[L][f"mixed"], 16)

        def experts_pool(pool, L):
            q, n = r[L], TILES[L]

            def gather(t):
                nc.gpsimd.indirect_dma_start(
                    out=gx[:, t, :], out_offset=None, in_=normed[L],
                    in_offset=bass.IndirectOffsetOnAxis(ap=slot_from[:, t:t + 1].bitcast(U32), axis=0)).then_inc(q[GATHERED[t % 14]], 16)

            pool.wait_ge(q["saved"], 16)
            pool.wait_ge(q["slots_ok"], 1)
            for t in range(12):
                gather(t)
            for t in range(n):
                pool.wait_ge(q["y_copied" if L == 0 else "y_ok"], t + 1)
                nc.gpsimd.indirect_dma_start(
                    out=results[L], out_offset=bass.IndirectOffsetOnAxis(ap=slot_to[:, t:t + 1].bitcast(U32), axis=0),
                    in_=ys[:, t % 4, :], in_offset=None).then_inc(q[SCATTERED[t % 4]], 16)
                if t + 12 < n:
                    gather(t + 12)

        def route_dve(dve, step, L):
            E, q = EXPERTS[L], r[L]
            dve.wait_ge(q["logits_pe"], 1)
            step(nc.vector.tensor_copy(logits[:, :, 0:E], bank[5][:, 0:T * E].rearrange("p (t e) -> p t e", e=E)))
            for t in range(T):
                ins = nc.vector.max(top8[:, t, :], logits[:, t, 0:E])
            step(ins)
            for t in range(T):
                ins = nc.vector.max_index(top8_at[:, t, :], top8[:, t, :], logits[:, t, 0:E])
            step(ins)
            nc.vector.tensor_tensor(gate[:, 0, :], top8[:, :, 1], top8[:, :, 0], ALU.subtract).then_inc(q["diff_ok"], 1)
            step(nc.vector.tensor_copy(top2_at[:], top8_at[:, :, 0:2].rearrange("p t k -> p k t")))
            for k in range(2):
                ins = nc.vector.tensor_tensor(onehot[:, k, :, 0:E], iota_e[:, 0:E].unsqueeze(1).to_broadcast([P, T, E]),
                                              top2_at[:, k, :].unsqueeze(2).to_broadcast([P, T, E]), ALU.is_equal)
            step(ins)
            nc.vector.tensor_tensor(chosen[:, :, 0:E], onehot[:, 0, :, 0:E], onehot[:, 1, :, 0:E], ALU.add).then_inc(q["chosen_ok"], 1)
            dve.wait_ge(q["exp_ok"], 1)
            step(nc.vector.tensor_scalar(gate[:, 1, :], gate[:, 0, :], 1.0, None, ALU.add))
            step(nc.vector.reciprocal(gate[:, 2, :], gate[:, 1, :]))
            step(nc.vector.tensor_tensor(gate[:, 3, :], gate[:, 0, :], gate[:, 2, :], ALU.mult))
            dve.wait_ge(q["rank_pe"], 1)
            step(nc.vector.tensor_scalar(counts_i[:, 0, 0:E], bank[7][:, 0:E], float(P - 1), None, ALU.add))
            step(nc.vector.tensor_scalar(counts_i[:, 1, 0:E], counts_i[:, 0, 0:E], 7, None, ALU.arith_shift_right))
            nc.vector.memset(scan[0][:, 0:16], 0.0)
            nc.vector.memset(scan[1][:, 0:16], 0.0)
            nc.vector.tensor_copy(tiles_f[:, 0:E], counts_i[:, 1, 0:E])
            step(nc.vector.tensor_copy(scan[0][:, 16:16 + E], counts_i[:, 1, 0:E]))
            a = 0
            shift = 1
            while shift < E:
                step(nc.vector.tensor_tensor(scan[1 - a][:, 16:16 + E], scan[a][:, 16:16 + E],
                                             scan[a][:, 16 - shift:16 - shift + E], ALU.add))
                a, shift = 1 - a, shift * 2
            upto = scan[a][:, 16:16 + E]
            step(nc.vector.tensor_tensor(counts_f[:, 0:E], upto, tiles_f[:, 0:E], ALU.subtract))
            step(nc.vector.tensor_scalar(counts_f[:, 0:E], counts_f[:, 0:E], float(P), None, ALU.mult))
            step(nc.vector.tensor_tensor(rank[:, :, 0:E], bank[6][:, 0:T * E].rearrange("p (t e) -> p t e", e=E),
                                         counts_f[:, 0:E].unsqueeze(1).to_broadcast([P, T, E]), ALU.add))
            for k in range(2):
                ins = nc.vector.tensor_tensor(ranked[:, k, :, 0:E], onehot[:, k, :, 0:E], rank[:, :, 0:E], ALU.mult)
            step(ins)
            step(nc.vector.tensor_reduce(slot_f[:].rearrange("p k t -> p (k t)"), ranked[:, :, :, 0:E].rearrange("p k t e -> p (k t) e"), AX.X, ALU.add))
            NT = TILES[L]
            step(nc.vector.tensor_copy(slot_i[:, 0], slot_f[:]))
            nc.vector.tensor_scalar(slot_i[:, 1], slot_i[:, 0], P - 1, None, ALU.bitwise_and)
            step(nc.vector.tensor_scalar(slot_i[:, 2], slot_i[:, 0], 7, None, ALU.arith_shift_right))
            step(nc.vector.tensor_copy(slot_rt[:], slot_i[:, 1:3]))
            step(nc.vector.tensor_tensor(slot_hit[:, :, 0:NT], iota_s[:, 0:NT].unsqueeze(1).to_broadcast([P, 2 * T, NT]),
                                         slot_rt[:, 1].rearrange("p k t -> p (k t)").unsqueeze(2).to_broadcast([P, 2 * T, NT]), ALU.is_equal))
            for i, factor in enumerate((place_1, gate[:, 2:4])):
                nc.vector.tensor_tensor(slot_tile[:, :, i, 0:NT], slot_hit[:, :, 0:NT],
                                        factor[:].rearrange("p k t -> p (k t)").unsqueeze(2).to_broadcast([P, 2 * T, NT]), ALU.mult)
            for i in range(2 * T):
                nc.vector.tensor_scalar(slot_row[:, i, :], iota_r[:], slot_rt[:, 0].rearrange("p k t -> p (k t)")[:, i:i + 1],
                                        None, ALU.is_equal).then_inc(q["slot_hit_ok"], 1)
            dve.wait_ge(q["slot_pe"], 1)
            found = bank[5][:, 0:NT]
            nc.vector.tensor_copy(slot_gate[:, 0:NT], bank[5][:, NT:2 * NT])
            step(nc.vector.scalar_tensor_tensor(out=slot_none[:, 0:NT], in0=found, scalar=0.5, in1=spare_row[:, 0:NT],
                                                op0=ALU.is_lt, op1=ALU.mult))
            step(nc.vector.scalar_tensor_tensor(out=slot_to[:, 0:NT], in0=found, scalar=-1.0, in1=slot_none[:, 0:NT],
                                                op0=ALU.add, op1=ALU.add))
            nc.vector.tensor_scalar(slot_from[:, 0:NT], slot_to[:, 0:NT], B * S - 1, None, ALU.bitwise_and).then_inc(q["slots_ok"], 1)
            NT = TILES[L]
            step(nc.vector.tensor_tensor(before[:, 0:NT, 0:E], upto.unsqueeze(1).to_broadcast([P, NT, E]),
                                         iota_s[:, 0:NT].unsqueeze(2).to_broadcast([P, NT, E]), ALU.is_le))
            step(nc.vector.tensor_reduce(expert_f[:, 0:NT], before[:, 0:NT, 0:E], AX.X, ALU.add))
            nc.vector.tensor_scalar(expert_i[:, 0:NT], expert_f[:, 0:NT], float(E - 1), None, ALU.min).then_inc(q["experts_ok"], 1)
            if L == 0:
                dve.wait_ge(s["ld_b1"], 32)
                step(nc.vector.tensor_copy(b1_hi[:], b1_cols[:]))
                nc.vector.tensor_tensor(b1_lo[:], b1_cols[:], b1_hi[:].bitcast(F32), ALU.subtract).then_inc(s["b1_ok"], 1)

        def experts_dve(dve, step, L):
            q = r[L]
            n = TILES[L]
            if L == 1:
                for t in range(n + 2 + 4):
                    if t < n:
                        dve.wait_ge(q["act_ok"], t + 1)
                        if t >= 2:
                            dve.wait_ge(q["hidT_pe"], t - 1)
                        nc.vector.tensor_tensor(hid[:, t % 2, :], act_h[:, t % 2, :], bank[2 + 2 * (t % 2)][:], ALU.mult).then_inc(q["hid_ok"], 1)
                    u = t - 2
                    if 0 <= u < n:
                        dve.wait_ge(q["y_copied"], u + 1)
                        nc.vector.bn_stats(y_stats[:, u % 4, :], y[:, u % 8, :]).then_inc(q["y_stats_ok"], 1)
                    if 0 <= u - 4 < n:
                        expert_scale(dve, step, q, u - 4)
                    if 0 <= u < n and (u % 4 == 3 or u == n - 1):
                        expert_norm(dve, step, q, u // 4 * 4, u + 1)
            for k in range(2):
                dve.wait_ge(q["mixed"], 32)
                for b in range(B):
                    ts = slice(b * QT, (b + 1) * QT)
                    ins = nc.vector.tensor_tensor(x[:, ts, :], x[:, ts, :], parts[:, k * T + b * QT:k * T + (b + 1) * QT, :], ALU.add)
                    if k == 1:
                        ins.then_inc(q["summed"], 1)
                if k == 0:
                    step(ins)
            dve.wait_ge(q["summed"], B)

        def expert_norm(dve, step, q, first, end):
            m = end - first
            dve.wait_ge(q["y_stats_ok"], end)
            for u in range(first, end):
                ins = nc.vector.bn_aggr(y_mv[:, u - first, :], y_stats[:, u - first, :])
            step(ins)
            inverse_root(step, y_mv[:, 0:m, 1], y_root[:, 0, 0:m], y_root[:, 1, 0:m], y_root[:, 2, 0:m], y_root[:, 3, 0:m])
            step(nc.vector.tensor_tensor(y_root[:, 4, 0:m], y_root[:, 3, 0:m], slot_gate[:, first:end], ALU.mult))

        def expert_scale(dve, step, q, u):
            i = u % 4
            e = dve.value_load(expert_i[0:1, u:u + 1], min_val=0, max_val=EXPERTS[1] - 1)
            if u >= 4:
                dve.wait_ge(q[SCATTERED[i]], 16 * (u // 4))
            step(nc.vector.tensor_scalar(ys[:, i, :], y[:, u % 8, :], y_mv[:, i, 0:1], y_root[:, 4, i:i + 1], ALU.subtract, ALU.mult))
            step(nc.vector.tensor_tensor(ys[:, i, :], ys[:, i, :], gamma[:].rearrange("p e d -> p (e d)")[:, bass.ds(e * D, D)], ALU.mult))
            nc.vector.scalar_tensor_tensor(out=ys[:, i, :], in0=beta[:].rearrange("p e d -> p (e d)")[:, bass.ds(e * D, D)],
                                           scalar=slot_gate[:, u:u + 1], in1=ys[:, i, :], op0=ALU.mult, op1=ALU.add).then_inc(q["y_ok"], 1)

        def experts_act(act, L):
            q = r[L]
            act.wait_ge(q["diff_ok"], 1)
            nc.scalar.activation(gate[:, 0, :], gate[:, 0, :], ACT.Exp).then_inc(q["exp_ok"], 1)
            def rows(t):
                act.wait_ge(q["gxT_pe"], t + 1)
                if t >= 2:
                    act.wait_ge(q["up_pe"], t - 1)
                nc.scalar.copy(gxT[:, t % 2, :], bank[0][:, 0:P]).then_inc(q["gxT_ok"], 1)

            def hidden(t):
                act.wait_ge(q["up_pe"], t + 1)
                if L == 0:
                    if t >= 2:
                        act.wait_ge(q["hidT_pe"], t - 1)
                    nc.scalar.activation(hid[:, t % 2, :], bank[1 + 2 * (t % 2)][:], ACT.Relu).then_inc(q["hid_ok"], 1)
                else:
                    if t >= 2:
                        act.wait_ge(q["hid_ok"], t - 1)
                    nc.scalar.activation(act_h[:, t % 2, :], bank[1 + 2 * (t % 2)][:], ACT.Silu).then_inc(q["act_ok"], 1)

            n = TILES[L]
            for t in range(3):
                rows(t)
                if t >= 1:
                    hidden(t - 1)
            for t in range(n):
                act.wait_ge(q["hidT_pe"], t + 1)
                if t >= 2:
                    act.wait_ge(q["y_pe"], t - 1)
                nc.scalar.copy(hidT[:, t % 2, :], bank[5][:]).then_inc(q["hidT_ok"], 1)
                if t + 3 < n:
                    rows(t + 3)
                if t + 2 < n:
                    hidden(t + 2)
                act.wait_ge(q["y_pe"], t + 1)
                if L == 0:
                    if t >= 4:
                        act.wait_ge(q[SCATTERED[t % 4]], 16 * (t // 4))
                    nc.scalar.activation(ys[:, t % 4, :], bank[6 + t % 2][:, 0:D], ACT.Copy, scale=slot_gate[:, t:t + 1]).then_inc(q["y_copied"], 1)
                else:
                    if t >= 8:
                        act.wait_ge(q["y_ok"], t - 7)
                    nc.scalar.copy(y[:, t % 8, :], bank[6 + t % 2][:, 0:D]).then_inc(q["y_copied"], 1)

        def experts_pe(pe, L):
            E, q = EXPERTS[L], r[L]
            pe.wait_ge(s["xnT_ok"], 2 * (2 * L + 2))
            for t in range(T):
                b, qt = divmod(t, QT)
                dst = bank[5][:, t * E:(t + 1) * E]
                mm(dst, xnT[:, b, qt * P:(qt + 1) * P], wr[L][:], start=True, stop=False)
                ins = mm(dst, ones[0:1, 0:P], br[L][0:1, :], start=False, stop=True)
            ins.then_inc(q["logits_pe"], 1)
            pe.wait_ge(q["chosen_ok"], 1)
            for back in range(T):
                ins = mm(bank[6][:, back * E:T * E], tri[:] if back == 0 else ones_b[:], chosen[:, 0:T - back, 0:E],
                         start=(back == 0), stop=(back == T - 1), skip_group_check=True)
            for t in range(T):
                ins = mm(bank[7][:, 0:E], ones_b[:], chosen[:, t, 0:E], start=(t == 0), stop=(t == T - 1))
            ins.then_inc(q["rank_pe"], 1)
            for i in range(2 * T):
                pe.wait_ge(q["slot_hit_ok"], i + 1)
                ins = mm(bank[5][:, 0:2 * TILES[L]].rearrange("p (a n) -> p a n", a=2), slot_row[:, i, :], slot_tile[:, i, :, 0:TILES[L]],
                         start=(i == 0), stop=(i == 2 * T - 1))
            ins.then_inc(q["slot_pe"], 1)
            w1, w2 = (w1_0, w2_0) if L == 0 else (w1_1, w2_1)

            def expert_of(t):
                return pe.value_load(expert_i[0:1, t:t + 1], min_val=0, max_val=E - 1)

            def turn_rows(t):
                if t:
                    pe.wait_ge(q["gxT_ok"], t)
                pe.wait_ge(q[GATHERED[t % 14]], 16 * (t // 14 + 1))
                nc.tensor.transpose(bank[0][:, 0:P], gx[:, t, :], ident[:]).then_inc(q["gxT_pe"], 1)

            def up(t, e):
                pe.wait_ge(q["gxT_ok"], t + 1)
                if t >= 2:
                    pe.wait_ge(q["hid_ok"], t - 1)
                cols = bass.ds(e * HID, HID)
                first, second = bank[1 + 2 * (t % 2)], bank[2 + 2 * (t % 2)]
                if L == 0:
                    mm(first[:], gxT[:, t % 2, :], w1[:, cols], start=True, stop=False)
                    mm(first[:], ones_r[0:2, 0:P], b1_rows[0:2, cols], start=False, stop=True).then_inc(q["up_pe"], 1)
                else:
                    mm(first[:], gxT[:, t % 2, :], w1[:, cols], start=True, stop=True)
                    mm(second[:], gxT[:, t % 2, :], w3_1[:, cols], start=True, stop=True).then_inc(q["up_pe"], 1)

            def turn_hidden(t):
                pe.wait_ge(q["hid_ok"], t + 1)
                if t:
                    pe.wait_ge(q["hidT_ok"], t)
                for c in range(4):
                    ins = nc.tensor.transpose(bank[5][:, c * P:(c + 1) * P], hid[:, t % 2, c * P:(c + 1) * P], ident[:])
                ins.then_inc(q["hidT_pe"], 1)

            def down(t, e):
                pe.wait_ge(q["hidT_ok"], t + 1)
                result = bank[6 + t % 2][:, 0:D]
                if t >= 2:
                    pe.wait_ge(q["y_copied"], t - 1)
                for c in range(4):
                    ins = mm(result, hidT[:, t % 2, c * P:(c + 1) * P], w2[:, bass.ds(e * HID + c * P, P)],
                             start=(c == 0), stop=(L == 1 and c == 3))
                if L == 0:
                    ins = mm(result, ones_r[0:2, 0:P], b1_rows[0:2, bass.ds(e * D + E * HID, D)], start=False, stop=True)
                ins.then_inc(q["y_pe"], 1)

            pe.wait_ge(q["experts_ok"], 1)
            if L == 0:
                pe.wait_ge(s["ld_b1_rows"], 64)
            pe.wait_ge(q["ld_w"], 16 * (2 + L))
            n = TILES[L]
            e = {}
            for t in range(3):
                turn_rows(t)
                if t >= 1:
                    e[t - 1] = expert_of(t - 1)
                    up(t - 1, e[t - 1])
            for t in range(n):
                turn_hidden(t)
                if t + 2 < n:
                    e[t + 2] = expert_of(t + 2)
                if t + 3 < n:
                    turn_rows(t + 3)
                if t + 2 < n:
                    up(t + 2, e[t + 2])
                down(t, e[t])


        def hard_attention_dve(dve, step):
            nc.vector.memset(nmT[:].bitcast(F32), 0.0)
            for n in ("q_hi", "q_lo"):
                nc.vector.memset(sel1[n][:].bitcast(F32), 0.0)
            for n in ("k_hi", "k_lo", "mask"):
                nc.vector.memset(sel1k[n][:].bitcast(F32), 0.0)
            nc.vector.memset(kst1[:].bitcast(F32), 0.0)
            nc.vector.memset(krem1[:].bitcast(F32), 0.0)
            nc.vector.memset(v1[:], 0.0)
            step(nc.vector.memset(vrem1[:], 0.0))
            id_q = ident[:].rearrange("p (h f) -> p h f", f=DH)
            id_k = ident[0:DH, 0:DH].unsqueeze(1).to_broadcast([DH, 4, DH])
            nc.vector.memset(sel1k["mask"][0:1, :, 3, 0:1].bitcast(F32), 1.0)
            for tile, quarter, src in ((sel1["q_hi"], 0, id_q), (sel1["q_hi"], 1, id_q), (sel1["q_lo"], 2, id_q),
                                       (sel1k["k_hi"][0:DH], 0, id_k), (sel1k["k_hi"][0:DH], 2, id_k), (sel1k["k_lo"][0:DH], 1, id_k)):
                ins = nc.vector.tensor_copy(tile[:, :, quarter, :], src)
            ins.then_inc(s["sel1_ok"], 1)
            for b in range(B):
                dve.wait_ge(s["qp_ok"], b + 1)
                step(nc.vector.tensor_copy(qp_hi[:, b, :], qp[:, b, :]))
                nc.vector.tensor_tensor(qp_lo[:, b, :], qp[:, b, :], qp_hi[:, b, :].bitcast(F32), ALU.subtract).then_inc(s["qp_split"], 1)
            for b in range(B):
                for qt in range(QT):
                    u = b * QT + qt
                    score = bank[u % 3][:, 0:KEYS]
                    dve.wait_ge(s["hit_pe"], u + 1)
                    step(nc.vector.max(hit8[:, u, :], score))
                    step(nc.vector.max_index(hit8_at[:, u, :], hit8[:, u, :], score))
                    step(nc.vector.tensor_copy(hit_f[:, u:u + 1], hit8_at[:, u, 0:1]))
                    if u >= QT:
                        dve.wait_ge(s["count_pe"], 1)
                    nc.vector.tensor_scalar(hits[:, qt, :], iota_k[:], hit_f[:, u:u + 1], None, ALU.is_equal).then_inc(s["hit_ok"], 1)
            dve.wait_ge(s["count_pe"], 2)
            step(nc.vector.tensor_copy(counts[:], bank[7][:, 0:2 * B]))
            step(nc.vector.tensor_scalar(mask_row[0:1, :], bank[7][0:1, 128:128 + B * KP], 0.5, MASKED, ALU.is_lt, ALU.mult))
            dve.wait_ge(s["mk_pe"], 1)
            for b in range(B):
                diagonal = v1[:, b].rearrange("p (j x) -> p j x", x=9 * DH)
                nc.vector.tensor_scalar(diagonal[:, :, 0:DH],
                                        bank[3][:, (2 * b) * 16 + DH:(2 * b) * 16 + 2 * DH].unsqueeze(1).to_broadcast([P, 4, DH]),
                                        counts[:, 2 * b:2 * b + 1], None, ALU.mult)
                nc.vector.tensor_copy(diagonal[:, :, 4 * DH:5 * DH], counts[:, 2 * b:2 * b + 1].unsqueeze(2).to_broadcast([P, 4, DH]))
                for j in range(4):
                    rows = slice(32 * j, 32 * j + 32)
                    nc.vector.tensor_scalar(vrem1[rows, b, j * DH:(j + 1) * DH], bank[3][rows, (2 * b + 1) * 16 + DH:(2 * b + 1) * 16 + 2 * DH],
                                            counts[rows, 2 * b + 1:2 * b + 2], None, ALU.mult)
                    nc.vector.tensor_copy(vrem1[rows, b, (4 + j) * DH:(5 + j) * DH], counts[rows, 2 * b + 1:2 * b + 2].to_broadcast([32, DH]))
            step(nc.vector.tensor_copy(mk_hi[0:DH, :], bank[4][0:DH, 0:B * KP]))
            nc.vector.tensor_tensor(mk_lo[0:DH, :], bank[4][0:DH, 0:B * KP], mk_hi[0:DH, :].bitcast(F32), ALU.subtract).then_inc(s["mk_ok"], 1)
            dve.wait_ge(s["kst1_pe"], 1)
            src = bank[0][:, 0:B * KP].rearrange("p (b k) -> p b k", b=B)
            for a in range(4):
                rows = slice(32 * a, 32 * a + 32)
                nc.vector.tensor_copy(kst1[rows, a], src[rows])
                ins = nc.vector.tensor_copy(krem1[rows, :, a, :], src[rows, :, P:KP])
            ins.then_inc(s["kst1_ok"], 1)
            for u in range(B * NQUAD):
                b, g = divmod(u, NQUAD)
                dve.wait_ge(s["qst1_pe"], u + 1)
                nc.vector.tensor_copy(qst[:, g, b, :], bank[1 + u % 4][:]).then_inc(s["qst1_ok"], 1)

        def hard_attention_pe(pe):
            for b in range(B):
                pe.wait_ge(s["xnT_ok"], 4 + b + 1)
                mm(bank[5 + b][:], small_wT[:, 2, :], xnT[:, b, :], start=True, stop=True).then_inc(s["qp_pe"], 1)
            for b in range(B):
                for half, lhs in enumerate((ctxT[:, b, 0:P], ctxT_rep[:, b].rearrange("p j k -> p (j k)"))):
                    i = 2 * b + half
                    if i == 0:
                        pe.wait_ge(s["xnT_ok"], 6)
                    mm(bank[3][:, i * 16:(i + 1) * 16], lhs, wkvT[:], start=True, stop=True)
            mm(bank[4][0:DH, 0:B * KP], wkvT[:, 0:DH], ctxT[:].rearrange("p b k -> p (b k)"), start=True, stop=True).then_inc(s["mk_pe"], 1)
            for b in range(B):
                pe.wait_ge(s["qp_ok"], b + 1)
                for qt in range(QT):
                    u = b * QT + qt
                    if u >= 3:
                        pe.wait_ge(s["hit_ok"], u - 2)
                    mm(bank[u % 3][:, 0:KEYS], qp[:, b, qt * P:(qt + 1) * P], ctxT[:, b, 0:KEYS], start=True, stop=True).then_inc(s["hit_pe"], 1)
                pe.wait_ge(s["hit_ok"], (b + 1) * QT)
                for half in range(2):
                    for qt in range(QT):
                        mm(bank[7][:, 2 * b + half:2 * b + half + 1], hits[:, qt, half * P:(half + 1) * P], ones_b[:, 0:1],
                           start=(qt == 0), stop=(qt == QT - 1))
                for qt in range(QT):
                    ins = mm(bank[7][0:1, 128 + b * KP:128 + (b + 1) * KP], ones_b[:, 0:1], hits[:, qt, 0:KP],
                             start=(qt == 0), stop=(qt == QT - 1))
                ins.then_inc(s["count_pe"], 1)
            pe.wait_ge(s["mk_ok"], 1)
            pe.wait_ge(s["sel1_ok"], 1)
            dst = bank[0][:, 0:B * KP]
            mm(dst, sel1k["k_hi"][0:DH].rearrange("p a c f -> p (a c f)"), mk_hi[0:DH, :], start=True, stop=False)
            mm(dst, sel1k["k_lo"][0:DH].rearrange("p a c f -> p (a c f)"), mk_lo[0:DH, :], start=False, stop=False)
            mm(dst, sel1k["mask"][0:1].rearrange("p a c f -> p (a c f)"), mask_row[0:1, :], start=False, stop=True).then_inc(s["kst1_pe"], 1)
            for u in range(B * NQUAD):
                b, g = divmod(u, NQUAD)
                pe.wait_ge(s["qp_split"], b + 1)
                if u >= 4:
                    pe.wait_ge(s["qst1_ok"], u - 3)
                dst = bank[1 + u % 4][:]
                for i, n in enumerate(("q_hi", "q_lo")):
                    mm(dst, sel1[n][:, 4 * g:4 * g + 4].rearrange("p a c f -> p (a c f)"), (qp_hi, qp_lo)[i][:, b, :], start=(i == 0), stop=False)
                mm(dst, sel1k["mask"][0:1].rearrange("p a c f -> p (a c f)"), ones_r[0:1, :], start=False, stop=True).then_inc(s["qst1_pe"], 1)
            pe.wait_ge(s["kst1_ok"], 1)
            pe.wait_ge(s["qst1_ok"], B * NQUAD)

        @block.sync
        def _(sp):
            sp.dma_start(ctx_main[:], A["ctx_1024"][:, 0:P, :].rearrange("b k d -> k b d")).then_inc(s["ld_ctx"], 16)
            sp.dma_start(ctx_rem[0:KR], A["ctx_1024"][:, P:KEYS, :].rearrange("b k d -> k b d")).then_inc(s["ld_ctx"], 16)
            sp.dma_start(fm_w[0:DH, :], A["L0_xattn_fm_w"]).then_inc(s["ld_small"], 16)
            sp.dma_start(fm_b[0:DH, :], A["L0_xattn_fm_b"].rearrange("(e a) -> e a", a=1)).then_inc(s["ld_small"], 16)
            sp.dma_start(x[:], A["x"].rearrange("b (t p) d -> p (b t) d", p=P)).then_inc(s["ld_x"], 16)
            sp.dma_start(small_w[:, 0:2, :], A["L0_xattn_fc_w"].rearrange("e (a f) -> e a f", a=2)).then_inc(s["ld_small"], 16)
            sp.dma_start(small_w[:, 2, :], A["L1_xattn_Wq"]).then_inc(s["ld_small"], 16)
            sp.dma_start(small_w[:, 3, :], A["L1_xattn_Wc"]).then_inc(s["ld_small"], 16)
            sp.dma_start(wkv[0:2 * DH, :], A["L1_xattn_Wkv"]).then_inc(s["ld_small"], 16)
            sp.dma_start(fc_b[0:1, :], A["L0_xattn_fc_b"].rearrange("(a e) -> a e", a=1)).then_inc(s["ld_small"], 16)
            for L in range(2):
                sp.dma_start(wr[L][:], A[f"L{L}_ffn_Wr"]).then_inc(s["ld_small"], 16)
                sp.dma_start(br[L][0:1, :], A[f"L{L}_ffn_br"].rearrange("(a e) -> a e", a=1)).then_inc(s["ld_small"], 16)
            experts_sync(sp, 0)
            mix_sync(sp, 0)
            for name, tile in (("W1", w1_1), ("W3", w3_1)):
                sp.dma_start(tile[:].rearrange("p (e f) -> p e f", f=HID), A[f"L1_ffn_{name}"].rearrange("e d f -> d e f")).then_inc(r[1]["ld_w"], 16)
            sp.wait_ge(s["x1_ok"], 4)
            sp.dma_start(w2_1[:].rearrange("p (e c d) -> p e c d", c=4, d=D),
                         A["L1_ffn_W2"].rearrange("e (c p) d -> p e c d", p=P)).then_inc(r[1]["ld_w"], 16)
            sp.dma_start(gamma[:].rearrange("p e d -> p (e d)"), A["L1_ffn_gamma"].rearrange("e d -> (e d)").partition_broadcast(P)).then_inc(s["ld_gb"], 16)
            sp.dma_start(beta[:].rearrange("p e d -> p (e d)"), A["L1_ffn_beta"].rearrange("e d -> (e d)").partition_broadcast(P)).then_inc(s["ld_gb"], 16)
            experts_sync(sp, 1)
            mix_sync(sp, 1)
            for b in range(B):
                sp.wait_ge(r[1]["summed"], b + 1)
                sp.dma_start(out[b].rearrange("(t p) d -> p t d", p=P), x[:, b * QT:(b + 1) * QT, :]).then_inc(s["stored"], 16)
            sp.wait_ge(s["stored"], 32)

        @block.gpsimd
        def _(pool):
            step = Steps(pool, s["pool_step"])
            step(nc.gpsimd.memset(ident[:], 0.0))
            step(nc.gpsimd.affine_select(out=ident[:], in_=ident[:], pattern=[[-1, P]], compare_op=ALU.not_equal,
                                         fill=1.0, base=0, channel_multiplier=1))
            nc.gpsimd.memset(ones[:], 1.0).then_inc(s["pool_consts"], 1)
            step(nc.gpsimd.memset(bmask[:], 1.0))
            step(nc.gpsimd.affine_select(out=bmask[:], in_=bmask[:], pattern=[[-DH, H]], compare_op=ALU.is_ge,
                                         fill=0.0, base=0, channel_multiplier=1))
            nc.gpsimd.affine_select(out=bmask[:], in_=bmask[:], pattern=[[DH, H]], compare_op=ALU.is_ge,
                                    fill=0.0, base=DH - 1, channel_multiplier=-1).then_inc(s["pool_consts"], 1)
            pool.wait_ge(s["pool_consts"], 2)
            for a in range(2):
                step(nc.gpsimd.memset(kst0[64 * (1 - a):64 * (1 - a) + 64].rearrange("p (n a) b k -> p n a (b k)", a=2)[:, :, a].bitcast(F32), 0.0))
            nc.gpsimd.memset(ind[:].bitcast(F32), 0.0)
            nc.gpsimd.memset(ind_rem[:].bitcast(F32), 0.0)
            nc.gpsimd.memset(nmT[:].bitcast(F32), 0.0)
            nc.gpsimd.memset(krem0[:].bitcast(F32), 0.0).then_inc(s["pool_consts"], 1)
            nc.gpsimd.memset(v0[:], 0.0)
            step(nc.gpsimd.memset(vrem0[:], 0.0))
            for j in range(4):
                step(nc.gpsimd.memset(vrem0[32 * j:32 * j + KR, :, :, (4 + j) * F0:(5 + j) * F0], 1.0))
            nc.gpsimd.memset(ones_r[:].bitcast(F32), 1.0).then_inc(s["pool_consts"], 1)
            nc.gpsimd.iota(iota_e[:], pattern=[[1, 16]], base=0, channel_multiplier=0, allow_small_or_imprecise_dtypes=True)
            nc.gpsimd.iota(iota_s[:], pattern=[[1, 32]], base=0, channel_multiplier=0, allow_small_or_imprecise_dtypes=True)
            nc.gpsimd.iota(iota_k[:, 0:P], pattern=[[1, P]], base=0, channel_multiplier=0, allow_small_or_imprecise_dtypes=True)
            nc.gpsimd.iota(iota_k[:, P:], pattern=[[0, 4], [1, 32]], base=P, channel_multiplier=0, allow_small_or_imprecise_dtypes=True)
            step(nc.gpsimd.memset(ones_b[:], 1.0))
            nc.gpsimd.affine_select(out=tri[:], in_=ones_b[:], pattern=[[1, P]], compare_op=ALU.is_gt,
                                    fill=0.0, base=0, channel_multiplier=-1).then_inc(s["pool_consts"], 1)
            nc.gpsimd.iota(place_1[:], pattern=[[B * S, 2], [P, T]], base=1, channel_multiplier=1, allow_small_or_imprecise_dtypes=True)
            nc.gpsimd.iota(iota_r[:], pattern=[[1, P]], base=0, channel_multiplier=0, allow_small_or_imprecise_dtypes=True)
            nc.gpsimd.iota(spare_row[:], pattern=[[P, 32]], base=2 * B * S + 1, channel_multiplier=1,
                           allow_small_or_imprecise_dtypes=True).then_inc(s["pool_consts"], 1)
            experts_pool(pool, 0)
            experts_pool(pool, 1)

        @block.vector
        def _(dve):
            step = Steps(dve, s["dve_step"])
            step(nc.vector.memset(ctxT[:], 0.0))
            nc.vector.memset(sel0["q_hi"][:].bitcast(F32), 0.0)
            nc.vector.memset(sel0["q_lo"][:].bitcast(F32), 0.0)
            nc.vector.memset(sel0["k_hi"][:].bitcast(F32), 0.0)
            step(nc.vector.memset(sel0["k_lo"][:].bitcast(F32), 0.0))
            dve.wait_ge(s["ld_small"], LD_SMALL)
            dve.wait_ge(s["pool_consts"], POOL_CONSTS)
            nc.vector.tensor_copy(fm_rep[0:DH], fm_w[0:DH, :].unsqueeze(1).to_broadcast([DH, H, DH]))
            nc.vector.tensor_copy(sign_id[0:DH, :, 0, :], ident[0:DH, 0:DH].unsqueeze(1).to_broadcast([DH, H, DH]))
            step(nc.vector.tensor_scalar(sign_id[0:DH, :, 1, :], ident[0:DH, 0:DH].unsqueeze(1).to_broadcast([DH, H, DH]),
                                         -1.0, None, ALU.mult))
            for b in range(B):
                ins = nc.vector.memset(v0[:, b].rearrange("p g (j x) -> p g j x", x=9 * F0)[:, :, :, 4 * F0:5 * F0], 1.0)
            ins.then_inc(s["fm_ok"], 1)
            sel_in = ident[:].rearrange("p (h f) -> p h f", f=F0)
            for name, quarters in (("q_hi", (0, 1)), ("q_lo", (2, 3)), ("k_hi", (0, 2)), ("k_lo", (1, 3))):
                for quarter in quarters:
                    ins = nc.vector.tensor_copy(sel0[name][:, :, quarter, :], sel_in)
            step(ins)
            step(nc.vector.tensor_tensor(pair32[0:32, :], ident[0:32, 0:16], ident[0:32, 16:32], ALU.add))
            nc.vector.tensor_copy(ind_rem[0:32], pair32[0:32, :].unsqueeze(2).to_broadcast([32, H, 32]))
            nc.vector.tensor_copy(ind[0:32], pair32[0:32, :].unsqueeze(2).to_broadcast([32, H, P])).then_inc(s["consts_dve"], 1)
            dve.wait_ge(s["ld_x"], 16)
            layer_norm(dve, step, s["xn_ok"])
            dve.wait_ge(s["ctxT_pe"], 1)
            step(nc.vector.tensor_copy(ctxT[:, :, 0:KEYS], bank[0][:, 0:B * KP].rearrange("p (b k) -> p b k", b=B)[:, :, 0:KEYS]))
            nc.vector.tensor_copy(ctxT_rep[:], ctxT[:, :, P:KP].unsqueeze(2).to_broadcast([P, B, 4, 32])).then_inc(s["ctxT_ok"], 1)
            dve.wait_ge(s["fm_pe"], 1)
            nc.vector.tensor_copy(wkvT[:], bank[2][:, 0:2 * DH])
            fmT = bank[2][:, 16:16 + DH].unsqueeze(1).to_broadcast([P, H, DH])
            mask = bmask[:].unsqueeze(2).to_broadcast([P, H, DH])
            nc.vector.tensor_copy(bias_col[:], bank[2][:, 24:25])
            nc.vector.tensor_copy(bias_row[0:1, :], bank[2][0:1, 128:128 + H * F0])
            nc.vector.tensor_tensor(wexp[:, :, 0, :], fmT, mask, ALU.mult)
            nc.vector.scalar_tensor_tensor(out=wexp[:, :, 1, :], in0=fmT, scalar=-1.0, in1=mask,
                                           op0=ALU.mult, op1=ALU.mult).then_inc(s["fm2_ok"], 1)
            for t in range(2):
                dve.wait_ge(s["kf_ok"], t + 1)
                step(nc.vector.tensor_copy(kf_hi[:, t, :], kf[:, t, :]))
                nc.vector.tensor_tensor(kf_lo[:, t, :], kf[:, t, :], kf_hi[:, t, :].bitcast(F32), ALU.subtract).then_inc(s["kf_split"], 1)
            for b in range(B):
                for t in range(2):
                    dve.wait_ge(s["f_ok"], 2 * b + t + 1)
                    step(nc.vector.tensor_copy(f_hi[:, t, b, :], f[:, t, b, :]))
                    nc.vector.tensor_tensor(f_lo[:, t, b, :], f[:, t, b, :], f_hi[:, t, b, :].bitcast(F32),
                                            ALU.subtract).then_inc(s["f_split"], 1)
            for p in range(NPAIR):
                dve.wait_ge(s["kst_pe"], p + 1)
                src = bank[(5, 6, 7, 0)[p % 4]][:, 0:B * KP].rearrange("p (b k) -> p b k", b=B)
                for a in range(2):
                    j = (2 * p + a) % 4
                    nc.vector.tensor_copy(kst0[64 * a:64 * a + 64, 2 * p + a], src[64 * a:64 * a + 64])
                    ins = nc.vector.tensor_copy(krem0[64 * a:64 * a + 64, :, p, j, 0:KR], src[64 * a:64 * a + 64, :, P:KEYS])
                ins.then_inc(s["kst_ok"], 1)
            for u in range(0, B * NPAIR, 2):
                b, p = divmod(u, NPAIR)
                dve.wait_ge(s["qst_pe"], u + 1)
                nc.vector.tensor_copy(qst[:, p, b, :], bank[1 + u % 4][:]).then_inc(s["qst_dve"], 1)

            attention_dve(dve, step, 0)
            dve.wait_ge(s["x1_ok"], 2)
            layer_norm(dve, step, s["xn_ok"])
            route_dve(dve, step, 0)
            experts_dve(dve, step, 0)
            layer_norm(dve, step, s["xn_ok"])
            hard_attention_dve(dve, step)
            attention_dve(dve, step, 1)
            dve.wait_ge(s["x1_ok"], 4)
            layer_norm(dve, step, s["xn_ok"])
            route_dve(dve, step, 1)
            dve.wait_ge(s["ld_gb"], 32)
            experts_dve(dve, step, 1)

        @block.scalar
        def _(act):
            act.wait_ge(s["wT_pe"], 1)
            nc.scalar.copy(small_wT[:].rearrange("p a d -> p (a d)"), bank[1][:]).then_inc(s["wT_ok"], 1)
            copy_xnT(act, 0)
            act.wait_ge(s["fm2_ok"], 1)
            for t in range(2):
                act.wait_ge(s["zk_pe"], t + 1)
                nc.scalar.activation(kf[:, t, :], bank[1 + t][:, 0:B * KP], ACT.Exp, bias=bias_col[:]).then_inc(s["kf_ok"], 1)
            for b in range(B):
                for t in range(2):
                    act.wait_ge(s["zq_pe"], 2 * b + t + 1)
                    nc.scalar.activation(f[:, t, b, :], bank[(5, 6, 7, 0)[2 * b + t]][:], ACT.Exp,
                                         bias=bias_col[:]).then_inc(s["f_ok"], 1)
            act.wait_ge(s["pool_consts"], POOL_CONSTS)
            act.wait_ge(s["fm_ok"], 1)
            for b in range(B):
                act.wait_ge(s["vz_pe"], b + 1)
                diagonal = v0[:, b].rearrange("p g (j x) -> p g j x", x=9 * F0)
                nc.scalar.activation(diagonal[:, :, :, 0:F0], bank[3 + b][:, 0:H * F0].rearrange("p (g j v) -> p g j v", g=NQUAD, j=4), ACT.Exp)
                for j in range(4):
                    rows = slice(32 * j, 32 * j + KR)
                    ins = nc.scalar.activation(vrem0[rows, b, :, j * F0:(j + 1) * F0],
                                               bank[3 + b][rows, H * F0:2 * H * F0].rearrange("p (g j v) -> p g j v", g=NQUAD, j=4)[:, :, j, :],
                                               ACT.Exp)
                ins.then_inc(s["v_ok"], 1)
            for u in range(1, B * NPAIR, 2):
                b, p = divmod(u, NPAIR)
                act.wait_ge(s["qst_pe"], u + 1)
                nc.scalar.copy(qst[:, p, b, :], bank[1 + u % 4][:]).then_inc(s["qst_act"], 1)
            attention_act(act, 0, SCALE0)
            copy_xnT(act, 1)
            experts_act(act, 0)
            copy_xnT(act, 2)
            for b in range(B):
                act.wait_ge(s["qp_pe"], b + 1)
                nc.scalar.copy(qp[:, b, :], bank[5 + b][:]).then_inc(s["qp_ok"], 1)
            attention_act(act, 1, SCALE1)
            copy_xnT(act, 3)
            experts_act(act, 1)

        @block.tensor
        def _(pe):
            pe.wait_ge(s["pool_consts"], 1)
            pe.wait_ge(s["ld_ctx"], 32)
            for b in range(B):
                nc.tensor.transpose(bank[0][:, b * KP:b * KP + P], ctx_main[:, b, :], ident[:])
                ins = nc.tensor.transpose(bank[0][:, b * KP + P:b * KP + KEYS], ctx_rem[0:KR, b, :], ident[0:KR, 0:KR])
            ins.then_inc(s["ctxT_pe"], 1)
            pe.wait_ge(s["ld_small"], LD_SMALL)
            for a in range(4):
                ins = nc.tensor.transpose(bank[1][:, a * P:(a + 1) * P], small_w[:, a, :], ident[:])
            ins.then_inc(s["wT_pe"], 1)
            nc.tensor.transpose(bank[2][:, 0:2 * DH], wkv[0:2 * DH, :], ident[0:2 * DH, 0:2 * DH])
            pe.wait_ge(s["fm_ok"], 1)
            mm(bank[2][:, 16:16 + DH], fm_rep[0:DH].rearrange("e h d -> e (h d)"), ident[0:DH, 0:DH], start=True, stop=True)
            mm(bank[2][:, 24:25], sign_id[0:DH, 0:8].rearrange("e h s f -> e (h s f)"), fm_b[0:DH, :], start=True, stop=True)
            mm(bank[2][0:1, 128:128 + H * F0], fm_b[0:DH, :], sign_id[0:DH].rearrange("e h s f -> e (h s f)"),
               start=True, stop=True).then_inc(s["fm_pe"], 1)
            pe.wait_ge(s["xn_ok"], 1)
            transpose_xn(pe)
            pe.wait_ge(s["wT_ok"], 1)
            pe.wait_ge(s["ctxT_ok"], 1)
            pe.wait_ge(s["fm2_ok"], 1)
            wexp_t = wexp[:].rearrange("p h s e -> p (h s e)")
            for t in range(2):
                mm(bank[1 + t][:, 0:B * KP], wexp_t[:, t * P:(t + 1) * P], ctxT[:].rearrange("p b k -> p (b k)"),
                   start=True, stop=True).then_inc(s["zk_pe"], 1)
            for b in range(B):
                pe.wait_ge(s["xnT_ok"], b + 1)
                for t in range(2):
                    mm(bank[(5, 6, 7, 0)[2 * b + t]][:], wexp_t[:, t * P:(t + 1) * P], xnT[:, b, :],
                       start=True, stop=True).then_inc(s["zq_pe"], 1)
            for b in range(B):
                for half, lhs in enumerate((ctxT[:, b, 0:P], ctxT_rep[:, b].rearrange("p j k -> p (j k)"))):
                    dst = bank[3 + b][:, half * H * F0:(half + 1) * H * F0]
                    mm(dst, lhs, wexp_t[:], start=True, stop=False)
                    ins = mm(dst, ones[0:1, 0:P], bias_row[0:1, :], start=False, stop=True)
                ins.then_inc(s["vz_pe"], 1)
            pe.wait_ge(s["f_ok"], 4)
            pe.wait_ge(s["kf_split"], 2)
            pe.wait_ge(s["consts_dve"], 1)
            for p in range(NPAIR):
                t, i = divmod(p, 4)
                if p >= 4:
                    pe.wait_ge(s["kst_ok"], p - 3)
                dst = bank[(5, 6, 7, 0)[p % 4]][:, 0:B * KP]
                mm(dst, sel0["k_hi"][:, 2 * i:2 * i + 2].rearrange("p a c f -> p (a c f)"), kf_hi[:, t, :], start=True, stop=False)
                mm(dst, sel0["k_lo"][:, 2 * i:2 * i + 2].rearrange("p a c f -> p (a c f)"), kf_lo[:, t, :],
                   start=False, stop=True).then_inc(s["kst_pe"], 1)
            pe.wait_ge(s["kf_ok"], 2)
            pe.wait_ge(s["v_ok"], 2)
            for u in range(B * NPAIR):
                b, p = divmod(u, NPAIR)
                t, i = divmod(p, 4)
                pe.wait_ge(s["f_split"], 2 * b + t + 1)
                if u >= 4:
                    wait_qst(pe, u - 4)
                dst = bank[1 + u % 4][:]
                mm(dst, sel0["q_hi"][:, 2 * i:2 * i + 2].rearrange("p a c f -> p (a c f)"), f_hi[:, t, b, :], start=True, stop=False)
                mm(dst, sel0["q_lo"][:, 2 * i:2 * i + 2].rearrange("p a c f -> p (a c f)"), f_lo[:, t, b, :],
                   start=False, stop=True).then_inc(s["qst_pe"], 1)
            pe.wait_ge(s["kst_ok"], NPAIR)
            pe.wait_ge(s["qst_dve"], B * NPAIR // 2)
            pe.wait_ge(s["qst_act"], B * NPAIR // 2)

            def query(b, h, cols):
                return qst[:, h // 2, b, cols]

            def keys(b, h, heads, n):
                return kst0[:, h:h + heads, b, 0:n]

            def rem_scores(dst, b, hg):
                for i in range(2):
                    p = 2 * hg + i
                    mm(dst, krem0[:, b, p].rearrange("p j k -> p (j k)"), qst[:, p, b, :], start=(i == 0), stop=False)

            attention_pe(pe, 0, 2, query, keys, rem_scores, lambda b, hg, j: v0[:, b, hg, j * 8 * F0:(j + 1) * 8 * F0],
                         lambda b, hg: vrem0[:, b, hg, :])
            pe.wait_ge(s["xn_ok"], 2)
            transpose_xn(pe)
            experts_pe(pe, 0)
            pe.wait_ge(s["xn_ok"], 3)
            transpose_xn(pe)
            hard_attention_pe(pe)
            attention_pe(pe, 1, 4, lambda b, h, cols: qst[:, h // 4, b, cols],
                         lambda b, h, heads, n: kst1[:, h % 4:h % 4 + heads, b, 0:n],
                         lambda dst, b, hg: mm(dst, krem1[:, b].rearrange("p a k -> p (a k)"), qst[:, hg, b, :], start=True, stop=False),
                         lambda b, hg, j: v1[:, b, j * 8 * DH:(j + 1) * 8 * DH], lambda b, hg: vrem1[:, b, :])
            pe.wait_ge(s["xn_ok"], 4)
            transpose_xn(pe)
            experts_pe(pe, 1)

_OUTS = [((B, S, D), "float32")]


def kernel(**inputs):
    import numpy as _np
    import concourse.bacc as _bacc
    from concourse import mybir as _mybir
    from concourse.bass_utils import run_bass_kernel_spmd as _run

    nc = _bacc.Bacc("TRN2", target_bir_lowering=False, num_devices=1)
    arrays, args = {}, {}
    for name in inputs:
        a = _np.ascontiguousarray(inputs[name])
        arrays[f"in_{name}_dram"] = a
        args[name] = nc.dram_tensor(f"in_{name}_dram", a.shape, _mybir.dt.from_np(a.dtype), kind="ExternalInput").ap()
    out = nc.dram_tensor("out_0_dram", _OUTS[0][0], _mybir.dt.float32, kind="ExternalOutput").ap()
    build(nc, args, out)
    r = _run(nc, [arrays], core_ids=[0])
    return r.results[0]["out_0_dram"]
```

```python
import numpy as np
import concourse.bass as bass
from concourse import mybir
from contextlib import ExitStack

F32 = mybir.dt.float32
F32R = mybir.dt.float32r
BF16 = mybir.dt.bfloat16
I32 = mybir.dt.int32
U32 = mybir.dt.uint32
ALU = mybir.AluOpType
ACT = mybir.ActivationFunctionType
AX = mybir.AxisListType

P = 128
B, S, D = 2, 512, 128
T = B * S // P
QT = S // P
KEYS = 154
KM, KR = P, KEYS - P
KP = 160
H, DH = 16, D // 16
F0 = 2 * DH
NPAIR, NQUAD = H // 2, H // 4
PARTS = 2 * QT
POOL_ROWS = 9
FIRST_STACKS = 8
GATHERED = tuple(f"gathered_{i}" for i in range(14))
SCATTERED = tuple(f"scattered_{i}" for i in range(4))
HID = 512
EXPERTS = (8, 16)
TILES = tuple((2 * B * S - E) // P + E for E in EXPERTS)
EPS = 1e-5
MASKED = -float(2 ** 100)
SCALE0 = float(1.0 / np.sqrt(np.float32(D)))
SCALE1 = float(np.float32(1.0 / np.sqrt(DH)))


def even(n):
    return n + n % 2


class Steps:

    def __init__(self, engine, semaphore):
        self.engine, self.semaphore, self.count = engine, semaphore, 0

    def __call__(self, instruction):
        self.wait(self.mark(instruction))

    def mark(self, instruction):
        self.count += 1
        instruction.then_inc(self.semaphore, 1)
        return self.count

    def wait(self, count):
        self.engine.wait_ge(self.semaphore, count)


def build(nc, A, out):
    ctx = ExitStack()
    with ctx:
        base = [(nc.sbuf_base + 31) // 32 * 32]

        def sb(name, shape, dt):
            n = int(np.prod(shape[1:])) * (2 if dt == BF16 else 4)
            t = nc.alloc_sbuf_tensor_at(name, shape, dt, offset=base[0])
            base[0] += (n + 31) // 32 * 32
            return t

        def sem(name):
            return ctx.enter_context(nc.semaphore(name))

        bank = [ctx.enter_context(nc.psum_tensor(f"bank{i}", [P, 512], F32)) for i in range(8)]

        ident = sb("ident", [P, P], F32)
        ones = sb("ones", [P, P], F32)
        ones_r = sb("ones_r", [P, 512], F32R)
        ones_b = sb("ones_b", [P, P], BF16)
        tri = sb("tri", [P, P], BF16)
        iota_e = sb("iota_e", [P, 16], F32)
        iota_s = sb("iota_s", [P, 32], F32)
        iota_k = sb("iota_k", [P, 2 * P], F32)
        x = sb("x", [P, T, D], F32)
        xn = sb("xn", [P, T, D], F32)
        xnT = sb("xnT", [P, B, S], F32)
        stats = sb("stats", [P, T, 6], F32)
        mv = sb("mv", [P, T, 2], F32)
        rstd = sb("rstd", [P, T], F32)
        var = sb("var", [P, T], F32)
        guess = sb("guess", [P, T], F32)
        newton = sb("newton", [P, T], F32)
        ctx_main = sb("ctx_main", [P, B, D], F32)
        ctx_rem = sb("ctx_rem", [P, B, D], F32)
        ctxT = sb("ctxT", [P, B, KP], F32)
        ctxT_rep = sb("ctxT_rep", [P, B, 4, 32], F32)
        small_w = sb("small_w", [P, 4, D], F32)
        small_wT = sb("small_wT", [P, 4, D], F32)
        wkv = sb("wkv", [P, D], F32)
        wkvT = sb("wkvT", [P, 2 * DH], F32)
        fm_w = sb("fm_w", [P, DH], F32)
        fm_b = sb("fm_b", [P, 1], F32)
        fc_b = sb("fc_b", [P, D], F32)
        ind = sb("ind", [P, H, 32], F32R)
        wr = [sb(f"wr{L}", [P, E], F32) for L, E in enumerate(EXPERTS)]
        br = [sb(f"br{L}", [P, E], F32) for L, E in enumerate(EXPERTS)]
        top8 = sb("top8", [P, T, 8], F32)
        top8_at = sb("top8_at", [P, T, 8], U32)
        top2_at = sb("top2_at", [P, 2, T], F32)
        onehot = sb("onehot", [P, 2, T, 16], F32)
        chosen = sb("chosen", [P, T, 16], BF16)
        gate = sb("gate", [P, 4, T], F32)
        gate_hi = sb("gate_hi", [P, 2, T], F32R)
        gate_lo = sb("gate_lo", [P, 2, T], F32R)
        counts_f = sb("counts_f", [P, 16], F32)
        counts_i = sb("counts_i", [P, 2, 16], I32)
        tiles_f = sb("tiles_f", [P, 16], F32)
        scan = [sb(f"scan{i}", [P, 32], F32) for i in range(2)]
        ranked = sb("ranked", [P, 2, T, 16], F32)
        slot_f = sb("slot_f", [P, 2, T], F32)
        slot_i = sb("slot_i", [P, 3, 2, T], I32)
        slot_rt = sb("slot_rt", [P, 2, 2, T], F32)
        slot_gate = sb("slot_gate", [P, 32], F32)
        slot_from = sb("slot_from", [P, 32], I32)
        slot_to = sb("slot_to", [P, 32], I32)
        slot_none = sb("slot_none", [P, 32], F32)
        place_1 = sb("place_1", [P, 2, T], F32)
        iota_r = sb("iota_r", [P, P], F32)
        warm = sb("warm", [P, 1], F32)
        spare_row = sb("spare_row", [P, 32], F32)
        before = sb("before", [P, 32, 16], F32)
        expert_f = sb("expert_f", [P, 32], F32)
        expert_i = sb("expert_i", [P, 32], I32)
        shared = base[0]
        mx = sb("mx", [P, B, QT, H], F32)
        nm_hi = sb("nm_hi", [P, B, QT, H], F32R)
        nm = sb("nm", [P, B, QT, 2, H], F32)
        nmT = sb("nmT", [P, B, S], F32R)
        qst = sb("qst", [P, NPAIR, B, S], F32R)
        prob = sb("prob", [P, 2, 5, 512], F32)
        oT = sb("oT", [P, 2, B, S], F32)
        f = prob[:, 0].rearrange("p a q -> p (a q)")[:, 0:2 * B * S].rearrange("p (n b q) -> p n b q", n=2, b=B)
        kf = prob[:, 1].rearrange("p a q -> p (a q)")[:, 0:2 * B * KP].rearrange("p (n k) -> p n k", n=2)
        shared_end = base[0]
        base[0] = shared
        gx = sb("gx", [P, max(TILES), D], F32)
        gxT = sb("gxT", [P, 2, P], F32)
        parts = gx[:, 0:2 * T, :]
        slots_at = base[0]
        slot_hit = sb("slot_hit", [P, 2 * T, 32], F32)
        slot_tile = sb("slot_tile", [P, 2 * T, 3, 32], F32R)
        slot_row = sb("slot_row", [P, 2 * T, P], F32R)
        slots_end, base[0] = base[0], slots_at
        hid = sb("hid", [P, 2, HID], F32)
        act_h = sb("act_h", [P, 2, HID], F32)
        hidT = sb("hidT", [P, 2, HID], F32)
        y = sb("y", [P, 8, D], F32)
        ys = sb("ys", [P, 4, D], F32)
        y_stats = sb("y_stats", [P, 4, 6], F32)
        y_mv = sb("y_mv", [P, 4, 2], F32)
        y_root = sb("y_root", [P, 5, 4], F32)
        spare = base[0]
        assert slots_end <= spare
        b1_cols = sb("b1_cols", [P, 32 + 8], F32)
        b1_hi = sb("b1_hi", [P, 32 + 8], F32R)
        b1_lo = sb("b1_lo", [P, 32 + 8], F32R)
        b1_rows = sb("b1_rows", [P, EXPERTS[0] * (HID + D)], F32R)
        assert base[0] <= shared_end, (base[0], shared_end)
        base[0] = spare
        gamma = sb("gamma", [P, EXPERTS[1], D], F32)
        beta = sb("beta", [P, EXPERTS[1], D], F32)
        assert base[0] <= shared_end, (base[0], shared_end)
        base[0] = scratch0 = shared_end
        bmask = sb("bmask", [P, H], F32)
        sign_id = sb("sign_id", [P, H, 2, DH], F32)
        fm_rep = sb("fm_rep", [P, H, DH], F32)
        wexp = sb("wexp", [P, H, 2, DH], F32)
        bias_col = sb("bias_col", [P, 1], F32)
        bias_row = sb("bias_row", [P, H * F0], F32)
        f_hi = sb("f_hi", [P, 2, B, S], F32R)
        f_lo = sb("f_lo", [P, 2, B, S], F32R)
        split_at = base[0]
        kf_hi = sb("kf_hi", [P, 2, B * KP], F32R)
        kf_lo = sb("kf_lo", [P, 2, B * KP], F32R)
        sel0 = {n: sb(f"sel0_{n}", [P, 8, 4, F0], F32R) for n in ("q_hi", "q_lo", "k_hi", "k_lo")}
        kst0 = sb("kst0", [P, H, B, KP], F32R)
        krem0 = sb("krem0", [P, B, NPAIR, 4, 32], F32R)
        scratch0_end = base[0]
        base[0] = split_at
        recips0 = sb("recips0", [P, 2, S], F32)
        base[0] = scratch0
        w1_1 = sb("w1_1", [P, EXPERTS[1] * HID], F32)
        w3_1 = sb("w3_1", [P, EXPERTS[1] * HID], F32)
        base[0] = weights0 = max(base[0], scratch0_end)
        w1_0 = sb("w1_0", [P, EXPERTS[0] * HID], F32)
        w2_0 = sb("w2_0", [P, EXPERTS[0] * HID], F32)
        base[0] = weights0
        v0 = sb("v0", [P, B, NQUAD, 4 * (8 + 1) * F0], F32)
        vrem0 = sb("vrem0", [P, B, NQUAD, 8 * F0], F32)
        base[0] = weights0
        w2_1 = sb("w2_1", [P, EXPERTS[1] * HID], F32)
        base[0] = weights0
        qp = sb("qp", [P, B, S], F32)
        qp_hi = sb("qp_hi", [P, B, S], F32R)
        qp_lo = sb("qp_lo", [P, B, S], F32R)
        sel1 = {n: sb(f"sel1_{n}", [P, H, 4, DH], F32R) for n in ("q_hi", "q_lo")}
        sel1k = {n: sb(f"sel1_{n}", [P, 4, 4, DH], F32R) for n in ("k_hi", "k_lo", "mask")}
        hits = sb("hits", [P, QT, 2 * P], BF16)
        hit8 = sb("hit8", [P, T, 8], F32)
        hit8_at = sb("hit8_at", [P, T, 8], U32)
        hit_f = sb("hit_f", [P, T], F32)
        counts = sb("counts", [P, 2 * B], F32)
        mask_row = sb("mask_row", [P, B * KP], F32R)
        mk_hi = sb("mk_hi", [P, B * KP], F32R)
        mk_lo = sb("mk_lo", [P, B * KP], F32R)
        kst1 = sb("kst1", [P, 4, B, KP], F32R)
        krem1 = sb("krem1", [P, B, 4, 32], F32R)
        v1 = sb("v1", [P, B, 4 * (8 + 1) * DH], F32)
        vrem1 = sb("vrem1", [P, B, 8 * DH], F32)
        normed = [nc.dram_tensor(f"normed{L}", (B * S, D), F32, kind="Internal").ap() for L in range(2)]
        results = [nc.dram_tensor(f"results{L}", (2 * B * S + TILES[L] * P, D), F32, kind="Internal").ap() for L in range(2)]

        s = {n: sem(n) for n in (
            "ld_x", "ld_ctx", "ld_small", "pool_step", "pool_consts", "dve_step",
            "xn_ok", "ctxT_pe", "wT_pe", "ctxT_ok", "wT_ok", "xnT_pe", "xnT_ok",
            "fm_pe", "fm_ok", "fm2_ok", "zq_pe", "f_ok", "zk_pe", "kf_ok", "vz_pe", "v_ok", "f_split",
            "kf_split",  "stack_pe", "stack_dve", "stack_act", "f_split_pool", "score_pe", "max_ok", "nm_ok",
            "nmT_pe", "nmT_ok", "prob_pe", "prob_ok", "pv_pe", "o_ok", "fc_pe", "x1_ok", "stored",
            "ld_b1", "ld_b1_rows", "ld_gb", "qp_pe", "qp_ok", "qp_split", "sel1_ok", "mask_ok", "v1_ok", "krem1_ok", "ld_fm", "hit_pe", "hit_ok", "count_pe", 
            "mk_pe", "mk_ok", "kst1_pe", "kst1_ok", "qst1_pe", "qst1_ok", "b1_ok",
            *GATHERED, *SCATTERED)}
        r = [{n: sem(f"{n}_L{L}") for n in (
            "ld_w", "logits_pe", "diff_ok", "exp_ok", "chosen_ok", "rank_pe", "slots_ok", "experts_ok",
            "saved", "place_ok", "slot_tile_ok", "slot_row_ok", "slot_row_dve", "slot_pe",  "gxT_pe", "gxT_ok", "up_pe", "act_ok", "hid_ok", "hidT_pe", "hidT_ok", "y_pe",
            "y_ok", "y_copied", "y_stats_ok", "mixed_0", "mixed_1", "summed")} for L in range(2)]

        def gathered(L, t):
            u = t + L * TILES[0]
            return s[GATHERED[u % 14]], 16 * (u // 14 + 1)

        def scattered(L, t):
            u = t + L * TILES[0]
            return s[SCATTERED[u % 4]], 16 * (u // 4 + 1)

        block = ctx.enter_context(nc.Block())

        LD_SMALL = 16 * 9

        POOL_CONSTS = 6

        def root_starts(step, variance, var, guess, root):
            step(nc.vector.tensor_scalar(var, variance, EPS, None, ALU.add))
            step(nc.vector.tensor_scalar(guess.bitcast(I32), var.bitcast(I32), 1, None, ALU.arith_shift_right))
            step(nc.vector.tensor_scalar(root.bitcast(I32), guess.bitcast(I32), -1.0, float(0x5F3759DF), ALU.mult, ALU.add))

        def root_goes_on(step, times, var, newton, root):
            for _ in range(times):
                step(nc.vector.tensor_tensor(newton, root, root, ALU.mult))
                step(nc.vector.scalar_tensor_tensor(out=newton, in0=newton, scalar=-0.5, in1=var, op0=ALU.mult, op1=ALU.mult))
                step(nc.vector.scalar_tensor_tensor(out=root, in0=newton, scalar=1.5, in1=root, op0=ALU.add, op1=ALU.mult))

        def norm_roots(step, first, end):
            for t in range(first, end):
                ins = nc.vector.bn_stats(stats[:, t, :], x[:, t, :])
            step(ins)
            for t in range(first, end):
                ins = nc.vector.bn_aggr(mv[:, t, :], stats[:, t, :])
            step(ins)
            root_starts(step, mv[:, first:end, 1], var[:, first:end], guess[:, first:end], rstd[:, first:end])
            root_goes_on(step, 3, var[:, first:end], newton[:, first:end], rstd[:, first:end])

        def norm_write(b):
            for t in range(b * QT, (b + 1) * QT):
                ins = nc.vector.tensor_scalar(xn[:, t, :], x[:, t, :], mv[:, t, 0:1], rstd[:, t:t + 1],
                                              ALU.subtract, ALU.mult)
            ins.then_inc(s["xn_ok"], 1)

        def layer_norm(step):
            norm_roots(step, 0, T)
            for b in range(B):
                norm_write(b)

        def maxima(dve, L, group, parts):
            b, hg = divmod(group, NQUAD)
            for n in parts:
                qt, pair = divmod(n, 2)
                u = group * PARTS + n
                h = 4 * hg + 2 * pair
                dve.wait_ge(s["score_pe"], L * B * NQUAD * PARTS + u + 1)
                nc.vector.tensor_reduce(mx[:, b, qt, h:h + 2], bank[6 + u % 2][:, 0:2 * KEYS].rearrange("p (h k) -> p h k", h=2),
                                        AX.X, ALU.max).then_inc(s["max_ok"], 1)

        def negate_maxima(dve, step, L, group):
            b, hg = divmod(group, NQUAD)
            dve.wait_ge(s["max_ok"], (L * B * NQUAD + group + 1) * PARTS)
            heads = slice(4 * hg, 4 * hg + 4)
            step(nc.vector.tensor_scalar(nm_hi[:, b, :, heads], mx[:, b, :, heads], -1.0, None, ALU.mult))
            nc.vector.tensor_copy(nm[:, b, :, 0, heads], nm_hi[:, b, :, heads].bitcast(F32))
            nc.vector.scalar_tensor_tensor(out=nm[:, b, :, 1, heads], in0=mx[:, b, :, heads], scalar=-1.0,
                                           in1=nm_hi[:, b, :, heads].bitcast(F32),
                                           op0=ALU.mult, op1=ALU.subtract).then_inc(s["nm_ok"], 1)

        reciprocal_at = {}

        def normalise_piece(dve, step, L, g, qt):
            b, hg = divmod(g, NQUAD)
            rows = 4 * (F0 if L == 0 else DH)
            acc = bank[(0, 4)[g % 2]]
            recip = (recips0[:, g % 2, :] if L == 0 else qp[:, g % 2, :])
            n, at = divmod(hg * rows, P)

            def product(i):
                cols = slice(i * P, (i + 1) * P)
                step.wait(reciprocal_at[i])
                return nc.vector.tensor_tensor(oT[at:at + rows, n, b, cols], acc[0:rows, cols], recip[0:rows, cols], ALU.mult)

            if qt == 0:
                dve.wait_ge(s["pv_pe"], L * B * NQUAD + g + 1)
            cols = slice(qt * P, (qt + 1) * P)
            reciprocal_at[qt] = step.mark(nc.vector.reciprocal(recip[0:rows, cols], acc[rows:2 * rows, cols]))
            if qt:
                product(qt - 1)
            if qt == QT - 1:
                product(qt).then_inc(s["o_ok"], 1)

        def normalise(dve, step, L, b, hg):
            g = b * NQUAD + hg
            rows = 4 * (F0 if L == 0 else DH)
            acc = bank[(0, 4)[g % 2]]
            recip = (recips0[:, g % 2, :] if L == 0 else qp[:, g % 2, :])
            n, at = divmod(hg * rows, P)
            dve.wait_ge(s["pv_pe"], L * B * NQUAD + g + 1)
            pieces = 2 if g == B * NQUAD - 1 else 1
            for i in range(pieces):
                cols = slice(i * S // pieces, (i + 1) * S // pieces)
                step(nc.vector.reciprocal(recip[0:rows, cols], acc[rows:2 * rows, cols]))
                nc.vector.tensor_tensor(oT[at:at + rows, n, b, cols], acc[0:rows, cols], recip[0:rows, cols], ALU.mult).then_inc(s["o_ok"], 1)

        def projected(b, half):
            return bank[7 if b == 1 and half == 1 else 5 + b]

        def add_projected(dve, step, L, b, half=None):
            if half is None:
                at, n, count = 0, QT, 1
            else:
                at, n, count = half * 2, 2, 2 + half
            dve.wait_ge(s["fc_pe"], 3 * L + count)
            tiles = slice(b * QT + at, b * QT + at + n)
            nc.vector.tensor_tensor(x[:, tiles, :], x[:, tiles, :],
                                    projected(b, half)[:, at * D:(at + n) * D].rearrange("p (q e) -> p q e", q=n), ALU.add).then_inc(s["x1_ok"], 1)

        def attention_dve(dve, step, L):
            maxima(dve, L, 0, range(PARTS))
            negate_maxima(dve, step, L, 0)
            maxima(dve, L, 1, range(2))
            for group in range(B * NQUAD):
                def divide(qt):
                    if group >= 2:
                        normalise_piece(dve, step, L, group - 2, qt)

                if group + 1 < B * NQUAD:
                    for qt in range(1, QT):
                        divide(qt - 1)
                        maxima(dve, L, group + 1, (2 * qt, 2 * qt + 1))
                    negate_maxima(dve, step, L, group + 1)
                    divide(3)
                    if group + 2 < B * NQUAD:
                        maxima(dve, L, group + 2, range(2))
                elif group >= 2:
                    normalise(dve, step, L, *divmod(group - 2, NQUAD))
                if group == 7:
                    add_projected(dve, step, L, 0)
                    dve.wait_ge(s["x1_ok"], 3 * L + 1)
                    norm_roots(step, 0, QT)
                    norm_write(0)
            normalise(dve, step, L, 1, 2)
            normalise(dve, step, L, 1, 3)
            pick_experts(dve, step, L, 0)
            for half in range(2):
                add_projected(dve, step, L, 1, half)
            dve.wait_ge(s["x1_ok"], 3 * L + 3)
            norm_roots(step, QT, T)
            norm_write(1)

        def copy_maxima(act, L, group):
            act.wait_ge(s["nmT_pe"], L * B * NQUAD + group + 1)
            nc.scalar.copy(nmT[0:32, group % 2, :], bank[3][0:32, :]).then_inc(s["nmT_ok"], 1)

        def attention_act(act, L, scale, beside=lambda group, i: None):
            copy_maxima(act, L, 0)
            for g in range(B * NQUAD):
                group = L * B * NQUAD + g
                if group >= 2:
                    act.wait_ge(s["pv_pe"], group - 1)
                for i in range(5):
                    u = g * 5 + i
                    act.wait_ge(s["prob_pe"], L * B * NQUAD * 5 + u + 1)
                    nc.scalar.activation(prob[:, group % 2, i, :], bank[1 + u % 2][:], ACT.Exp,
                                         scale=scale).then_inc(s["prob_ok"], 1)
                    beside(g, i)
                if g + 1 < B * NQUAD:
                    copy_maxima(act, L, g + 1)
            for b in range(B):
                copy_xnT(act, 2 * L + 1, b, (1, 7)[b])

        mm = nc.tensor.matmul

        def stack_bank(u):
            return bank[1 + u % 4 if u < FIRST_STACKS else 3]

        def stack_of(u):
            if u < 2 * NPAIR:
                return ("q" if u % 2 else "k"), 0, u // 2
            return "q", 1, u - 2 * NPAIR

        def key_stack_copies(copy, u):
            p = u // 2
            src = stack_bank(u)[:, 0:B * KP].rearrange("p (b k) -> p b k", b=B)
            for a in range(2):
                rows = slice(64 * a, 64 * a + 64)
                copy(kst0[rows, 2 * p + a], src[rows])
                ins = copy(krem0[rows, :, p, (2 * p + a) % 4, 0:KR], src[rows, :, P:KEYS])
            return ins

        def copy_stack(act, u):
            if u not in (0, 2):
                kind, b, p = stack_of(u)
                act.wait_ge(s["stack_pe"], u + 1)
                if kind == "k":
                    ins = key_stack_copies(nc.scalar.copy, u)
                else:
                    ins = nc.scalar.copy(qst[:, p, b, :], stack_bank(u)[:])
                ins.then_inc(s["stack_act"], 1)

        def wait_stack(pe, u):
            if u in (0, 2):
                pe.wait_ge(s["stack_dve"], u // 2 + 1)
            else:
                pe.wait_ge(s["stack_act"], 1 if u == 1 else u - 1)

        def turn_xn(pe, n, b, to):
            pe.wait_ge(s["xn_ok"], B * n + b + 1)
            for qt in range(QT):
                ins = nc.tensor.transpose(bank[to][:, qt * P:(qt + 1) * P], xn[:, b * QT + qt, :], ident[:])
            ins.then_inc(s["xnT_pe"], 1)

        def copy_xnT(act, n, b, at):
            act.wait_ge(s["xnT_pe"], B * n + b + 1)
            nc.scalar.copy(xnT[:, b, :], bank[at][:]).then_inc(s["xnT_ok"], 1)

        def router_scores(pe, L, b):
            E = EXPERTS[L]
            pe.wait_ge(s["xnT_ok"], B * (2 * L + 1) + b + 1)
            if b == 0:
                mm(bank[5][:, 0:T * E].rearrange("p (t e) -> p t e", t=T), ones[0:1, 0:P],
                   br[L][0:1, :].unsqueeze(1).to_broadcast([1, T, E]), start=True, stop=False, skip_group_check=True)
            for qt in range(QT):
                t = b * QT + qt
                ins = mm(bank[5][:, t * E:(t + 1) * E], xnT[:, b, qt * P:(qt + 1) * P], wr[L][:], start=False, stop=True,
                         skip_group_check=True)
            ins.then_inc(r[L]["logits_pe"], 1)

        def attention_pe(pe, L, query, keys, rem_scores, values, rem_values, beside=lambda group, i: None):
            first = L * B * NQUAD
            o_first = L * (B * NQUAD + 1)

            def score_part(group, n):
                b, hg = divmod(group, NQUAD)
                qt, pair = divmod(n, 2)
                u = group * PARTS + n
                if u >= 2:
                    pe.wait_ge(s["max_ok"], first * PARTS + u - 1)
                h = 4 * hg + 2 * pair
                mm(bank[6 + u % 2][:, 0:2 * KEYS].rearrange("p (h k) -> p h k", h=2), query(b, h, slice(qt * P, (qt + 1) * P)),
                   keys(b, h, 2, KEYS), start=True, stop=True).then_inc(s["score_pe"], 1)

            def turn_max(group):
                b = group // NQUAD
                pe.wait_ge(s["nm_ok"], first + group + 1)
                for qt in range(QT):
                    ins = nc.tensor.transpose(bank[3][0:32, qt * P:(qt + 1) * P],
                                              nm[:, b, qt].rearrange("p a h -> p (a h)"), ident[:])
                ins.then_inc(s["nmT_pe"], 1)

            def prob_unit(b, hg, i):
                u = (b * NQUAD + hg) * 5 + i
                if u >= 2:
                    pe.wait_ge(s["prob_ok"], first * 5 + u - 1)
                dst = bank[1 + u % 2][:]
                if i == 0:
                    if L == 1 and b == 0 and hg == 0:
                        pe.wait_ge(s["krem1_ok"], 1)
                    rem_scores(dst, b, hg)
                    lhs = ind[0:32, 4 * hg:4 * hg + 4, :].rearrange("p h k -> p (h k)")
                else:
                    h = 4 * hg + i - 1
                    mm(dst, keys(b, h, 1, P)[:, 0, :], query(b, h, slice(0, S)), start=True, stop=False)
                    lhs = ind[0:32, h, 0:1].to_broadcast([32, P])
                mm(dst, lhs, nmT[0:32, (b * NQUAD + hg) % 2, :], start=False, stop=True).then_inc(s["prob_pe"], 1)

            def sum_unit(group, i):
                b, hg = divmod(group, NQUAD)
                pe.wait_ge(s["prob_ok"], 5 * (first + group) + i + 1)
                if group == 0 and i == 0:
                    pe.wait_ge(s["v1_ok"], 1) if L == 1 else pe.wait_ge(s["v_ok"], 2)
                if i == 0 and group >= 2:
                    pe.wait_ge(s["o_ok"], o_first + group - 1)
                lhs = rem_values(b, hg) if i == 0 else values(b, hg, i - 1)
                ins = mm(bank[(0, 4)[group % 2]][0:lhs.shape[-1], :], lhs, prob[:, group % 2, i, :], start=(i == 0), stop=(i == 4))
                if i == 4:
                    ins.then_inc(s["pv_pe"], 1)

            def project_part(b, i, half=None):
                last = L == 1 or i == 1
                for qt in (range(QT) if half is None else (2 * half, 2 * half + 1)):
                    ins = mm(projected(b, qt // 2)[:, qt * P:(qt + 1) * P], oT[:, i, b, qt * P:(qt + 1) * P],
                             small_wT[:, (0 if L == 0 else 3) + i, :], start=(L == 1), stop=last, skip_group_check=True)
                if last:
                    ins.then_inc(s["fc_pe"], 1)

            def project_early(b):
                for half in range(B):
                    if b == 1 or half == 0:
                        mm(projected(b, half)[:].rearrange("p (q e) -> p q e", q=QT), ones[0:1, 0:P],
                           fc_b[0:1, :].unsqueeze(1).to_broadcast([1, QT, D]), start=True, stop=False, skip_group_check=True)
                project_part(b, 0)

            for n in range(PARTS):
                beside(-1, n)
                score_part(0, n)
            for n in range(2):
                beside(-1, PARTS + n)
                score_part(1, n)
            turn_max(0)
            for group in range(B * NQUAD):
                b, hg = divmod(group, NQUAD)
                pe.wait_ge(s["nmT_ok"], first + group + 1)
                for i in range(5):
                    prob_unit(b, hg, i)
                    beside(group, i)
                    if i == 4 and group + 1 < B * NQUAD:
                        turn_max(group + 1)
                    if group:
                        sum_unit(group - 1, i)
                    if i < 3 and group + 1 < B * NQUAD:
                        score_part(group + 1, 2 * i + 2)
                        score_part(group + 1, 2 * i + 3)
                    if i == 4 and group + 2 < B * NQUAD:
                        score_part(group + 2, 0)
                        score_part(group + 2, 1)
                if group == NQUAD + 1:
                    pe.wait_ge(s["o_ok"], o_first + NQUAD)
                    if L == 0:
                        project_early(0)
                    project_part(0, 1 if L == 0 else 0)
            for i in range(5):
                sum_unit(B * NQUAD - 1, i)
                if L == 0 and i == 3:
                    pe.wait_ge(s["o_ok"], o_first + NQUAD + 2)
                    project_early(1)
            turn_xn(pe, 2 * L + 1, 0, 1)
            router_scores(pe, L, 0)
            for half in range(2):
                pe.wait_ge(s["o_ok"], o_first + B * NQUAD + half)
                project_part(1, 1 if L == 0 else 0, half)
            turn_xn(pe, 2 * L + 1, 1, 7)
            router_scores(pe, L, 1)


        def experts_sync(sp, L):
            for b in range(B):
                if L == 0 and b == 1:
                    sp.wait_ge(s["x1_ok"], 3)
                    sp.dma_start(b1_cols[:, 0:32], A["L0_ffn_b1"].rearrange("e f -> (e f)").rearrange("(p c) -> p c", c=32)).then_inc(s["ld_b1"], 16)
                    sp.dma_start(b1_cols[:, 32:40], A["L0_ffn_b2"].rearrange("e f -> (e f)").rearrange("(p c) -> p c", c=8)).then_inc(s["ld_b1"], 16)
                    sp.dma_start(w1_0[:].rearrange("p (e f) -> p e f", f=HID), A["L0_ffn_W1"].rearrange("e d f -> d e f")).then_inc(r[0]["ld_w"], 16)
                    sp.dma_start(w2_0[:].rearrange("p (e c d) -> p e c d", c=4, d=D),
                                 A["L0_ffn_W2"].rearrange("e (c p) d -> p e c d", p=P)).then_inc(r[0]["ld_w"], 16)
                sp.wait_ge(s["xn_ok"], B * (2 * L + 1) + b + 1)
                sp.dma_start(normed[L][b * S:(b + 1) * S].rearrange("(t p) d -> p t d", p=P),
                             xn[:, b * QT:(b + 1) * QT, :]).then_inc(r[L]["saved"], 16)
            if L == 0:
                sp.wait_ge(s["b1_ok"], 1)
                n = EXPERTS[0] * HID
                for row, part in enumerate((b1_hi, b1_lo)):
                    sp.dma_start(b1_rows[row:row + 1, 0:n].bitcast(F32), part[:, 0:32].bitcast(F32)).then_inc(s["ld_b1_rows"], 16)
                    sp.dma_start(b1_rows[row:row + 1, n:].bitcast(F32), part[:, 32:40].bitcast(F32)).then_inc(s["ld_b1_rows"], 16)

        def mix_sync(sp, L):
            for t in range(TILES[L] - 4, TILES[L]):
                sp.wait_ge(*scattered(L, t))
            for b in range(B):
                for k in range(2):
                    row = (k * B + b) * S
                    sp.dma_start(parts[:, k * T + b * QT:k * T + (b + 1) * QT, :],
                                 results[L][row:row + S, :].rearrange("(t p) d -> p t d", p=P)).then_inc(r[L][f"mixed_{b}"], 16)

        def experts_pool(pool, L):
            q, n = r[L], TILES[L]

            def gather(t):
                nc.gpsimd.indirect_dma_start(
                    out=gx[:, t, :], out_offset=None, in_=normed[L],
                    in_offset=bass.IndirectOffsetOnAxis(ap=slot_from[:, t:t + 1].bitcast(U32), axis=0)).then_inc(gathered(L, t)[0], 16)

            pool.wait_ge(q["place_ok"], 1)
            for i in range(POOL_ROWS):
                slot_row_of(nc.gpsimd, i).then_inc(q["slot_row_ok"], 1)
            pool.wait_ge(q["saved"], 32)
            pool.wait_ge(q["slots_ok"], 1)
            for t in range(12):
                gather(t)
            for t in range(n):
                pool.wait_ge(q["y_copied" if L == 0 else "y_ok"], t + 1)
                nc.gpsimd.indirect_dma_start(
                    out=results[L], out_offset=bass.IndirectOffsetOnAxis(ap=slot_to[:, t:t + 1].bitcast(U32), axis=0),
                    in_=ys[:, t % 4, :], in_offset=None).then_inc(scattered(L, t)[0], 16)
                if t + 12 < n:
                    gather(t + 12)

        def pick_experts(dve, step, L, b):
            E, q = EXPERTS[L], r[L]
            tiles = range(b * QT, (b + 1) * QT)
            dve.wait_ge(q["logits_pe"], b + 1)
            for t in tiles:
                ins = nc.vector.max(top8[:, t, :], bank[5][:, t * E:(t + 1) * E])
            step(ins)
            for t in tiles:
                ins = nc.vector.max_index(top8_at[:, t, :], top8[:, t, :], bank[5][:, t * E:(t + 1) * E])
            step(ins)
            ts = slice(b * QT, (b + 1) * QT)
            if b == 1:
                nc.vector.tensor_tensor(gate[:, 0, :], top8[:, :, 1], top8[:, :, 0], ALU.subtract).then_inc(q["diff_ok"], 1)
            step(nc.vector.tensor_copy(top2_at[:, :, ts], top8_at[:, ts, 0:2].rearrange("p t k -> p k t")))
            for k in range(2):
                ins = nc.vector.tensor_tensor(onehot[:, k, ts, 0:E], iota_e[:, 0:E].unsqueeze(1).to_broadcast([P, QT, E]),
                                              top2_at[:, k, ts].unsqueeze(2).to_broadcast([P, QT, E]), ALU.is_equal)
            step(ins)
            nc.vector.tensor_tensor(chosen[:, ts, 0:E], onehot[:, 0, ts, 0:E], onehot[:, 1, ts, 0:E], ALU.add).then_inc(q["chosen_ok"], 1)

        def slot_row_of(engine, i):
            return engine.tensor_scalar(slot_row[:, i, :], iota_r[:], slot_rt[:, 0].rearrange("p k t -> p (k t)")[:, i:i + 1],
                                        None, ALU.is_equal)

        def route_dve(dve, step, L):
            E, q = EXPERTS[L], r[L]
            pick_experts(dve, step, L, 1)
            if L == 0:
                dve.wait_ge(s["ld_b1"], 32)
                step(nc.vector.tensor_copy(b1_hi[:], b1_cols[:]))
                nc.vector.tensor_tensor(b1_lo[:], b1_cols[:], b1_hi[:].bitcast(F32), ALU.subtract).then_inc(s["b1_ok"], 1)
            dve.wait_ge(q["exp_ok"], 1)
            step(nc.vector.tensor_scalar(gate[:, 1, :], gate[:, 0, :], 1.0, None, ALU.add))
            step(nc.vector.reciprocal(gate[:, 2, :], gate[:, 1, :]))
            step(nc.vector.tensor_tensor(gate[:, 3, :], gate[:, 0, :], gate[:, 2, :], ALU.mult))
            step(nc.vector.tensor_copy(gate_hi[:], gate[:, 2:4]))
            nc.vector.tensor_tensor(gate_lo[:], gate[:, 2:4], gate_hi[:].bitcast(F32), ALU.subtract)
            dve.wait_ge(q["rank_pe"], 1)
            for k in range(2):
                ins = nc.vector.tensor_tensor(ranked[:, k, :, 0:E], onehot[:, k, :, 0:E],
                                              bank[6][:, 0:T * E].rearrange("p (t e) -> p t e", e=E), ALU.mult)
            step(ins)
            in_expert = slot_f[:].rearrange("p k t -> p (k t)")
            step(nc.vector.tensor_reduce(in_expert, ranked[:, :, :, 0:E].rearrange("p k t e -> p (k t) e"), AX.X, ALU.add))
            step(nc.vector.tensor_copy(slot_i[:, 0], slot_f[:]))
            nc.vector.tensor_scalar(slot_i[:, 1], slot_i[:, 0], P - 1, None, ALU.bitwise_and)
            step(nc.vector.tensor_scalar(slot_i[:, 2], slot_i[:, 0], 7, None, ALU.arith_shift_right))
            nc.vector.tensor_copy(slot_rt[:], slot_i[:, 1:3]).then_inc(q["place_ok"], 1)
            step(nc.vector.tensor_scalar(counts_i[:, 0, 0:E], bank[7][:, 0:E], float(P - 1), None, ALU.add))
            step(nc.vector.tensor_scalar(counts_i[:, 1, 0:E], counts_i[:, 0, 0:E], 7, None, ALU.arith_shift_right))
            nc.vector.memset(scan[0][:, 0:16], 0.0)
            nc.vector.memset(scan[1][:, 0:16], 0.0)
            nc.vector.tensor_copy(tiles_f[:, 0:E], counts_i[:, 1, 0:E])
            step(nc.vector.tensor_copy(scan[0][:, 16:16 + E], counts_i[:, 1, 0:E]))
            a = 0
            shift = 1
            while shift < E:
                step(nc.vector.tensor_tensor(scan[1 - a][:, 16:16 + E], scan[a][:, 16:16 + E],
                                             scan[a][:, 16 - shift:16 - shift + E], ALU.add))
                a, shift = 1 - a, shift * 2
            upto = scan[a][:, 16:16 + E]
            step(nc.vector.tensor_tensor(counts_f[:, 0:E], upto, tiles_f[:, 0:E], ALU.subtract))
            for k in range(2):
                ins = nc.vector.tensor_tensor(ranked[:, k, :, 0:E], onehot[:, k, :, 0:E],
                                              counts_f[:, 0:E].unsqueeze(1).to_broadcast([P, T, E]), ALU.mult)
            step(ins)
            step(nc.vector.tensor_reduce(in_expert, ranked[:, :, :, 0:E].rearrange("p k t e -> p (k t) e"), AX.X, ALU.add))
            step(nc.vector.tensor_tensor(slot_f[:], slot_f[:], slot_rt[:, 1], ALU.add))
            NT = TILES[L]
            NE = even(NT)
            step(nc.vector.tensor_tensor(slot_hit[:, :, 0:NE], iota_s[:, 0:NE].unsqueeze(1).to_broadcast([P, 2 * T, NE]),
                                         in_expert.unsqueeze(2).to_broadcast([P, 2 * T, NE]), ALU.is_equal))
            for i, factor in enumerate((place_1, gate_hi.bitcast(F32), gate_lo.bitcast(F32))):
                ins = nc.vector.tensor_tensor(slot_tile[:, :, i, 0:NE], slot_hit[:, :, 0:NE],
                                              factor[:].rearrange("p k t -> p (k t)").unsqueeze(2).to_broadcast([P, 2 * T, NE]), ALU.mult)
            ins.then_inc(q["slot_tile_ok"], 1)
            for i in range(POOL_ROWS, 2 * T):
                slot_row_of(nc.vector, i).then_inc(q["slot_row_dve"], 1)
            dve.wait_ge(q["slot_pe"], 1)
            found = bank[5][:, 0:NT]
            step(nc.vector.tensor_copy(slot_gate[:, 0:NT], bank[5][:, NE:NE + NT]))
            nc.vector.tensor_tensor(slot_gate[:, 0:NT], slot_gate[:, 0:NT], bank[5][:, 2 * NE:2 * NE + NT], ALU.add)
            step(nc.vector.scalar_tensor_tensor(out=slot_none[:, 0:NT], in0=found, scalar=0.5, in1=spare_row[:, 0:NT],
                                                op0=ALU.is_lt, op1=ALU.mult))
            step(nc.vector.scalar_tensor_tensor(out=slot_to[:, 0:NT], in0=found, scalar=-1.0, in1=slot_none[:, 0:NT],
                                                op0=ALU.add, op1=ALU.add))
            nc.vector.tensor_scalar(slot_from[:, 0:NT], slot_to[:, 0:NT], B * S - 1, None, ALU.bitwise_and).then_inc(q["slots_ok"], 1)
            NT = TILES[L]
            step(nc.vector.tensor_tensor(before[:, 0:NT, 0:E], upto.unsqueeze(1).to_broadcast([P, NT, E]),
                                         iota_s[:, 0:NT].unsqueeze(2).to_broadcast([P, NT, E]), ALU.is_le))
            step(nc.vector.tensor_reduce(expert_f[:, 0:NT], before[:, 0:NT, 0:E], AX.X, ALU.add))
            nc.vector.tensor_scalar(expert_i[:, 0:NT], expert_f[:, 0:NT], float(E - 1), None, ALU.min).then_inc(q["experts_ok"], 1)
        def experts_dve(dve, step, L):
            q = r[L]
            n = TILES[L]
            if L == 1:
                for t in range((n + 3) // 4 * 4 + 2):
                    if t < n:
                        dve.wait_ge(q["act_ok"], t + 1)
                        if t >= 2:
                            dve.wait_ge(q["hidT_pe"], t - 1)
                        nc.vector.tensor_tensor(hid[:, t % 2, :], act_h[:, t % 2, :], bank[2 + 2 * (t % 2)][:], ALU.mult).then_inc(q["hid_ok"], 1)
                    u = t - 2
                    if 0 <= u < n:
                        dve.wait_ge(q["y_copied"], u + 1)
                        nc.vector.bn_stats(y_stats[:, u % 4, :], y[:, u % 8, :]).then_inc(q["y_stats_ok"], 1)
                    last = (n - 1) // 4 * 4
                    if u % 4 == 0 and 4 <= u <= last:
                        expert_norm_ends(step, u - 4, u)
                    if 0 <= u - 4 < last:
                        expert_scale(dve, step, q, [u - 4])
                    if u == last + 3:
                        expert_norm_starts(dve, step, q, last, n)
                        expert_norm_ends(step, last, n)
                        expert_scale(dve, step, q, range(last, n))
                    elif 0 <= u < last and u % 4 == 3:
                        expert_norm_starts(dve, step, q, u // 4 * 4, u + 1)
            if L == 0:
                dve.wait_ge(q["y_pe"], n)
                layer1_constants(dve, step)
            for b in range(B):
                ts = slice(b * QT, (b + 1) * QT)
                dve.wait_ge(q[f"mixed_{b}"], 32)
                step(nc.vector.tensor_tensor(x[:, ts, :], x[:, ts, :], parts[:, b * QT:(b + 1) * QT, :], ALU.add))
                nc.vector.tensor_tensor(x[:, ts, :], x[:, ts, :], parts[:, T + b * QT:T + (b + 1) * QT, :], ALU.add).then_inc(q["summed"], 1)
            dve.wait_ge(q["summed"], B)

        def expert_norm_starts(dve, step, q, first, end):
            m = end - first
            dve.wait_ge(q["y_stats_ok"], end)
            for u in range(first, end):
                ins = nc.vector.bn_aggr(y_mv[:, u - first, :], y_stats[:, u - first, :])
            step(ins)
            root_starts(step, y_mv[:, 0:m, 1], y_root[:, 0, 0:m], y_root[:, 1, 0:m], y_root[:, 3, 0:m])
            root_goes_on(step, 1, y_root[:, 0, 0:m], y_root[:, 2, 0:m], y_root[:, 3, 0:m])

        def expert_norm_ends(step, first, end):
            m = end - first
            root_goes_on(step, 2, y_root[:, 0, 0:m], y_root[:, 2, 0:m], y_root[:, 3, 0:m])
            step(nc.vector.tensor_tensor(y_root[:, 4, 0:m], y_root[:, 3, 0:m], slot_gate[:, first:end], ALU.mult))

        def expert_scale(dve, step, q, tiles):
            e = {}
            for u in tiles:
                i = u % 4
                e[u] = dve.value_load(expert_i[0:1, u:u + 1], min_val=0, max_val=EXPERTS[1] - 1)
                if u >= 4:
                    dve.wait_ge(*scattered(1, u - 4))
                ins = nc.vector.tensor_scalar(ys[:, i, :], y[:, u % 8, :], y_mv[:, i, 0:1], y_root[:, 4, i:i + 1], ALU.subtract, ALU.mult)
            step(ins)
            for u in tiles:
                ins = nc.vector.tensor_tensor(ys[:, u % 4, :], ys[:, u % 4, :], gamma[:].rearrange("p e d -> p (e d)")[:, bass.ds(e[u] * D, D)], ALU.mult)
            step(ins)
            for u in tiles:
                nc.vector.scalar_tensor_tensor(out=ys[:, u % 4, :], in0=beta[:].rearrange("p e d -> p (e d)")[:, bass.ds(e[u] * D, D)],
                                               scalar=slot_gate[:, u:u + 1], in1=ys[:, u % 4, :], op0=ALU.mult, op1=ALU.add).then_inc(q["y_ok"], 1)

        def experts_act(act, L):
            q = r[L]
            act.wait_ge(q["diff_ok"], 1)
            nc.scalar.activation(gate[:, 0, :], gate[:, 0, :], ACT.Exp).then_inc(q["exp_ok"], 1)
            if L == 1:
                nc.scalar.activation(warm[:], ones[:, 0:1], ACT.Silu)

            def rows(t):
                act.wait_ge(q["gxT_pe"], t + 1)
                if t >= 2:
                    act.wait_ge(q["up_pe"], t - 1)
                nc.scalar.copy(gxT[:, t % 2, :], bank[0][:, 0:P]).then_inc(q["gxT_ok"], 1)

            def hidden(t):
                act.wait_ge(q["up_pe"], t + 1)
                if L == 0:
                    if t >= 2:
                        act.wait_ge(q["hidT_pe"], t - 1)
                    nc.scalar.activation(hid[:, t % 2, :], bank[1 + 2 * (t % 2)][:], ACT.Relu).then_inc(q["hid_ok"], 1)
                else:
                    if t >= 2:
                        act.wait_ge(q["hid_ok"], t - 1)
                    nc.scalar.activation(act_h[:, t % 2, :], bank[1 + 2 * (t % 2)][:], ACT.Silu).then_inc(q["act_ok"], 1)

            n = TILES[L]
            for t in range(3):
                rows(t)
                if t >= 1:
                    hidden(t - 1)
            for t in range(n):
                act.wait_ge(q["hidT_pe"], t + 1)
                if t >= 2:
                    act.wait_ge(q["y_pe"], t - 1)
                nc.scalar.copy(hidT[:, t % 2, :], bank[5][:]).then_inc(q["hidT_ok"], 1)
                if t + 3 < n:
                    rows(t + 3)
                if t + 2 < n:
                    hidden(t + 2)
                act.wait_ge(q["y_pe"], t + 1)
                if L == 0:
                    if t >= 4:
                        act.wait_ge(*scattered(0, t - 4))
                    nc.scalar.activation(ys[:, t % 4, :], bank[6 + t % 2][:, 0:D], ACT.Copy, scale=slot_gate[:, t:t + 1]).then_inc(q["y_copied"], 1)
                else:
                    if t >= 8:
                        act.wait_ge(q["y_ok"], t - 7)
                    nc.scalar.copy(y[:, t % 8, :], bank[6 + t % 2][:, 0:D]).then_inc(q["y_copied"], 1)

        def experts_pe(pe, L):
            E, q = EXPERTS[L], r[L]
            pe.wait_ge(q["chosen_ok"], B)
            for back in range(T):
                ins = mm(bank[6][:, back * E:T * E], tri[:] if back == 0 else ones_b[:], chosen[:, 0:T - back, 0:E],
                         start=(back == 0), stop=(back == T - 1), skip_group_check=True)
            for t in range(T):
                ins = mm(bank[7][:, 0:E], ones_b[:], chosen[:, t, 0:E], start=(t == 0), stop=(t == T - 1))
            ins.then_inc(q["rank_pe"], 1)
            pe.wait_ge(q["slot_tile_ok"], 1)
            for i in range(2 * T):
                if i < POOL_ROWS:
                    pe.wait_ge(q["slot_row_ok"], i + 1)
                else:
                    pe.wait_ge(q["slot_row_dve"], i + 1 - POOL_ROWS)
                ins = mm(bank[5][:, 0:3 * even(TILES[L])].rearrange("p (a n) -> p a n", a=3), slot_row[:, i, :], slot_tile[:, i, :, 0:even(TILES[L])],
                         start=(i == 0), stop=(i == 2 * T - 1))
            ins.then_inc(q["slot_pe"], 1)
            w1, w2 = (w1_0, w2_0) if L == 0 else (w1_1, w2_1)

            def expert_of(t):
                return pe.value_load(expert_i[0:1, t:t + 1], min_val=0, max_val=E - 1)

            def turn_rows(t):
                if t:
                    pe.wait_ge(q["gxT_ok"], t)
                pe.wait_ge(*gathered(L, t))
                nc.tensor.transpose(bank[0][:, 0:P], gx[:, t, :], ident[:]).then_inc(q["gxT_pe"], 1)

            def up(t, e):
                pe.wait_ge(q["gxT_ok"], t + 1)
                if t >= 2:
                    pe.wait_ge(q["hid_ok"], t - 1)
                cols = bass.ds(e * HID, HID)
                first, second = bank[1 + 2 * (t % 2)], bank[2 + 2 * (t % 2)]
                if L == 0:
                    mm(first[:], gxT[:, t % 2, :], w1[:, cols], start=True, stop=False)
                    mm(first[:], ones_r[0:2, 0:P], b1_rows[0:2, cols], start=False, stop=True).then_inc(q["up_pe"], 1)
                else:
                    mm(first[:], gxT[:, t % 2, :], w1[:, cols], start=True, stop=True)
                    mm(second[:], gxT[:, t % 2, :], w3_1[:, cols], start=True, stop=True).then_inc(q["up_pe"], 1)

            def turn_hidden(t):
                pe.wait_ge(q["hid_ok"], t + 1)
                if t:
                    pe.wait_ge(q["hidT_ok"], t)
                for c in range(4):
                    ins = nc.tensor.transpose(bank[5][:, c * P:(c + 1) * P], hid[:, t % 2, c * P:(c + 1) * P], ident[:])
                ins.then_inc(q["hidT_pe"], 1)

            def down(t, e):
                pe.wait_ge(q["hidT_ok"], t + 1)
                result = bank[6 + t % 2][:, 0:D]
                if t >= 2:
                    pe.wait_ge(q["y_copied"], t - 1)
                for c in range(4):
                    ins = mm(result, hidT[:, t % 2, c * P:(c + 1) * P], w2[:, bass.ds(e * HID + c * P, P)],
                             start=(c == 0), stop=(L == 1 and c == 3))
                if L == 0:
                    ins = mm(result, ones_r[0:2, 0:P], b1_rows[0:2, bass.ds(e * D + E * HID, D)], start=False, stop=True)
                ins.then_inc(q["y_pe"], 1)

            pe.wait_ge(q["experts_ok"], 1)
            if L == 0:
                pe.wait_ge(s["ld_b1_rows"], 64)
            pe.wait_ge(q["ld_w"], 16 * (2 + L))
            n = TILES[L]
            e = {}
            for t in range(3):
                turn_rows(t)
                if t >= 1:
                    e[t - 1] = expert_of(t - 1)
                    up(t - 1, e[t - 1])
            for t in range(n):
                turn_hidden(t)
                if t + 2 < n:
                    e[t + 2] = expert_of(t + 2)
                if t + 3 < n:
                    turn_rows(t + 3)
                if t + 2 < n:
                    up(t + 2, e[t + 2])
                down(t, e[t])


        def layer1_constants(dve, step):
            for n in ("q_hi", "q_lo"):
                nc.vector.memset(sel1[n][:].bitcast(F32), 0.0)
            for n in ("k_hi", "k_lo", "mask"):
                nc.vector.memset(sel1k[n][:].bitcast(F32), 0.0)
            nc.vector.memset(kst1[:].bitcast(F32), 0.0)
            nc.vector.memset(krem1[:].bitcast(F32), 0.0)
            nc.vector.memset(v1[:], 0.0)
            step(nc.vector.memset(vrem1[:], 0.0))
            id_q = ident[:].rearrange("p (h f) -> p h f", f=DH)
            id_k = ident[0:DH, 0:DH].unsqueeze(1).to_broadcast([DH, 4, DH])
            nc.vector.memset(sel1k["mask"][0:1, :, 3, 0:1].bitcast(F32), 1.0)
            for tile, quarter, src in ((sel1["q_hi"], 0, id_q), (sel1["q_hi"], 1, id_q), (sel1["q_lo"], 2, id_q),
                                       (sel1k["k_hi"][0:DH], 0, id_k), (sel1k["k_hi"][0:DH], 2, id_k), (sel1k["k_lo"][0:DH], 1, id_k)):
                ins = nc.vector.tensor_copy(tile[:, :, quarter, :], src)
            ins.then_inc(s["sel1_ok"], 1)

        def match(u):
            b, qt = divmod(u, QT)
            return bank[2 * b + qt // 3][:, qt % 3 * KEYS:(qt % 3 + 1) * KEYS]

        def hard_attention_dve(dve, step):
            dve.wait_ge(s["mk_pe"], 1)
            step(nc.vector.tensor_copy(mk_hi[0:DH, :], bank[7][0:DH, 128:128 + B * KP]))
            nc.vector.tensor_tensor(mk_lo[0:DH, :], bank[7][0:DH, 128:128 + B * KP], mk_hi[0:DH, :].bitcast(F32), ALU.subtract).then_inc(s["mk_ok"], 1)
            for b in range(B):
                tiles = range(b * QT, (b + 1) * QT)
                dve.wait_ge(s["hit_pe"], b + 1)
                for u in tiles:
                    ins = nc.vector.max(hit8[:, u, :], match(u))
                step(ins)
                for u in tiles:
                    ins = nc.vector.max_index(hit8_at[:, u, :], hit8[:, u, :], match(u))
                step(ins)
                step(nc.vector.tensor_copy(hit_f[:, b * QT:(b + 1) * QT], hit8_at[:, b * QT:(b + 1) * QT, 0]))
                if b:
                    dve.wait_ge(s["count_pe"], 1)
                for u in tiles:
                    ins = nc.vector.tensor_scalar(hits[:, u % QT, :], iota_k[:], hit_f[:, u:u + 1], None, ALU.is_equal)
                ins.then_inc(s["hit_ok"], 1)
            dve.wait_ge(s["count_pe"], 2)
            nc.vector.tensor_copy(counts[:], bank[0][:, 0:2 * B])
            nc.vector.tensor_scalar(mask_row[0:1, :], bank[0][0:1, 128:128 + B * KP], 0.5, MASKED, ALU.is_lt, ALU.mult).then_inc(s["mask_ok"], 1)
            dve.wait_ge(s["kst1_pe"], 1)
            src = bank[1][:, 0:B * KP].rearrange("p (b k) -> p b k", b=B)
            for a in range(4):
                rows = slice(32 * a, 32 * a + 32)
                ins = nc.vector.tensor_copy(kst1[rows, a], src[rows])
            ins.then_inc(s["kst1_ok"], 1)

        def hard_attention_pe(pe):
            for b in range(B):
                pe.wait_ge(s["xnT_ok"], 4 + b + 1)
                mm(bank[5 + b][:], small_wT[:, 2, :], xnT[:, b, :], start=True, stop=True).then_inc(s["qp_pe"], 1)
            for b in range(B):
                for half, lhs in enumerate((ctxT[:, b, 0:P], ctxT_rep[:, b].rearrange("p j k -> p (j k)"))):
                    i = 2 * b + half
                    mm(bank[4][:, i * 16:(i + 1) * 16], lhs, wkvT[:], start=True, stop=True)
            mm(bank[7][0:DH, 128:128 + B * KP], wkvT[:, 0:DH], ctxT[:].rearrange("p b k -> p (b k)"), start=True, stop=True).then_inc(s["mk_pe"], 1)
            for b in range(B):
                pe.wait_ge(s["qp_ok"], b + 1)
                for qt in range(QT):
                    ins = mm(match(b * QT + qt), qp[:, b, qt * P:(qt + 1) * P], ctxT[:, b, 0:KEYS], start=True, stop=True)
                ins.then_inc(s["hit_pe"], 1)
            pe.wait_ge(s["sel1_ok"], 1)
            for b in range(B):
                pe.wait_ge(s["qp_split"], b + 1)
                for g in range(NQUAD):
                    u = b * NQUAD + g
                    if u >= 2:
                        pe.wait_ge(s["qst1_ok"], u - 1)
                    dst = bank[(5, 6)[u % 2]][:]
                    for i, n in enumerate(("q_hi", "q_lo")):
                        mm(dst, sel1[n][:, 4 * g:4 * g + 4].rearrange("p a c f -> p (a c f)"), (qp_hi, qp_lo)[i][:, b, :], start=(i == 0), stop=False)
                    mm(dst, sel1k["mask"][0:1].rearrange("p a c f -> p (a c f)"), ones_r[0:1, :], start=False, stop=True).then_inc(s["qst1_pe"], 1)
                pe.wait_ge(s["hit_ok"], b + 1)
                for half in range(2):
                    for qt in range(QT):
                        mm(bank[0][:, 2 * b + half:2 * b + half + 1], hits[:, qt, half * P:(half + 1) * P], ones_b[:, 0:1],
                           start=(qt == 0), stop=(qt == QT - 1))
                for qt in range(QT):
                    ins = mm(bank[0][0:1, 128 + b * KP:128 + (b + 1) * KP], ones_b[:, 0:1], hits[:, qt, 0:KP],
                             start=(qt == 0), stop=(qt == QT - 1))
                ins.then_inc(s["count_pe"], 1)
            pe.wait_ge(s["mk_ok"], 1)
            dst = bank[1][:, 0:B * KP]
            mm(dst, sel1k["k_hi"][0:DH].rearrange("p a c f -> p (a c f)"), mk_hi[0:DH, :], start=True, stop=False)
            mm(dst, sel1k["k_lo"][0:DH].rearrange("p a c f -> p (a c f)"), mk_lo[0:DH, :], start=False, stop=False)
            pe.wait_ge(s["mask_ok"], 1)
            mm(dst, sel1k["mask"][0:1].rearrange("p a c f -> p (a c f)"), mask_row[0:1, :], start=False, stop=True).then_inc(s["kst1_pe"], 1)
            pe.wait_ge(s["qst1_ok"], B * NQUAD)
            pe.wait_ge(s["kst1_ok"], 1)

        @block.sync
        def _(sp):
            sp.dma_start(ctx_main[:], A["ctx_1024"][:, 0:P, :].rearrange("b k d -> k b d")).then_inc(s["ld_ctx"], 16)
            sp.dma_start(ctx_rem[0:KR], A["ctx_1024"][:, P:KEYS, :].rearrange("b k d -> k b d")).then_inc(s["ld_ctx"], 16)
            sp.dma_start(fm_w[0:DH, :], A["L0_xattn_fm_w"]).then_inc(s["ld_fm"], 16)
            sp.dma_start(fm_b[0:DH, :], A["L0_xattn_fm_b"].rearrange("(e a) -> e a", a=1)).then_inc(s["ld_fm"], 16)
            sp.dma_start(x[:], A["x"].rearrange("b (t p) d -> p (b t) d", p=P)).then_inc(s["ld_x"], 16)
            sp.dma_start(small_w[:, 0:2, :], A["L0_xattn_fc_w"].rearrange("e (a f) -> e a f", a=2)).then_inc(s["ld_small"], 16)
            sp.dma_start(small_w[:, 2, :], A["L1_xattn_Wq"]).then_inc(s["ld_small"], 16)
            sp.dma_start(small_w[:, 3, :], A["L1_xattn_Wc"]).then_inc(s["ld_small"], 16)
            sp.dma_start(wkv[0:2 * DH, :], A["L1_xattn_Wkv"]).then_inc(s["ld_small"], 16)
            sp.dma_start(fc_b[0:1, :], A["L0_xattn_fc_b"].rearrange("(a e) -> a e", a=1)).then_inc(s["ld_small"], 16)
            for L in range(2):
                sp.dma_start(wr[L][:], A[f"L{L}_ffn_Wr"]).then_inc(s["ld_small"], 16)
                sp.dma_start(br[L][0:1, :], A[f"L{L}_ffn_br"].rearrange("(a e) -> a e", a=1)).then_inc(s["ld_small"], 16)
            experts_sync(sp, 0)
            mix_sync(sp, 0)
            for name, tile in (("W1", w1_1), ("W3", w3_1)):
                sp.dma_start(tile[:].rearrange("p (e f) -> p e f", f=HID), A[f"L1_ffn_{name}"].rearrange("e d f -> d e f")).then_inc(r[1]["ld_w"], 16)
            sp.wait_ge(s["x1_ok"], 6)
            sp.dma_start(w2_1[:].rearrange("p (e c d) -> p e c d", c=4, d=D),
                         A["L1_ffn_W2"].rearrange("e (c p) d -> p e c d", p=P)).then_inc(r[1]["ld_w"], 16)
            sp.dma_start(gamma[:].rearrange("p e d -> p (e d)"), A["L1_ffn_gamma"].rearrange("e d -> (e d)").partition_broadcast(P)).then_inc(s["ld_gb"], 16)
            sp.dma_start(beta[:].rearrange("p e d -> p (e d)"), A["L1_ffn_beta"].rearrange("e d -> (e d)").partition_broadcast(P)).then_inc(s["ld_gb"], 16)
            experts_sync(sp, 1)
            mix_sync(sp, 1)
            for b in range(B):
                sp.wait_ge(r[1]["summed"], b + 1)
                sp.dma_start(out[b].rearrange("(t p) d -> p t d", p=P), x[:, b * QT:(b + 1) * QT, :]).then_inc(s["stored"], 16)
            sp.wait_ge(s["stored"], 32)

        @block.gpsimd
        def _(pool):
            step = Steps(pool, s["pool_step"])
            step(nc.gpsimd.memset(ident[:], 0.0))
            step(nc.gpsimd.affine_select(out=ident[:], in_=ident[:], pattern=[[-1, P]], compare_op=ALU.not_equal,
                                         fill=1.0, base=0, channel_multiplier=1))
            nc.gpsimd.memset(ones[:], 1.0).then_inc(s["pool_consts"], 1)
            step(nc.gpsimd.memset(bmask[:], 1.0))
            step(nc.gpsimd.affine_select(out=bmask[:], in_=bmask[:], pattern=[[-DH, H]], compare_op=ALU.is_ge,
                                         fill=0.0, base=0, channel_multiplier=1))
            nc.gpsimd.affine_select(out=bmask[:], in_=bmask[:], pattern=[[DH, H]], compare_op=ALU.is_ge,
                                    fill=0.0, base=DH - 1, channel_multiplier=-1).then_inc(s["pool_consts"], 1)
            pool.wait_ge(s["pool_consts"], 2)
            for a in range(2):
                step(nc.gpsimd.memset(kst0[64 * (1 - a):64 * (1 - a) + 64].rearrange("p (n a) b k -> p n a (b k)", a=2)[:, :, a].bitcast(F32), 0.0))
            nc.gpsimd.memset(krem0[:].bitcast(F32), 0.0).then_inc(s["pool_consts"], 1)
            step(nc.gpsimd.memset(v0[:], 0.0))
            for b in range(B):
                nc.gpsimd.memset(v0[:, b].rearrange("p g (j x) -> p g j x", x=9 * F0)[:, :, :, 4 * F0:5 * F0], 1.0)
            step(nc.gpsimd.memset(vrem0[:], 0.0))
            for j in range(4):
                step(nc.gpsimd.memset(vrem0[32 * j:32 * j + KR, :, :, (4 + j) * F0:(5 + j) * F0], 1.0))
            nc.gpsimd.memset(ones_r[:].bitcast(F32), 1.0).then_inc(s["pool_consts"], 1)
            nc.gpsimd.iota(iota_e[:], pattern=[[1, 16]], base=0, channel_multiplier=0, allow_small_or_imprecise_dtypes=True)
            nc.gpsimd.iota(iota_s[:], pattern=[[1, 32]], base=0, channel_multiplier=0, allow_small_or_imprecise_dtypes=True)
            nc.gpsimd.iota(iota_k[:, 0:P], pattern=[[1, P]], base=0, channel_multiplier=0, allow_small_or_imprecise_dtypes=True)
            nc.gpsimd.iota(iota_k[:, P:], pattern=[[0, 4], [1, 32]], base=P, channel_multiplier=0, allow_small_or_imprecise_dtypes=True)
            step(nc.gpsimd.memset(ones_b[:], 1.0))
            nc.gpsimd.affine_select(out=tri[:], in_=ones_b[:], pattern=[[1, P]], compare_op=ALU.is_gt,
                                    fill=0.0, base=0, channel_multiplier=-1).then_inc(s["pool_consts"], 1)
            nc.gpsimd.iota(place_1[:], pattern=[[B * S, 2], [P, T]], base=1, channel_multiplier=1, allow_small_or_imprecise_dtypes=True)
            nc.gpsimd.iota(iota_r[:], pattern=[[1, P]], base=0, channel_multiplier=0, allow_small_or_imprecise_dtypes=True)
            nc.gpsimd.iota(spare_row[:], pattern=[[P, 32]], base=2 * B * S + 1, channel_multiplier=1,
                           allow_small_or_imprecise_dtypes=True).then_inc(s["pool_consts"], 1)
            for t in range(2):
                pool.wait_ge(s["f_ok"], 2 + t + 1)
                nc.gpsimd.tensor_tensor(f_lo[:, t, 1, :], f[:, t, 1, :], f_hi[:, t, 1, :].bitcast(F32), ALU.subtract).then_inc(s["f_split_pool"], 1)
            experts_pool(pool, 0)
            for b in range(B):
                pool.wait_ge(s["qp_ok"], b + 1)
                nc.gpsimd.tensor_tensor(qp_lo[:, b, :], qp[:, b, :], qp_hi[:, b, :].bitcast(F32), ALU.subtract).then_inc(s["qp_split"], 1)
            pool.wait_ge(s["kst1_ok"], 1)
            for a in range(4):
                rows = slice(32 * a, 32 * a + 32)
                ins = nc.gpsimd.tensor_copy(krem1[rows, :, a, :], kst1[rows, a, :, P:KP])
            ins.then_inc(s["krem1_ok"], 1)
            experts_pool(pool, 1)

        @block.vector
        def _(dve):
            step = Steps(dve, s["dve_step"])
            nc.vector.memset(nm[:], 0.0)
            step(nc.vector.memset(ctxT[:], 0.0))
            nc.vector.memset(sel0["q_hi"][:].bitcast(F32), 0.0)
            nc.vector.memset(sel0["q_lo"][:].bitcast(F32), 0.0)
            nc.vector.memset(sel0["k_hi"][:].bitcast(F32), 0.0)
            step(nc.vector.memset(sel0["k_lo"][:].bitcast(F32), 0.0))
            dve.wait_ge(s["ld_fm"], 32)
            dve.wait_ge(s["pool_consts"], 1)
            nc.vector.tensor_copy(fm_rep[0:DH], fm_w[0:DH, :].unsqueeze(1).to_broadcast([DH, H, DH]))
            nc.vector.tensor_copy(sign_id[0:DH, :, 0, :], ident[0:DH, 0:DH].unsqueeze(1).to_broadcast([DH, H, DH]))
            nc.vector.tensor_scalar(sign_id[0:DH, :, 1, :], ident[0:DH, 0:DH].unsqueeze(1).to_broadcast([DH, H, DH]),
                                    -1.0, None, ALU.mult).then_inc(s["fm_ok"], 1)
            sel_in = ident[:].rearrange("p (h f) -> p h f", f=F0)
            for name, quarters in (("q_hi", (0, 1)), ("q_lo", (2, 3)), ("k_hi", (0, 2)), ("k_lo", (1, 3))):
                for quarter in quarters:
                    ins = nc.vector.tensor_copy(sel0[name][:, :, quarter, :], sel_in)
            step(nc.vector.tensor_tensor(ind[0:32], ident[0:32, 0:16].unsqueeze(2).to_broadcast([32, H, 32]),
                                         ident[0:32, 16:32].unsqueeze(2).to_broadcast([32, H, 32]), ALU.add))
            dve.wait_ge(s["fm_pe"], 1)
            dve.wait_ge(s["pool_consts"], 2)
            fmT = bank[2][:, 16:16 + DH].unsqueeze(1).to_broadcast([P, H, DH])
            mask = bmask[:].unsqueeze(2).to_broadcast([P, H, DH])
            nc.vector.tensor_copy(bias_col[:], bank[2][:, 24:25])
            nc.vector.tensor_copy(bias_row[0:1, :], bank[2][0:1, 128:128 + H * F0])
            nc.vector.tensor_tensor(wexp[:, :, 0, :], fmT, mask, ALU.mult)
            nc.vector.scalar_tensor_tensor(out=wexp[:, :, 1, :], in0=fmT, scalar=-1.0, in1=mask,
                                           op0=ALU.mult, op1=ALU.mult).then_inc(s["fm2_ok"], 1)
            dve.wait_ge(s["ctxT_pe"], 1)
            step(nc.vector.tensor_copy(ctxT[:, :, 0:KEYS], bank[0][:, 0:B * KP].rearrange("p (b k) -> p b k", b=B)[:, :, 0:KEYS]))
            nc.vector.tensor_copy(ctxT_rep[:], ctxT[:, :, P:KP].unsqueeze(2).to_broadcast([P, B, 4, 32])).then_inc(s["ctxT_ok"], 1)
            dve.wait_ge(s["ld_x"], 16)
            layer_norm(step)
            for t in range(2):
                dve.wait_ge(s["kf_ok"], t + 1)
                nc.vector.tensor_tensor(kf_lo[:, t, :], kf[:, t, :], kf_hi[:, t, :].bitcast(F32), ALU.subtract).then_inc(s["kf_split"], 1)
            for t in range(2):
                dve.wait_ge(s["f_ok"], t + 1)
                nc.vector.tensor_tensor(f_lo[:, t, 0, :], f[:, t, 0, :], f_hi[:, t, 0, :].bitcast(F32),
                                        ALU.subtract).then_inc(s["f_split"], 1)
            dve.wait_ge(s["pool_consts"], POOL_CONSTS)
            for u in (0, 2):
                dve.wait_ge(s["stack_pe"], u + 1)
                key_stack_copies(nc.vector.tensor_copy, u).then_inc(s["stack_dve"], 1)

            attention_dve(dve, step, 0)
            route_dve(dve, step, 0)
            experts_dve(dve, step, 0)
            nc.vector.memset(nm[:], 0.0)
            layer_norm(step)
            hard_attention_dve(dve, step)
            attention_dve(dve, step, 1)
            route_dve(dve, step, 1)
            dve.wait_ge(s["ld_gb"], 32)
            experts_dve(dve, step, 1)

        @block.scalar
        def _(act):
            act.wait_ge(s["pool_consts"], 1)
            nc.scalar.activation(warm[:], ones[:, 0:1], ACT.Exp)
            act.wait_ge(s["fm2_ok"], 1)
            for t in range(2):
                act.wait_ge(s["zk_pe"], t + 1)
                nc.scalar.activation(kf_hi[:, t, :], bank[(1, 7)[t]][:, 0:B * KP], ACT.Exp, bias=bias_col[:])
                nc.scalar.activation(kf[:, t, :], bank[(1, 7)[t]][:, 0:B * KP], ACT.Exp, bias=bias_col[:]).then_inc(s["kf_ok"], 1)
            act.wait_ge(s["wT_pe"], 1)
            nc.scalar.copy(wkvT[:], bank[2][:, 0:2 * DH])
            nc.scalar.copy(small_wT[:].rearrange("p a d -> p (a d)"), bank[0][:]).then_inc(s["wT_ok"], 1)
            for b in range(B):
                copy_xnT(act, 0, b, 3 + b)
            for b in range(B):
                for t in range(2):
                    act.wait_ge(s["zq_pe"], 2 * b + t + 1)
                    nc.scalar.activation(f_hi[:, t, b, :], bank[(5, 6, 7, 0)[2 * b + t]][:], ACT.Exp, bias=bias_col[:])
                    nc.scalar.activation(f[:, t, b, :], bank[(5, 6, 7, 0)[2 * b + t]][:], ACT.Exp,
                                         bias=bias_col[:]).then_inc(s["f_ok"], 1)
            act.wait_ge(s["pool_consts"], POOL_CONSTS)
            for u in range(FIRST_STACKS):
                copy_stack(act, u)
            act.wait_ge(s["f_split_pool"], 2)
            def exponents_of_values(b):
                act.wait_ge(s["vz_pe"], b + 1)
                exponents = bank[(0, 4)[b]]
                diagonal = v0[:, b].rearrange("p g (j x) -> p g j x", x=9 * F0)
                nc.scalar.activation(diagonal[:, :, :, 0:F0], exponents[:, 0:H * F0].rearrange("p (g j v) -> p g j v", g=NQUAD, j=4), ACT.Exp)
                for j in range(4):
                    rows = slice(32 * j, 32 * j + KR)
                    ins = nc.scalar.activation(vrem0[rows, b, :, j * F0:(j + 1) * F0],
                                               exponents[rows, H * F0:2 * H * F0].rearrange("p (g j v) -> p g j v", g=NQUAD, j=4)[:, :, j, :],
                                               ACT.Exp)
                ins.then_inc(s["v_ok"], 1)

            def beside_group(group, i):
                if group < NQUAD and i < 4:
                    copy_stack(act, FIRST_STACKS + 4 * group + i)
                if group == 0 and i in (1, 3):
                    exponents_of_values(i // 2)

            attention_act(act, 0, SCALE0, beside_group)
            experts_act(act, 0)
            for b in range(B):
                copy_xnT(act, 2, b, 3 + b)
            for b in range(B):
                act.wait_ge(s["qp_pe"], b + 1)
                nc.scalar.copy(qp_hi[:, b, :], bank[5 + b][:])
                nc.scalar.copy(qp[:, b, :], bank[5 + b][:]).then_inc(s["qp_ok"], 1)
            for u in range(B * NQUAD):
                b, g = divmod(u, NQUAD)
                act.wait_ge(s["qst1_pe"], u + 1)
                nc.scalar.copy(qst[:, g, b, :], bank[(5, 6)[u % 2]][:]).then_inc(s["qst1_ok"], 1)
            act.wait_ge(s["mask_ok"], 1)
            for b in range(B):
                diagonal = v1[:, b].rearrange("p (j x) -> p j x", x=9 * DH)
                nc.scalar.activation(diagonal[:, :, 0:DH],
                                     bank[4][:, (2 * b) * 16 + DH:(2 * b) * 16 + 2 * DH].unsqueeze(1).to_broadcast([P, 4, DH]),
                                     ACT.Copy, scale=counts[:, 2 * b:2 * b + 1])
                nc.scalar.copy(diagonal[:, :, 4 * DH:5 * DH], counts[:, 2 * b:2 * b + 1].unsqueeze(2).to_broadcast([P, 4, DH]))
                for j in range(4):
                    rows = slice(32 * j, 32 * j + 32)
                    nc.scalar.activation(vrem1[rows, b, j * DH:(j + 1) * DH], bank[4][rows, (2 * b + 1) * 16 + DH:(2 * b + 1) * 16 + 2 * DH],
                                         ACT.Copy, scale=counts[rows, 2 * b + 1:2 * b + 2])
                    ins = nc.scalar.copy(vrem1[rows, b, (4 + j) * DH:(5 + j) * DH], counts[rows, 2 * b + 1:2 * b + 2].to_broadcast([32, DH]))
            ins.then_inc(s["v1_ok"], 1)
            attention_act(act, 1, SCALE1)
            experts_act(act, 1)

        @block.tensor
        def _(pe):
            pe.wait_ge(s["pool_consts"], 1)
            pe.wait_ge(s["ld_ctx"], 32)
            for b in range(B):
                nc.tensor.transpose(bank[0][:, b * KP:b * KP + P], ctx_main[:, b, :], ident[:])
                ins = nc.tensor.transpose(bank[0][:, b * KP + P:b * KP + KEYS], ctx_rem[0:KR, b, :], ident[0:KR, 0:KR])
            ins.then_inc(s["ctxT_pe"], 1)
            pe.wait_ge(s["ld_fm"], 32)
            pe.wait_ge(s["fm_ok"], 1)
            mm(bank[2][:, 16:16 + DH], fm_rep[0:DH].rearrange("e h d -> e (h d)"), ident[0:DH, 0:DH], start=True, stop=True)
            mm(bank[2][:, 24:25], sign_id[0:DH, 0:8].rearrange("e h s f -> e (h s f)"), fm_b[0:DH, :], start=True, stop=True)
            mm(bank[2][0:1, 128:128 + H * F0], fm_b[0:DH, :], sign_id[0:DH].rearrange("e h s f -> e (h s f)"),
               start=True, stop=True).then_inc(s["fm_pe"], 1)
            pe.wait_ge(s["fm2_ok"], 1)
            pe.wait_ge(s["ctxT_ok"], 1)
            wexp_t = wexp[:].rearrange("p h s e -> p (h s e)")
            for t in range(2):
                mm(bank[(1, 7)[t]][:, 0:B * KP], wexp_t[:, t * P:(t + 1) * P], ctxT[:].rearrange("p b k -> p (b k)"),
                   start=True, stop=True).then_inc(s["zk_pe"], 1)
            pe.wait_ge(s["ld_small"], LD_SMALL)
            for a in range(4):
                nc.tensor.transpose(bank[0][:, a * P:(a + 1) * P], small_w[:, a, :], ident[:])
            nc.tensor.transpose(bank[2][:, 0:2 * DH], wkv[0:2 * DH, :], ident[0:2 * DH, 0:2 * DH]).then_inc(s["wT_pe"], 1)
            for b in range(B):
                turn_xn(pe, 0, b, 3 + b)
            pe.wait_ge(s["kf_ok"], 2)
            pe.wait_ge(s["wT_ok"], 1)
            for b in range(B):
                pe.wait_ge(s["xnT_ok"], b + 1)
                for t in range(2):
                    mm(bank[(5, 6, 7, 0)[2 * b + t]][:], wexp_t[:, t * P:(t + 1) * P], xnT[:, b, :],
                       start=True, stop=True).then_inc(s["zq_pe"], 1)
            pe.wait_ge(s["f_ok"], 4)
            pe.wait_ge(s["kf_split"], 2)

            def stack(u):
                if u >= 4:
                    wait_stack(pe, u - 4 if u < FIRST_STACKS else u - 1)
                kind, b, p = stack_of(u)
                t, i = divmod(p, 4)
                if kind == "q":
                    pe.wait_ge(s["f_split" if b == 0 else "f_split_pool"], t + 1)
                dst = stack_bank(u)[:, 0:B * KP] if kind == "k" else stack_bank(u)[:]
                for n, (part_of, features) in enumerate((("hi", kf_hi[:, t, :] if kind == "k" else f_hi[:, t, b, :]),
                                                         ("lo", kf_lo[:, t, :] if kind == "k" else f_lo[:, t, b, :]))):
                    ins = mm(dst, sel0[f"{kind}_{part_of}"][:, 2 * i:2 * i + 2].rearrange("p a c f -> p (a c f)"), features,
                             start=(n == 0), stop=(n == 1))
                ins.then_inc(s["stack_pe"], 1)

            def value_exponents(b):
                if b:
                    wait_stack(pe, FIRST_STACKS - 1)
                for half, lhs in enumerate((ctxT[:, b, 0:P], ctxT_rep[:, b].rearrange("p j k -> p (j k)"))):
                    dst = bank[(0, 4)[b]][:, half * H * F0:(half + 1) * H * F0]
                    mm(dst, lhs, wexp_t[:], start=True, stop=False)
                    ins = mm(dst, ones[0:1, 0:P], bias_row[0:1, :], start=False, stop=True)
                ins.then_inc(s["vz_pe"], 1)

            for u in range(FIRST_STACKS // 2):
                stack(u)
            for u in range(FIRST_STACKS // 2):
                wait_stack(pe, u)

            def beside_group(group, i):
                if group < 0:
                    if i < FIRST_STACKS // 2:
                        stack(FIRST_STACKS // 2 + i)
                    if i == PARTS:
                        for u in range(FIRST_STACKS // 2, FIRST_STACKS):
                            wait_stack(pe, u)
                elif group < NQUAD:
                    if i < 4:
                        stack(FIRST_STACKS + 4 * group + i)
                    else:
                        wait_stack(pe, FIRST_STACKS + 4 * group + 3)
                    if group == 0 and i in (1, 3):
                        value_exponents(i // 2)

            def query(b, h, cols):
                return qst[:, h // 2, b, cols]

            def keys(b, h, heads, n):
                return kst0[:, h:h + heads, b, 0:n]

            def rem_scores(dst, b, hg):
                for i in range(2):
                    p = 2 * hg + i
                    mm(dst, krem0[:, b, p].rearrange("p j k -> p (j k)"), qst[:, p, b, :], start=(i == 0), stop=False)

            attention_pe(pe, 0, query, keys, rem_scores, lambda b, hg, j: v0[:, b, hg, j * 8 * F0:(j + 1) * 8 * F0],
                         lambda b, hg: vrem0[:, b, hg, :], beside_group)
            experts_pe(pe, 0)
            for b in range(B):
                turn_xn(pe, 2, b, 3 + b)
            hard_attention_pe(pe)
            attention_pe(pe, 1, lambda b, h, cols: qst[:, h // 4, b, cols],
                         lambda b, h, heads, n: kst1[:, h % 4:h % 4 + heads, b, 0:n],
                         lambda dst, b, hg: mm(dst, krem1[:, b].rearrange("p a k -> p (a k)"), qst[:, hg, b, :], start=True, stop=False),
                         lambda b, hg, j: v1[:, b, j * 8 * DH:(j + 1) * 8 * DH], lambda b, hg: vrem1[:, b, :])
            experts_pe(pe, 1)

_OUTS = [((B, S, D), "float32")]


def kernel(**inputs):
    import numpy as _np
    import concourse.bacc as _bacc
    from concourse import mybir as _mybir
    from concourse.bass_utils import run_bass_kernel_spmd as _run

    nc = _bacc.Bacc("TRN2", target_bir_lowering=False, num_devices=1)
    arrays, args = {}, {}
    for name in inputs:
        a = _np.ascontiguousarray(inputs[name])
        arrays[f"in_{name}_dram"] = a
        args[name] = nc.dram_tensor(f"in_{name}_dram", a.shape, _mybir.dt.from_np(a.dtype), kind="ExternalInput").ap()
    out = nc.dram_tensor("out_0_dram", _OUTS[0][0], _mybir.dt.float32, kind="ExternalOutput").ap()
    build(nc, args, out)
    r = _run(nc, [arrays], core_ids=[0])
    return r.results[0]["out_0_dram"]
```
